# Optimizing a Trainium2 kernel written in Bass

```python
import numpy as np
import jax
import jax.numpy as jnp

def _softmax(x, axis=-1):
    return jax.nn.softmax(x, axis=axis)

def _gelu(x):
    return jax.nn.gelu(x, approximate=True)

def _silu(x):
    return jax.nn.silu(x)

def _sigmoid(x):
    return jax.nn.sigmoid(x)

def _layernorm(x, axis=-1, eps=1e-05):
    m = jnp.mean(x, axis=axis, keepdims=True)
    v = jnp.var(x, axis=axis, keepdims=True)
    return (x - m) / jnp.sqrt(v + eps)

def _scatter_add(tgt, idx, src, axis=0):
    return tgt.at[idx].add(src)

def _segment_sum(src, seg, n):
    return jax.ops.segment_sum(src, seg, n)
kernel_name = 'mk_prb_d1_jaxref_r8_358210'

def setup_inputs(seed: int=0):
    np.random.seed(seed)
    _w = jnp.asarray

    def _L0_attn_setup():
        import jax, jax.numpy as jnp
        import numpy as np
        BATCH, SEQ, D_MODEL, N_HEADS, D_HEAD = (2, 256, 256, 16, 128)
        ATTN_SCALE = np.sqrt(D_HEAD).astype(np.float32)
        IGNORE = jnp.float32(-100000.0)
        key = jax.random.key(seed)
        ks = jax.random.split(key, 5)
        init = 1.0 / np.sqrt(D_MODEL)
        return {'x': jax.random.normal(ks[0], (BATCH, SEQ, D_MODEL), jnp.float32), 'W_Q': jax.random.normal(ks[1], (N_HEADS, D_MODEL, D_HEAD), jnp.float32) * init, 'W_K': jax.random.normal(ks[2], (N_HEADS, D_MODEL, D_HEAD), jnp.float32) * init, 'W_V': jax.random.normal(ks[3], (N_HEADS, D_MODEL, D_HEAD), jnp.float32) * init, 'W_O': jax.random.normal(ks[4], (N_HEADS, D_HEAD, D_MODEL), jnp.float32) * init, 'b_Q': jnp.zeros((N_HEADS, D_HEAD), jnp.float32), 'b_K': jnp.zeros((N_HEADS, D_HEAD), jnp.float32), 'b_V': jnp.zeros((N_HEADS, D_HEAD), jnp.float32), 'b_O': jnp.zeros((D_MODEL,), jnp.float32)}
    _L0_attn_in = _L0_attn_setup()

    def _L0_ffn_setup():
        import jax, jax.numpy as jnp
        import numpy as np
        H = 256
        HQ = 16
        HKV = 4
        D = 128
        E = 32
        K = 4
        I = 128
        ISH = 128
        EPS = 1e-06
        THETA = 10000.0
        NORM_MIN = 1e-12

        def rmsnorm(x, w):
            xf = x.astype(jnp.float32)
            var = jnp.mean(xf * xf, axis=-1, keepdims=True)
            return w * (xf * jax.lax.rsqrt(var + EPS))

        def rotate_half(x):
            x1 = x[..., 0::2]
            x2 = x[..., 1::2]
            return jnp.stack((-x2, x1), axis=-1).reshape(x.shape)
        key = jax.random.key(seed)
        ks = jax.random.split(key, 14)
        s = 0.02
        B, S = (1, 128)
        return {'hidden_states': jax.random.normal(ks[0], (B, S, H), jnp.float32), 'ln1_w': jnp.ones((H,), jnp.float32), 'ln2_w': jnp.ones((H,), jnp.float32), 'wq': jax.random.normal(ks[1], (H, HQ * D), jnp.float32) * s, 'wk': jax.random.normal(ks[2], (H, HKV * D), jnp.float32) * s, 'wv': jax.random.normal(ks[3], (H, HKV * D), jnp.float32) * s, 'wo': jax.random.normal(ks[4], (HQ * D, H), jnp.float32) * s, 'gate_w': jax.random.normal(ks[5], (E, H), jnp.float32) * s, 'bias_e': jnp.zeros((E,), jnp.float32), 'weg': jax.random.normal(ks[6], (E, H, I), jnp.float32) * s, 'weu': jax.random.normal(ks[7], (E, H, I), jnp.float32) * s, 'wed': jax.random.normal(ks[8], (E, I, H), jnp.float32) * s, 'wsg': jax.random.normal(ks[9], (H, ISH), jnp.float32) * s, 'wsu': jax.random.normal(ks[10], (H, ISH), jnp.float32) * s, 'wsd': jax.random.normal(ks[11], (ISH, H), jnp.float32) * s}
    _L0_ffn_in = _L0_ffn_setup()
    _d = {'L0_attn_x': _L0_attn_in['x'], 'L0_attn_W_Q': _L0_attn_in['W_Q'], 'L0_attn_W_K': _L0_attn_in['W_K'], 'L0_attn_W_V': _L0_attn_in['W_V'], 'L0_attn_W_O': _L0_attn_in['W_O'], 'L0_attn_b_Q': _L0_attn_in['b_Q'], 'L0_attn_b_K': _L0_attn_in['b_K'], 'L0_attn_b_V': _L0_attn_in['b_V'], 'L0_attn_b_O': _L0_attn_in['b_O'], 'L0_ffn_ln1_w': _L0_ffn_in['ln1_w'], 'L0_ffn_ln2_w': _L0_ffn_in['ln2_w'], 'L0_ffn_wq': _L0_ffn_in['wq'], 'L0_ffn_wk': _L0_ffn_in['wk'], 'L0_ffn_wv': _L0_ffn_in['wv'], 'L0_ffn_wo': _L0_ffn_in['wo'], 'L0_ffn_gate_w': _L0_ffn_in['gate_w'], 'L0_ffn_bias_e': _L0_ffn_in['bias_e'], 'L0_ffn_weg': _L0_ffn_in['weg'], 'L0_ffn_weu': _L0_ffn_in['weu'], 'L0_ffn_wed': _L0_ffn_in['wed'], 'L0_ffn_wsg': _L0_ffn_in['wsg'], 'L0_ffn_wsu': _L0_ffn_in['wsu'], 'L0_ffn_wsd': _L0_ffn_in['wsd']}
    _x0 = _d['L0_attn_x']
    _d['L0_attn_x'] = jax.random.normal(jax.random.fold_in(jax.random.key(seed), 1), (2, 512, 256), dtype=_x0.dtype)
    del _x0
    return _d

def reference(L0_attn_x, L0_attn_W_Q, L0_attn_W_K, L0_attn_W_V, L0_attn_W_O, L0_attn_b_Q, L0_attn_b_K, L0_attn_b_V, L0_attn_b_O, L0_ffn_ln1_w, L0_ffn_ln2_w, L0_ffn_wq, L0_ffn_wk, L0_ffn_wv, L0_ffn_wo, L0_ffn_gate_w, L0_ffn_bias_e, L0_ffn_weg, L0_ffn_weu, L0_ffn_wed, L0_ffn_wsg, L0_ffn_wsu, L0_ffn_wsd):

    def _L0_attn_ref(x, W_Q, W_K, W_V, W_O, b_Q, b_K, b_V, b_O):
        import jax, jax.numpy as jnp
        import numpy as np
        BATCH, SEQ, D_MODEL, N_HEADS, D_HEAD = (2, 256, 256, 16, 128)
        ATTN_SCALE = np.sqrt(D_HEAD).astype(np.float32)
        IGNORE = jnp.float32(-100000.0)
        q = jnp.einsum('bpd,hde->bphe', x, W_Q) + b_Q
        k = jnp.einsum('bpd,hde->bphe', x, W_K) + b_K
        v = jnp.einsum('bpd,hde->bphe', x, W_V) + b_V
        scores = jnp.einsum('bqhe,bkhe->bhqk', q, k) / ATTN_SCALE
        S = x.shape[1]
        causal = jnp.tril(jnp.ones((S, S), bool))
        scores = jnp.where(causal, scores, IGNORE)
        attn = jax.nn.softmax(scores, axis=-1)
        z = jnp.einsum('bkhe,bhqk->bqhe', v, attn)
        out = jnp.einsum('bqhe,hed->bqd', z, W_O) + b_O
        return out

    def _L0_ffn_ref(hidden_states, ln1_w, ln2_w, wq, wk, wv, wo, gate_w, bias_e, weg, weu, wed, wsg, wsu, wsd):
        import jax, jax.numpy as jnp
        import numpy as np
        H = 256
        HQ = 16
        HKV = 4
        D = 128
        E = 32
        K = 4
        I = 128
        ISH = 128
        EPS = 1e-06
        THETA = 10000.0
        NORM_MIN = 1e-12

        def rmsnorm(x, w):
            xf = x.astype(jnp.float32)
            var = jnp.mean(xf * xf, axis=-1, keepdims=True)
            return w * (xf * jax.lax.rsqrt(var + EPS))

        def rotate_half(x):
            x1 = x[..., 0::2]
            x2 = x[..., 1::2]
            return jnp.stack((-x2, x1), axis=-1).reshape(x.shape)
        B, S, _ = hidden_states.shape
        resid = hidden_states
        x = rmsnorm(hidden_states, ln1_w)
        q = (x @ wq).reshape(B, S, HQ, D).transpose(0, 2, 1, 3)
        k = (x @ wk).reshape(B, S, HKV, D).transpose(0, 2, 1, 3)
        v = (x @ wv).reshape(B, S, HKV, D).transpose(0, 2, 1, 3)
        pos = jnp.arange(S, dtype=jnp.float32)
        inv_freq = 1.0 / THETA ** (jnp.arange(0, D, 2, dtype=jnp.float32) / D)
        ang = pos[:, None] * inv_freq[None, :]
        cos = jnp.repeat(jnp.cos(ang), 2, axis=-1)[None, None]
        sin = jnp.repeat(jnp.sin(ang), 2, axis=-1)[None, None]
        q = q * cos + rotate_half(q) * sin
        k = k * cos + rotate_half(k) * sin
        k = jnp.repeat(k, HQ // HKV, axis=1)
        v = jnp.repeat(v, HQ // HKV, axis=1)
        scores = jnp.einsum('bhqd,bhkd->bhqk', q, k) / jnp.sqrt(jnp.float32(D))
        causal = jnp.tril(jnp.ones((S, S), dtype=bool))
        scores = jnp.where(causal, scores, jnp.float32(-1000000000.0))
        attn = jax.nn.softmax(scores, axis=-1)
        o = jnp.einsum('bhqk,bhkd->bhqd', attn, v).transpose(0, 2, 1, 3).reshape(B, S, HQ * D)
        x = resid + o @ wo
        resid2 = x
        xn = rmsnorm(x, ln2_w)
        T = B * S
        xf = xn.reshape(T, H).astype(jnp.float32)
        router_logits = xf @ gate_w.T
        probs = jax.nn.softmax(router_logits, axis=-1)
        _, sel = jax.lax.top_k(probs + bias_e, K)
        rw = jnp.take_along_axis(probs, sel, axis=-1)
        rw = rw / jnp.maximum(jnp.sum(rw, axis=-1, keepdims=True), NORM_MIN)
        cw = jnp.zeros((T, E), jnp.float32).at[jnp.arange(T)[:, None], sel].set(rw)
        g = jnp.einsum('th,ehi->tei', xf, weg)
        u = jnp.einsum('th,ehi->tei', xf, weu)
        hmid = jax.nn.silu(g) * u * cw[:, :, None]
        moe_y = jnp.einsum('tei,eih->th', hmid, wed).reshape(B, S, H)
        shared = jax.nn.silu(xn @ wsg) * (xn @ wsu) @ wsd
        return resid2 + moe_y + shared
    x = L0_attn_x
    xn = _layernorm(x, axis=-1)
    x = x + _L0_attn_ref(xn, L0_attn_W_Q, L0_attn_W_K, L0_attn_W_V, L0_attn_W_O, L0_attn_b_Q, L0_attn_b_K, L0_attn_b_V, L0_attn_b_O) + _L0_ffn_ref(xn, L0_ffn_ln1_w, L0_ffn_ln2_w, L0_ffn_wq, L0_ffn_wk, L0_ffn_wv, L0_ffn_wo, L0_ffn_gate_w, L0_ffn_bias_e, L0_ffn_weg, L0_ffn_weu, L0_ffn_wed, L0_ffn_wsg, L0_ffn_wsu, L0_ffn_wsd)
    return x

_drawn_inputs = setup_inputs


def setup_inputs(seed=0):
    import zlib

    import numpy as np

    out = dict(_drawn_inputs(seed))
    spreads = {'L0_attn_b_Q': (0.0, 2.0),
     'L0_attn_b_K': (0.0, 2.0),
     'L0_attn_b_V': (0.0, 0.719),
     'L0_attn_b_O': (0.0, 2.0),
     'L0_ffn_ln1_w': (1.0, 0.6),
     'L0_ffn_ln2_w': (1.0, 0.6),
     'L0_ffn_bias_e': (0.0, 0.8)}
    factors = {'L0_ffn_wq': 8.0,
     'L0_ffn_wk': 8.0,
     'L0_ffn_wv': 3.276,
     'L0_ffn_wo': 3.288,
     'L0_ffn_gate_w': 8.0,
     'L0_ffn_weg': 8.0,
     'L0_ffn_weu': 8.0,
     'L0_ffn_wed': 8.0,
     'L0_ffn_wsg': 8.0,
     'L0_ffn_wsu': 8.0,
     'L0_ffn_wsd': 8.0,
     'L0_attn_W_Q': 3.926,
     'L0_attn_W_K': 3.736,
     'L0_attn_W_V': 2.909}
    for name, (base, spread) in spreads.items():
        noise = np.random.default_rng([zlib.crc32(name.encode()), seed]).standard_normal(out[name].shape)
        drawn = base * np.exp(spread * noise) if base else spread * noise
        out[name] = jnp.asarray(drawn.astype(out[name].dtype))
    for name, factor in factors.items():
        out[name] = (out[name] * factor).astype(out[name].dtype)
    return out
```

```python
import concourse.bass as bass
from concourse import mybir
from contextlib import ExitStack


def attention_pair_moe_kernel(
    nc: bass.Bass,
    x: bass.AP, W_Q: bass.AP, W_K: bass.AP, W_V: bass.AP, W_O: bass.AP,
    b_Q: bass.AP, b_K: bass.AP, b_V: bass.AP, b_O: bass.AP,
    ln1_w: bass.AP, ln2_w: bass.AP,
    wq: bass.AP, wk: bass.AP, wv: bass.AP, wo: bass.AP,
    gate_w: bass.AP, bias_e: bass.AP,
    weg: bass.AP, weu: bass.AP, wed: bass.AP,
    wsg: bass.AP, wsu: bass.AP, wsd: bass.AP,
    rope_table: bass.AP,
    out: bass.AP,
):
    f32, f32r = mybir.dt.float32, mybir.dt.float32r
    ALU = mybir.AluOpType
    ACT = mybir.ActivationFunctionType
    AX = mybir.AxisListType

    B, S, D = x.shape
    P = 128
    NH = W_Q.shape[0]
    E = gate_w.shape[0]
    TOPK = 4
    KD = D // P
    NT = B * S // P
    TB = S // P
    HALF = NH * B
    UNITS = 2 * HALF
    GS = 4 * B
    NPAIR = E // 2
    INV_SCALE = -float(P) ** -0.5
    MASKED = -1.0e30
    BIG = 3.0e38

    def chunks_of(n):
        if n == -2:
            return [("Krope", 0), ("Qrope", 0)]
        if n == -1:
            return [("VT", 0), ("Qrope", 1), ("Vx", 0)]
        v, c1, found = n + 2, n // 4 + 1, []
        if v < HALF:
            found.append(("Qrope", v))
        elif v < UNITS:
            found += [("Q", v), ("K", v)]
        if c1 < HALF // 4:
            if n % 4 < 3:
                found.append([("Krope", c1), ("VT", c1), ("Vx", c1)][n % 4])
        elif c1 < UNITS // 4:
            found += [[("V", c1, 0), ("V", c1, 1)], [("V", c1, 2)], [("V", c1, 3)], []][n % 4]
        return found

    CHUNK = {}
    for n in range(-2, UNITS):
        for ch in chunks_of(n):
            CHUNK[ch] = len(CHUNK)

    def late_k(n, steps):
        at = n - steps
        return [ch for ch in chunks_of(at) if ch[0] == "Krope"] if at >= 0 else []

    def jobs_of(n):
        if n == -2:
            return [("KV", 0)] + [(f"Q{q}", 0) for q in range(4)]
        a, s, found = n // GS, n % GS, []
        if n < 0 or n >= UNITS:
            return found
        if s == 0:
            found.append(("O0", a))
        if s == 3:
            if a + 1 < UNITS // GS:
                found.append(("KV", a + 1))
            found.append(("O1", a))
        if 4 <= s < 8 and a + 1 < UNITS // GS:
            found.append((f"Q{s - 4}", a + 1))
        return found

    JOB = {}
    for n in range(-2, UNITS):
        for job in jobs_of(n):
            JOB[job] = len(JOB)
    GA = HALF // GS
    START = 3
    CHUNKS_W = [sum(len(chunks_of(n)) for n in range(w, w + GS)) for w in (START, HALF + START)]
    ROT_W = {"Qrope": GS, "Krope": GS // 4}
    JOBS_W = 7
    assert all(c % 2 == 0 for c in CHUNKS_W)

    BLOCKS = [(3, 3), (0, 0), (0, 1), (0, 2), (0, 3), (1, 1), (1, 2), (1, 3), (2, 2), (2, 3)]
    PT_CHUNKS = [(0, 4), (4, 8), (8, 10)]
    PT_COLS = len(BLOCKS) * P + P
    PT_ROW = {0: (2 * P, 0), 1: (6 * P, P), 2: (9 * P, 2 * P), 3: (0, 2 * P)}
    P_OFF = [i * (i + 1) // 2 * P for i in range(TB)]
    P_COLS = TB * (TB + 1) // 2 * P
    PASSES = [(0, 0), (0, 1), (1, 0)]

    ctx = ExitStack()
    with ctx:
        def sb(name, cols, dt=f32, rows=P):
            return ctx.enter_context(nc.sbuf_tensor(name, [rows, cols], dt))

        def sem(name):
            return ctx.enter_context(nc.semaphore(name))

        accB_t = sb("acc_b", NT * D)
        accA_t = sb("acc_a", NT * D)
        xnT_t = sb("xnT", 2 * KD * NT * P, f32r)
        xrT_t = sb("xrT", 2 * KD * NT * P, f32r)
        q_t = sb("q_heads", 2 * 2 * S, f32r)
        k_t = sb("k_heads", 2 * 2 * S, f32r)
        v_t = sb("v_heads", 2 * 2 * TB * 4 * P, f32r)
        p_t = sb("probs", 2 * P_COLS)
        pt_t = sb("probsT", 2 * PT_COLS, f32r)
        z_t = sb("zT", 4 * 2 * S, f32r)
        wqk_t = sb("w_qk", 4 * 2 * 2 * KD * P, f32r)
        wkv_t = sb("w_kv", 2 * KD * 4 * P, f32r)
        wo_t = sb("w_o", 2 * 2 * 2 * D, f32r)
        rq_t = sb("raw_qk", 4 * 2 * KD * P)
        rkv_t = sb("raw_kv", KD * 4 * P)
        ro_t = sb("raw_o", 2 * 2 * D)
        rope_t = sb("rope", 2 * S)
        t1_t = sb("rope_sum", 3 * S)
        sw_t = sb("rope_swapped", 2 * S)
        vt_t = sb("vT", S)
        mask_t = sb("mask", S)
        ident = sb("ident", P)
        rows_t = sb("const_rows", P)
        cols_t = sb("const_cols", 64)
        gate_keep = sb("gate_cols", KD * E)
        bO_t = sb("b_o", D)
        be_t = sb("bias_e", E)
        nmax_t = sb("neg_max", 2 * TB)
        sum_t = sb("row_sum", 2 * TB)
        inv_t = sb("inv_sum", 2 * TB)
        stats_t = sb("ln_stats", NT * 6)
        mv_t = sb("ln_mean_var", NT * 2)
        var_t = sb("var", 4 * NT)
        rstd_t = sb("rstd", 4 * NT)
        mhalf_t = sb("minus_half", NT)
        cw_t = sb("combine", NT * E)
        rt_t = sb("router", 3 * NT * (E + TOPK))
        small_t = sb("router_small", NT * 8 + 4 * NT)

        accB = accB_t[:, :].rearrange("p (t d) -> p t d", t=NT)
        accA = accA_t[:, :].rearrange("p (t d) -> p t d", t=NT)
        xnT = xnT_t[:, :].rearrange("p (h k t) -> p h k t", h=2, k=KD)
        xrT = xrT_t[:, :].rearrange("p (h k t) -> p h k t", h=2, k=KD)
        qT = q_t[:, :].rearrange("p (s h t) -> p s h t", s=2, h=2)
        kT = k_t[:, :].rearrange("p (s h t) -> p s h t", s=2, h=2)
        vh = v_t[:, :].rearrange("p (s h t c) -> p s h t c", s=2, h=2, t=TB)
        pr = p_t[:, :].rearrange("p (s c) -> p s c", s=2)
        pT = pt_t[:, :].rearrange("p (h c) -> p h c", h=2)
        zT = z_t[:, :].rearrange("p (s h t) -> p s h t", s=4, h=2)
        wqk = wqk_t[:, :].rearrange("p (q w h k e) -> p q w h k e", q=4, w=2, h=2, k=KD)
        wkvA = wkv_t[:, :].rearrange("p (h c) -> p h c", h=2)
        wkvB = wkv_t[:, :].rearrange("p (h k e) -> p h k e", h=2, k=KD)
        w_o = wo_t[:, :].rearrange("p (o h j d) -> p o h j d", o=2, h=2, j=2)
        rq = rq_t[:, :].rearrange("p (q w k e) -> p q w k e", q=4, w=2, k=KD)
        ro = ro_t[:, :].rearrange("p (o j d) -> p o j d", o=2, j=2)
        cosT, sinT = rope_t[:, 0:S], rope_t[:, S:2 * S]
        t1 = t1_t[:, :].rearrange("p (s t) -> p s t", s=3)
        swapped = {"Qrope": sw_t[:, 0:S], "Krope": sw_t[:, S:2 * S]}
        rot_sum = lambda ch: t1[:, ch[1] % 2 if ch[0] == "Qrope" else 2]
        nmax = nmax_t[:, :].rearrange("p (s i) -> p s i", s=2)
        rsum = sum_t[:, :].rearrange("p (s i) -> p s i", s=2)
        rinv = inv_t[:, :].rearrange("p (s i) -> p s i", s=2)
        stats = stats_t[:, :].rearrange("p (t c) -> p t c", t=NT)
        mv = mv_t[:, :].rearrange("p (t c) -> p t c", t=NT)
        var = var_t[:, :].rearrange("p (w t) -> p w t", w=4)
        rstd = rstd_t[:, :].rearrange("p (w t) -> p w t", w=4)
        gaterow_t = sw_t[:, S:S + D]
        xr = p_t[:, 0:NT * D].rearrange("p (t d) -> p t d", t=NT)
        BQ, BK, BV, L1, L2 = 0, NH, 2 * NH, 3 * NH, 3 * NH + KD
        NROW = 3 * NH + 2 * KD
        cols = cols_t
        mgu = wqk_t[:, :].rearrange("p (s h k c) -> p s h k c", s=2, h=2, k=KD)
        mwd = wkv_t[:, :].rearrange("p (s h j d) -> p s h j d", s=2, h=2, j=2)
        rgu = rq_t[:, :].rearrange("p (s k c) -> p s k c", s=2, k=KD)
        rwd = rkv_t[:, :].rearrange("p (s j d) -> p s j d", s=2, j=2)
        gateT = q_t[:, 0:2 * KD * P].rearrange("p (h k e) -> p h k e", h=2, k=KD)
        hrow = p_t[:, 0:4 * 2 * P].rearrange("p (s t c) -> p s t c", s=2, t=2)
        silu = p_t[:, 4 * 2 * P:6 * 2 * P].rearrange("p (s c) -> p s c", s=2)
        hT = z_t[:, 0:2 * 2 * 4 * P].rearrange("p (s h c) -> p s h c", s=2, h=2)
        lgT = t1_t
        RW = E + TOPK
        route = rt_t[:, :].rearrange("p (w t e) -> p w t e", w=3, t=NT)
        cw = cw_t[:, :].rearrange("p (t e) -> p t e", t=NT)
        top8 = small_t[:, 0:NT * 8].rearrange("p (t e) -> p t e", t=NT)
        rsm = small_t[:, NT * 8:NT * 8 + 4 * NT].rearrange("p (w t) -> p w t", w=4)

        bank = {n: ctx.enter_context(nc.psum_tensor(n, [P, 512], f32))
                for n in ("s0", "s1", "t0", "t1", "j0", "j1", "zb", "ob")}
        bS = [bank["s0"], bank["s1"]]
        bT = [bank["t0"], bank["t1"]]
        bJ = [bank["j0"], bank["j1"]]
        bY = [bank["s0"], bank["s1"], bank["t0"], bank["t1"]]
        bH = [bank["zb"], bank["ob"]]

        x_in, rows_in, rope_in, bc_in = sem("x_in"), sem("rows_in"), sem("rope_in"), sem("bc_in")
        raw_in = {w: sem(f"raw_in_{w}") for w in ("KV", "Q0", "Q1", "Q2", "Q3", "O0", "O1")}
        consts = sem("pool_consts")
        zeroed = sem("zeroed")
        ln_step = sem("ln_vector")
        ln_ssq, ln_pow = sem("ssq_done"), sem("rstd_done")
        cx_mm, cx_ev = sem("const_turned"), sem("const_kept")
        x_mm, x_hi, x_lo = sem("x_turned"), sem("xT_hi"), sem("xT_lo")
        s_mm, s_free = sem("scores_done"), sem("scores_taken")
        e_done, r_done, p_norm = sem("exp_done"), sem("inverse_done"), sem("probs_normed")
        t_mm, pt_hi, pt_lo = sem("probs_turned"), sem("pT_hi"), sem("pT_lo")
        z_mm, z_hi, z_lo = sem("z_done"), sem("zT_hi"), sem("zT_lo")
        o_mm, o_add = sem("outproj_done"), sem("outproj_added")
        j_mm, j_hi, j_lo = sem("proj_done"), sem("proj_hi"), sem("proj_kept")
        sw_done, rp_sin, rp_sum, rp_hi, rp_lo = (
            {kind: sem(f"{kind}_{stage}") for kind in ("Qrope", "Krope")}
            for stage in ("swapped", "sin_done", "sum_done", "hi", "lo"))
        w_hi, w_done = sem("weights_hi"), sem("weights_split")
        lg_mm, lg_ev, lt_mm, rt = sem("logits_done"), sem("logits_kept"), sem("logits_turned"), sem("router_vector")
        rt_exp, cw_done = sem("router_exp"), sem("combine_done")
        g_hi = sem("gate_split")
        gu_mm, si_done, h_done = sem("gateup_done"), sem("silu_done"), sem("h_done")
        ht_mm, ht_hi, ht_lo = sem("h_turned"), sem("hT_hi"), sem("hT_lo")
        dn_mm = sem("down_done")
        mraw_gu = [sem("raw_gu0"), sem("raw_gu1")]
        mraw_d = [sem("raw_d0"), sem("raw_d1")]
        mw_hi, mw_done = sem("expert_weights_hi"), sem("expert_weights_split")
        waits_passed = sem("waits_passed")
        res_done, y_done, out_sem = sem("residual_sum"), sem("y_added"), sem("out_written")

        def until(eng, s, count, it=None, per=0):
            eng.wait_ge(s, count if it is None or per == 0 else it * per + count)

        def until_apart(eng, s, count, it=None, per=0):
            until(eng, s, count, it, per)
            stand_apart(eng, it)

        def stand_apart(eng, it):
            if it is not None:
                eng.sem_inc(waits_passed, 1)

        def windows(eng, step):
            for n in range(-2, START):
                step(n, None)
            for phase in range(2):
                first = phase * HALF + START
                with eng.Fori(0, GA - 1) as it:
                    for n in range(first, first + GS):
                        step(n, it)
                for n in range(first + (GA - 1) * GS, first + GA * GS):
                    step(n, None)

        block = ctx.enter_context(nc.Block())

        @block.sync
        def _(sp):
            xv = x.rearrange("b (t p) d -> p (b t) d", p=P)
            for b in range(B):
                sp.dma_start(accB[:, b * TB:(b + 1) * TB, :], xv[:, b * TB:(b + 1) * TB, :]).then_inc(x_in, 16)
            for at, src in ((BQ, b_Q), (BK, b_K), (BV, b_V)):
                sp.dma_start(rows_t[at:at + NH, :], src).then_inc(rows_in, 16)
            for at, src in ((L1, ln1_w), (L2, ln2_w)):
                sp.dma_start(rows_t[at:at + KD, :], src.rearrange("(k p) -> k p", p=P)).then_inc(rows_in, 16)
            sp.dma_start(gaterow_t[0:E, :], gate_w).then_inc(rows_in, 16)

            wqv = wq.rearrange("(k p) c -> p k c", p=P)
            wkv_ = wk.rearrange("(k p) c -> p k c", p=P)
            wvv = wv.rearrange("(k p) c -> p k c", p=P)
            wov = wo.rearrange("(h e) d -> e h d", e=P)

            def load(which, g, phase):
                if phase == 0:
                    if which == "KV":
                        for i, src in enumerate((wkv_, wvv)):
                            dst = rkv_t[:, i * KD * P:(i + 1) * KD * P].rearrange("p (k e) -> p k e", k=KD)
                            sp.dma_start(dst, src[:, :, bass.ds(g * P, P)]).then_inc(raw_in["KV"], 16)
                    elif which[0] == "Q":
                        q = int(which[1])
                        sp.dma_start(rq[:, q, 0], wqv[:, :, bass.ds(g * (4 * P) + q * P, P)]).then_inc(raw_in[which], 16)
                    else:
                        o = int(which[1])
                        sp.dma_start(ro[:, o], wov[:, bass.ds(g * 4 + 2 * o, 2), :]).then_inc(raw_in[which], 16)
                else:
                    if which == "KV":
                        for k in range(KD):
                            dst = rkv_t[:, k * 4 * P:(k + 1) * 4 * P].rearrange("p (h e) -> p h e", h=4)
                            sp.dma_start(dst, W_V[bass.ds(g * 4, 4), k * P:(k + 1) * P, :].rearrange("h p e -> p h e")
                                         ).then_inc(raw_in["KV"], 16)
                    elif which[0] == "Q":
                        q = int(which[1])
                        for i, src in enumerate((W_Q, W_K)):
                            sp.dma_start(rq[:, q, i], src[bass.ds(g * 4 + q, 1), :, :].rearrange("h (k p) e -> p (h k) e", p=P)
                                         ).then_inc(raw_in[which], 16)
                    else:
                        o = int(which[1])
                        sp.dma_start(ro[:, o], W_O[bass.ds(g * 4 + 2 * o, 2), :, :].rearrange("h e d -> e h d")
                                     ).then_inc(raw_in[which], 16)

            kinds = ("KV", "Q0", "Q1", "Q2", "Q3", "O0", "O1")
            for which in kinds:
                load(which, 0, 0)

            def loads(a, phase, g):
                for which in kinds:
                    done = {"KV": -6, "Q0": -5, "Q1": -4, "Q2": -3, "Q3": -2, "O0": -1, "O1": 1}[which]
                    sp.wait_ge(w_done, a * JOBS_W + done)
                    load(which, g, phase)

            with sp.Fori(1, GA) as a:
                loads(a, 0, a)
            with sp.Fori(GA, 2 * GA) as a:
                loads(a, 1, a - GA)

            sp.wait_ge(w_done, len(JOB))
            wsgv, wsuv = (w.rearrange("(k p) i -> p k i", p=P) for w in (wsg, wsu))

            def load_shared():
                for i, src in enumerate((wsgv, wsuv)):
                    sp.dma_start(rgu[:, 0, :, i * P:(i + 1) * P], src).then_inc(mraw_gu[0], 16)
                sp.dma_start(rwd[:, 0, 0], wsd).then_inc(mraw_d[0], 16)

            def load_pair(slot, m):
                for i, src in enumerate((weg, weu)):
                    for j in range(2):
                        at = (2 * i + j) * P
                        sp.dma_start(rgu[:, slot, :, at:at + P],
                                     src[bass.ds(m * 2 + j, 1), :, :].rearrange("e (k p) i -> p (e k) i", p=P)
                                     ).then_inc(mraw_gu[slot], 16)
                sp.dma_start(rwd[:, slot], wed[bass.ds(m * 2, 2), :, :].rearrange("e i d -> i e d")
                             ).then_inc(mraw_d[slot], 16)

            load_shared()
            load_pair(1, 0)
            with sp.Fori(1, NPAIR // 2) as r:
                for j in range(2):
                    sp.wait_ge(mw_done, r * 4 + 2 * j - 2)
                    load_pair(j, r * 2 + (j - 1))
            sp.wait_ge(mw_done, 2 * (NPAIR - 2) + 2)
            load_pair(0, NPAIR - 1)

            ov = out.rearrange("b (t p) d -> p (b t) d", p=P)
            for tp in range(NT // 2):
                sp.wait_ge(y_done, tp + 1)
                sp.dma_start(ov[:, 2 * tp:2 * tp + 2, :], accB[:, 2 * tp:2 * tp + 2, :]).then_inc(out_sem, 16)
            sp.wait_ge(out_sem, 16 * (NT // 2))

        @block.gpsimd
        def _(pool):
            pool.memset(ident[:, :], 0.0).then_inc(consts, 1)
            pool.memset(mask_t[:, :], 0.0).then_inc(consts, 1)
            pool.memset(mhalf_t[:, :], -0.5).then_inc(consts, 1)
            pool.wait_ge(consts, 2)
            pool.affine_select(out=ident[:, :], in_=ident[:, :], compare_op=ALU.not_equal, fill=1.0,
                               base=0, pattern=[[-1, P]], channel_multiplier=1).then_inc(consts, 1)
            diag = mask_t[:, S - P:S]
            pool.affine_select(out=diag, in_=diag, compare_op=ALU.is_ge, fill=MASKED,
                               base=0, pattern=[[-1, P]], channel_multiplier=1).then_inc(consts, 1)

            def power(w, count, src_ready, ready):
                pool.wait_ge(src_ready, ready)
                pool.tensor_tensor(rstd[:, w], var[:, w], mhalf_t[:, :], ALU.pow).then_inc(ln_pow, 1)

            pool.wait_ge(consts, 3)
            power(0, 1, ln_step, NT * 2 + 1)
            power(1, 2, ln_step, 3 * NT + 2)

            def weights(job, it):
                which, a = job
                phase, at = (0 if a < GA else 1), JOB[job]
                if which[0] == "Q":
                    count, per = (16 * (a + 1), 16) if phase == 0 else (16 * GA + 32 * (a - GA + 1), 32)
                elif which == "KV":
                    count, per = 32 * (a + 1), 32
                else:
                    count, per = 16 * (a + 1), 16
                until(pool, raw_in[which], count, it, per)
                if which[0] == "Q" and a:
                    v = GS * (a - 1) + 4 + int(which[1])
                    last = ("Qrope", v) if v < HALF else ("K", v)
                    until(pool, j_mm, CHUNK[last] + 1, it, CHUNKS_W[0 if v < HALF else 1])
                if which == "KV" and a:
                    c = 2 * (a - 1) + 1
                    last = ("VT", c) if c < HALF // 4 else ("V", c, 3)
                    until(pool, j_mm, CHUNK[last] + 1, it, CHUNKS_W[0 if c < HALF // 4 else 1])
                if which == "O0" and a:
                    until(pool, o_mm, GS * a - 2, it, GS)
                if which == "O1":
                    until(pool, o_mm, GS * a + 1, it, GS)
                if which[0] == "Q" and phase == 0:
                    q = int(which[1])
                    view = lambda ap: ap.rearrange("p k (w i) -> p k w i", w=2)
                    parts = [(view(wqk[:, q, 0, 0]), view(wqk[:, q, 0, 1]),
                              rq[:, q, 0].rearrange("p k (i w) -> p k w i", w=2))]
                elif which[0] == "Q":
                    q = int(which[1])
                    parts = [(wqk[:, q, :, 0], wqk[:, q, :, 1], rq[:, q])]
                elif which == "KV" and phase == 0:
                    half = KD * P
                    kk = lambda ap: ap[:, 0:half].rearrange("p (k w i) -> p k w i", k=KD, w=2)
                    parts = [(kk(wkvA[:, 0]), kk(wkvA[:, 1]),
                              rkv_t[:, 0:half].rearrange("p (k i w) -> p k w i", k=KD, w=2)),
                             (wkvA[:, 0, half:2 * half], wkvA[:, 1, half:2 * half], rkv_t[:, half:2 * half])]
                elif which == "KV":
                    parts = [(wkvA[:, 0], wkvA[:, 1], rkv_t[:, :])]
                else:
                    o = int(which[1])
                    parts = [(w_o[:, o, 0], w_o[:, o, 1], ro[:, o])]
                stand_apart(pool, it)
                for hi, _, raw in parts:
                    last = pool.tensor_scalar(hi, raw, 1.0, 1.0, ALU.mult, ALU.mult)
                last.then_inc(w_hi, 1)
                until(pool, w_hi, at + 1, it, JOBS_W)
                for hi, lo, raw in parts:
                    last = pool.tensor_tensor(lo, raw, hi.bitcast(f32), ALU.subtract)
                last.then_inc(w_done, 1)

            def normalise(n, it):
                if -1 <= n < UNITS - 1:
                    u = n + 1
                    for i in range(TB):
                        until_apart(pool, r_done, TB * u + i + 1, it, TB * GS)
                        piece = pr[:, u % 2, P_OFF[i]:P_OFF[i] + (i + 1) * P]
                        pool.tensor_scalar(piece, piece, rinv[:, u % 2, i:i + 1], 1.0,
                                           ALU.mult, ALU.mult).then_inc(p_norm, 1)

            def rope_los(n, it):
                if n < 0:
                    found = [ch for ch in chunks_of(n) if ch[0] in ROT_W]
                else:
                    found = [ch for ch in chunks_of(n) if ch[0] == "Qrope"] + late_k(n, 2)
                for kind, v in found:
                    until(pool, rp_hi[kind], v + 1, it, ROT_W[kind])
                    dst = (qT if kind == "Qrope" else kT)[:, v % 2]
                    pool.tensor_tensor(dst[:, 1], rot_sum((kind, v)), dst[:, 0].bitcast(f32),
                                       ALU.subtract).then_inc(rp_lo[kind], 1)

            def step(n, it):
                if n >= 0:
                    normalise(n, it)
                    rope_los(n, it)
                for job in jobs_of(n):
                    weights(job, it)
                if n < 0:
                    rope_los(n, it)
                    normalise(n, it)

            windows(pool, step)

            pool.wait_ge(j_mm, len(CHUNK))

            def expert_split(kind, M, it, raw_count, raw_per):
                slot = M % 2
                at = 2 * M + (kind == "d")
                if kind == "gu":
                    width = 2 * P if M == 0 else 4 * P
                    until(pool, mraw_gu[slot], raw_count, it, raw_per)
                    if M >= 2:
                        until(pool, gu_mm, 8 * M - 8, it, 16)
                    hi, lo, raw = mgu[:, slot, 0, :, 0:width], mgu[:, slot, 1, :, 0:width], rgu[:, slot, :, 0:width]
                else:
                    ne = 1 if M == 0 else 2
                    until(pool, mraw_d[slot], raw_count, it, raw_per)
                    if M >= 2:
                        until(pool, dn_mm, 4 * M - 4, it, 8)
                    hi, lo, raw = mwd[:, slot, 0, 0:ne], mwd[:, slot, 1, 0:ne], rwd[:, slot, 0:ne]
                stand_apart(pool, it)
                pool.tensor_scalar(hi, raw, 1.0, 1.0, ALU.mult, ALU.mult).then_inc(mw_hi, 1)
                until(pool, mw_hi, at + 1, it, 4)
                pool.tensor_tensor(lo, raw, hi.bitcast(f32), ALU.subtract).then_inc(mw_done, 1)

            def gu_raw(M):
                return 32 + 64 * (M // 2) if M % 2 == 0 else 64 * (M // 2 + 1)

            def d_raw(M):
                return 16 * (M // 2 + 1)

            expert_split("gu", 0, None, gu_raw(0), 0)
            power(2, 3, ln_step, 4 * NT + 3)
            expert_split("d", 0, None, d_raw(0), 0)
            expert_split("gu", 1, None, gu_raw(1), 0)
            expert_split("d", 1, None, d_raw(1), 0)
            expert_split("gu", 2, None, gu_raw(2), 0)
            with pool.Fori(0, NPAIR // 2 - 1) as it:
                expert_split("d", 2, it, d_raw(2), 16)
                expert_split("gu", 3, it, gu_raw(3), 64)
                expert_split("d", 3, it, d_raw(3), 16)
                expert_split("gu", 4, it, gu_raw(4), 64)
            expert_split("d", NPAIR, None, d_raw(NPAIR), 0)

        @block.tensor
        def _(pe):
            pe.wait_ge(consts, 4)
            pe.wait_ge(rows_in, 16 * 6)
            pe.transpose(bank["zb"][:, 0:NROW], rows_t[0:NROW, :], ident[0:NROW, 0:NROW])
            for k in range(KD):
                last = pe.transpose(bank["zb"][:, 64 + k * E:64 + (k + 1) * E],
                                    gaterow_t[0:E, k * P:(k + 1) * P], ident[0:E, 0:E])
            last.then_inc(cx_mm, 1)

            def turn_x(src, ready, first_bank):
                for b in range(B):
                    for k in range(KD):
                        for t in range(TB):
                            pe.wait_ge(ln_step, ready(b * TB + t))
                            last = pe.transpose(first_bank[b * KD + k][:, t * P:(t + 1) * P],
                                                src[:, b * TB + t, k * P:(k + 1) * P], ident[:, :])
                        last.then_inc(x_mm, 1)

            turn_x(xr, lambda t: 3 * NT + 3 + t, [bS[0], bS[1], bT[0], bT[1]])
            pe.wait_ge(cx_ev, 1)
            turn_x(accA, lambda t: 2 * NT + 2 + t, [bJ[0], bJ[1], bank["zb"], bank["ob"]])

            def mm3(dst, lhs, rhs, first, last_, skip=False):
                for i, (a, b) in enumerate(PASSES):
                    m = pe.matmul(dst, lhs(a), rhs(b), start=first and i == 0,
                                  stop=last_ and i == 2, skip_group_check=skip)
                return m

            def project(ch, it):
                at = CHUNK[ch]
                dst = bJ[at % 2]
                until(pe, j_lo, at + 1, it, per_of(ch))
                kind, v = ch[0], ch[1]
                if kind in ("Qrope", "Q", "K"):
                    a, b, q = v // GS, v % GS // 4, v % 4
                    src = xrT if kind == "Qrope" else xnT
                    until(pe, w_done, JOB[(f"Q{q}", a)] + 1, it, JOBS_W)
                    w = wqk[:, q, 1 if kind == "K" else 0]
                    for k in range(KD):
                        m = mm3(dst[:, :], lambda p: w[:, p, k, :],
                                lambda p: src[:, p, k, b * S:(b + 1) * S], k == 0, k == KD - 1)
                elif kind in ("Krope", "VT"):
                    a, b = v // 2, v % 2
                    until(pe, w_done, JOB[("KV", a)] + 1, it, JOBS_W)
                    half = KD * P
                    off = 0 if kind == "Krope" else half
                    for k in range(KD):
                        m = mm3(dst[:, :], lambda p: wkvA[:, p, off + k * P:off + (k + 1) * P],
                                lambda p: xrT[:, p, k, b * S:(b + 1) * S], k == 0, k == KD - 1)
                elif kind == "Vx":
                    until(pe, j_lo, CHUNK[("VT", v)] + 3, it, per_of(ch))
                    for t in range(TB):
                        m = pe.transpose(dst[:, t * P:(t + 1) * P], vt_t[:, t * P:(t + 1) * P], ident[:, :])
                else:
                    a, b, t = v // 2, v % 2, ch[2]
                    until(pe, w_done, JOB[("KV", a)] + 1, it, JOBS_W)
                    tok = (b * TB + t) * P
                    for k in range(KD):
                        m = mm3(dst[:, :], lambda p: xnT[:, p, k, tok:tok + P],
                                lambda p: wkvB[:, p, k, :], k == 0, k == KD - 1)
                m.then_inc(j_mm, 1)

            def per_of(ch):
                lim = HALF if ch[0] in ("Qrope", "Q", "K") else HALF // 4
                return CHUNKS_W[0 if ch[1] < lim else 1]

            def scores(u, i, it):
                until(pe, s_free, TB * u + i + 1, it, TB * GS)
                if i == 0:
                    if u < HALF:
                        until(pe, rp_lo["Qrope"], u + 1, it, ROT_W["Qrope"])
                        if u % 4 == 0:
                            until(pe, rp_lo["Krope"], u // 4 + 1, it, ROT_W["Krope"])
                    else:
                        until(pe, j_lo, CHUNK[("K", u)] + 3, it, CHUNKS_W[1])
                ks = u // 4 % 2 if u < HALF else u % 2
                width = max(2 * P, (i + 1) * P)
                mm3(bS[i % 2][:, 0:width], lambda p: qT[:, u % 2, p, i * P:(i + 1) * P],
                    lambda p: kT[:, ks, p, 0:width], True, True).then_inc(s_mm, 1)

            def turn_probs(u, c, it):
                at = 3 * u + c
                if c == 0:
                    until(pe, p_norm, TB * (u + 1), it, TB * GS)
                until(pe, pt_lo, at + 1, it, 3 * GS)
                lo_, hi_ = PT_CHUNKS[c]
                for j in range(lo_, hi_):
                    kt, qt = BLOCKS[j]
                    m = pe.transpose(bT[at % 2][:, (j - lo_) * P:(j - lo_ + 1) * P],
                                     pr[:, u % 2, P_OFF[qt] + kt * P:P_OFF[qt] + (kt + 1) * P], ident[:, :])
                m.then_inc(t_mm, 1)

            def attend(u, it):
                until(pe, pt_lo, 3 * u + 5, it, 3 * GS)
                until(pe, z_lo, u + 1, it, GS)
                if u % 4 == 0:
                    vc = ("Vx", u // 4) if u < HALF else ("V", u // 4, TB - 1)
                    until(pe, j_lo, CHUNK[vc] + 3, it, CHUNKS_W[0 if u < HALF else 1])
                col = 0 if u < HALF else u % 4 * P
                dst = bank["zb"]
                for kt in range(TB):
                    at, q0 = PT_ROW[kt]
                    m = mm3(dst[:, q0:S], lambda p: vh[:, u // 4 % 2, p, kt, col:col + P],
                            lambda p: pT[:, p, at:at + S - q0], kt == 0, kt == TB - 1, skip=True)
                m.then_inc(z_mm, 1)

            def out_project(n, t, it):
                o = n - 2
                m_, half = o // 2, o % 2
                a, b, hp = o // GS, o % GS // 4, m_ % 2
                if half == 0 and t == 0:
                    until(pe, z_lo, 2 * m_ + 3, it, GS)
                    until(pe, w_done, JOB[(f"O{hp}", a)] + 1, it, JOBS_W)
                if t == 0:
                    until(pe, o_add, o + 1, it, GS)
                tok = (2 * half + t) * P
                for j in range(2):
                    m = mm3(bank["ob"][:, t * D:(t + 1) * D],
                            lambda p: zT[:, (2 * m_ + j) % 4, p, tok:tok + P],
                            lambda p: w_o[:, hp, p, j, :], t == 0 and j == 0, t == 1 and j == 1, skip=True)
                if t == 1:
                    m.then_inc(o_mm, 1)

            def step(n, it):
                chs = chunks_of(n) if n < UNITS else []
                if n < 0:
                    if n == -2:
                        pe.wait_ge(x_lo, 2 * B * KD)
                    for ch in chs:
                        project(ch, it)
                    if n == -1:
                        for i in range(TB):
                            scores(0, i, it)
                        for c in range(2):
                            turn_probs(0, c, it)
                    return
                nxt = n + 1 < UNITS
                rotary = n + 2 < HALF
                if rotary:
                    project(chs[0], it)
                if nxt:
                    scores(n + 1, 0, it)
                    scores(n + 1, 1, it)
                if not rotary and 2 <= n < UNITS + 2:
                    out_project(n, 0, it)
                if n < UNITS:
                    turn_probs(n, 2, it)
                if nxt:
                    scores(n + 1, 2, it)
                    scores(n + 1, 3, it)
                if rotary and 2 <= n:
                    out_project(n, 0, it)
                if 2 <= n < UNITS + 2:
                    out_project(n, 1, it)
                for ch in [] if rotary else chs[:2]:
                    project(ch, it)
                if n < UNITS:
                    attend(n, it)
                for ch in chs[1:2] if rotary else []:
                    project(ch, it)
                if nxt:
                    turn_probs(n + 1, 0, it)
                    turn_probs(n + 1, 1, it)
                for ch in chs[2:]:
                    project(ch, it)

            windows(pe, step)

            turn_x(xr, lambda t: 4 * NT + 4 + t, [bJ[0], bJ[1], bank["zb"], bank["ob"]])
            pe.wait_ge(g_hi, 2)
            for b in range(B):
                pe.wait_ge(x_lo, 2 * B * KD + (b + 1) * KD)
                for k in range(KD):
                    m = mm3(bS[b][:, :], lambda p: gateT[:, p, k, :],
                            lambda p: xrT[:, p, k, b * S:(b + 1) * S], k == 0, k == KD - 1)
                m.then_inc(lg_mm, 1)
            pe.wait_ge(lg_ev, 2)
            for t in range(NT):
                m = pe.transpose(bT[0][:, t * E:(t + 1) * E], lgT[0:E, t * P:(t + 1) * P], ident[0:E, 0:E])
            m.then_inc(lt_mm, 1)

            NW = 4 * (NPAIR + 1)

            def gate_up(w, tt, it):
                M, tp, g = w // 4, w % 4, 2 * w + tt
                if g >= 2:
                    until(pe, h_done, g - 1, it, 16)
                if tt == 0:
                    until(pe, mw_done, 2 * M + 1, it, 4)
                width = 2 * P if M == 0 else 4 * P
                tok = (2 * tp + tt) * P
                for k in range(KD):
                    m = mm3(bJ[g % 2][:, 0:width], lambda p: xrT[:, p, k, tok:tok + P],
                            lambda p: mgu[:, M % 2, p, k, 0:width], k == 0, k == KD - 1)
                m.then_inc(gu_mm, 1)

            def turn_h(w, it):
                ne = 1 if w < 4 else 2
                until(pe, h_done, 2 * w + 2, it, 16)
                if w >= 2:
                    until(pe, ht_lo, w - 1, it, 8)
                for tt in range(2):
                    for j in range(ne):
                        c = tt * ne + j
                        m = pe.transpose(bH[w % 2][:, c * P:(c + 1) * P],
                                         hrow[:, w % 2, tt, j * P:(j + 1) * P], ident[:, :])
                m.then_inc(ht_mm, 1)

            def down(w, it):
                M, tp, ne = w // 4, w % 4, 1 if w < 4 else 2
                until(pe, ht_lo, w + 1, it, 8)
                if tp == 0:
                    until(pe, mw_done, 2 * M + 2, it, 4)
                for tt in range(2):
                    for j in range(ne):
                        c = tt * ne + j
                        m = mm3(bY[tp][:, tt * D:(tt + 1) * D],
                                lambda p: hT[:, w % 2, p, c * P:(c + 1) * P],
                                lambda p: mwd[:, M % 2, p, j, :],
                                w < 4 and tt == 0 and j == 0, w >= NW - 4, skip=True)
                m.then_inc(dn_mm, 1)

            def expert_step(w, it):
                if w + 1 < NW:
                    gate_up(w + 1, 0, it)
                turn_h(w, it)
                if w + 1 < NW:
                    gate_up(w + 1, 1, it)
                if w >= 1:
                    down(w - 1, it)

            gate_up(0, 0, None)
            gate_up(0, 1, None)
            pe.wait_ge(rt, 2)
            for w in range(5):
                expert_step(w, None)
            with pe.Fori(0, NPAIR // 2 - 1) as it:
                for w in range(5, 13):
                    expert_step(w, it)
            for w in range(5 + 8 * (NPAIR // 2 - 1), NW):
                expert_step(w, None)
            down(NW - 1, None)

        @block.scalar
        def _(act):
            act.dma_start(rope_t[:, :], rope_table).then_inc(rope_in, 16)
            act.dma_start(bO_t[:, :], b_O.rearrange("(a d) -> a d", a=1).broadcast_to([P, D])).then_inc(bc_in, 16)
            act.dma_start(be_t[:, :], bias_e.rearrange("(a d) -> a d", a=1).broadcast_to([P, E])).then_inc(bc_in, 16)

            def squares(src, ready, scratch, w):
                for t in range(NT):
                    act.wait_ge(ln_step, ready(t)) if ready else None
                    if t or w == 2:
                        act.wait_ge(ln_ssq, (w - 1) * NT + t)
                    act.activation(scratch, src[:, t, :], ACT.Square,
                                   accum_out=var[:, 3, t:t + 1]).then_inc(ln_ssq, 1)

            squares(accA, lambda t: 2 * NT + 2 + t, t1_t[:, 0:D], 1)

            def turned(src_hi, count0, banks, scale_at):
                for i in range(B * KD):
                    b, k = i // KD, i % KD
                    act.wait_ge(x_mm, count0 + i + 1)
                    dst = src_hi[:, 0, k, b * S:(b + 1) * S]
                    if scale_at is None:
                        act.activation(dst, banks[i][:, :], ACT.Copy).then_inc(x_hi, 1)
                    else:
                        act.activation(dst, banks[i][:, :], ACT.Identity,
                                       scale=cols[:, scale_at + k:scale_at + k + 1]).then_inc(x_hi, 1)

            act.wait_ge(cx_ev, 1)
            turned(xrT, 0, [bS[0], bS[1], bT[0], bT[1]], L1)
            turned(xnT, B * KD, [bJ[0], bJ[1], bank["zb"], bank["ob"]], None)

            def exp(u, i, it):
                until(act, s_free, TB * u + i + 3, it, TB * GS)
                piece = pr[:, u % 2, P_OFF[i]:P_OFF[i] + (i + 1) * P]
                act.activation(piece, piece, ACT.Exp, bias=nmax[:, u % 2, i:i + 1], scale=-1.0,
                               accum_out=rsum[:, u % 2, i:i + 1]).then_inc(e_done, 1)

            def probs_hi(u, c, it):
                until(act, t_mm, 3 * u + c + 1, it, 3 * GS)
                a, b = PT_CHUNKS[c]
                act.activation(pT[:, 0, (a + 1) * P:(b + 1) * P], bT[(3 * u + c) % 2][:, 0:(b - a) * P],
                               ACT.Copy).then_inc(pt_hi, 1)

            def z_part(u, it):
                until(act, z_mm, u + 1, it, GS)
                dst = zT[:, u % 4, 0, :]
                if u < HALF:
                    act.activation(dst, bank["zb"][:, :], ACT.Copy).then_inc(z_hi, 1)
                else:
                    stand_apart(act, it)
                    act.activation(dst, bank["zb"][:, :], ACT.Identity, bias=col_of(BV, u, it)).then_inc(z_hi, 1)

            def col_of(base, u, it):
                h = 4 * ((u - HALF) // GS) + u % 4 + base
                return cols[:, h:h + 1] if it is None else cols[:, bass.ds(it * 4 + h, 1)]

            def chunk_a(ch, it):
                at, kind, v = CHUNK[ch], ch[0], ch[1]
                src = bJ[at % 2]
                per = CHUNKS_W[0 if kind in ("Qrope", "Krope", "VT", "Vx") else 1]
                until(act, j_mm, at + 1, it, per)
                if kind in ROT_W:
                    if v:
                        until(act, rp_sum[kind], v, it, ROT_W[kind])
                    act.activation(swapped[kind][0:P // 2, :], src[P // 2:P, :], ACT.Copy)
                    act.activation(swapped[kind][P // 2:P, :], src[0:P // 2, :],
                                   ACT.Copy).then_inc(sw_done[kind], 1)
                elif kind == "VT":
                    until(act, j_lo, at + 2, it, per)
                    act.activation(vt_t[:, :], src[:, :], ACT.Copy).then_inc(j_lo, 1)
                elif kind in ("Q", "K"):
                    dst = (qT if kind == "Q" else kT)[:, v % 2, 0]
                    stand_apart(act, it)
                    act.activation(dst, src[:, :], ACT.Identity,
                                   bias=col_of(BQ if kind == "Q" else BK, v, it)).then_inc(j_hi, 1)
                elif kind == "Vx":
                    act.activation(vh[:, v % 2, 0, :, 0:P], src[:, :].rearrange("p (t e) -> p t e", t=TB),
                                   ACT.Copy).then_inc(j_hi, 1)
                else:
                    act.activation(vh[:, v % 2, 0, ch[2], :], src[:, :], ACT.Copy).then_inc(j_hi, 1)

            def chunk_b(ch, it):
                kind, v = ch[0], ch[1]
                if kind in ROT_W:
                    until(act, rp_sum[kind], v + 1, it, ROT_W[kind])
                    dst = (qT if kind == "Qrope" else kT)[:, v % 2, 0]
                    act.activation(dst, rot_sum(ch), ACT.Copy).then_inc(rp_hi[kind], 1)

            def step(n, it):
                chs = chunks_of(n) if n < UNITS else []
                if n < 0:
                    for ch in chs:
                        chunk_a(ch, it)
                        chunk_b(ch, it)
                    if n == -1:
                        for i in range(TB):
                            exp(0, i, it)
                        probs_hi(0, 0, it)
                        probs_hi(0, 1, it)
                    return
                nxt = n + 1 < UNITS
                rotary = n + 2 < HALF
                if rotary:
                    chunk_a(chs[0], it)
                if nxt:
                    exp(n + 1, 0, it)
                    exp(n + 1, 1, it)
                if n < UNITS:
                    probs_hi(n, 2, it)
                if nxt:
                    exp(n + 1, 2, it)
                    exp(n + 1, 3, it)
                if rotary:
                    chunk_b(chs[0], it)
                for ch in late_k(n, 2):
                    chunk_b(ch, it)
                for ch in [] if rotary else chs[:2]:
                    chunk_a(ch, it)
                if n < UNITS:
                    z_part(n, it)
                if nxt:
                    probs_hi(n + 1, 0, it)
                    probs_hi(n + 1, 1, it)
                for ch in chs[1:2] if rotary else []:
                    chunk_a(ch, it)
                for ch in chs[2:]:
                    chunk_a(ch, it)

            windows(act, step)

            act.wait_ge(o_add, HALF * 2 + 1)
            squares(accA, None, t1_t[:, 0:D], 2)
            turned(xrT, 2 * B * KD, [bJ[0], bJ[1], bank["zb"], bank["ob"]], L2)
            act.wait_ge(rt, 2)
            act.activation(route[:, 0, :, 0:E], route[:, 0, :, 0:E], ACT.Exp).then_inc(rt_exp, 1)

            NW = 4 * (NPAIR + 1)

            def silu_of(w, tt, it):
                g, width = 2 * w + tt, P if w < 4 else 2 * P
                until(act, gu_mm, g + 1, it, 16)
                if g >= 2:
                    until(act, h_done, g - 1, it, 16)
                act.activation(silu[:, g % 2, 0:width], bJ[g % 2][:, 0:width], ACT.Silu).then_inc(si_done, 1)

            def h_hi(w, it):
                width = 2 * P if w < 4 else 4 * P
                until(act, ht_mm, w + 1, it, 8)
                act.activation(hT[:, w % 2, 0, 0:width], bH[w % 2][:, 0:width], ACT.Copy).then_inc(ht_hi, 1)

            def expert_step(w, it):
                if w + 1 < NW:
                    silu_of(w + 1, 0, it)
                h_hi(w, it)
                if w + 1 < NW:
                    silu_of(w + 1, 1, it)

            silu_of(0, 0, None)
            silu_of(0, 1, None)
            for w in range(5):
                expert_step(w, None)
            with act.Fori(0, NPAIR // 2 - 1) as it:
                for w in range(5, 13):
                    expert_step(w, it)
            for w in range(5 + 8 * (NPAIR // 2 - 1), NW):
                expert_step(w, None)

        @block.vector
        def _(ve):
            ve.memset(pT[:, 0, 0:P].bitcast(f32), 0.0).then_inc(zeroed, 1)
            ve.memset(pT[:, 1, 0:P].bitcast(f32), 0.0).then_inc(zeroed, 1)
            ve.sem_inc(s_free, 2)
            ve.sem_inc(pt_lo, 2)
            ve.sem_inc(j_lo, 2)
            ve.sem_inc(z_lo, 1)
            ve.sem_inc(o_add, 1)

            done = [0]

            def did(ins):
                done[0] += 1
                ins.then_inc(ln_step, 1)

            for t in range(NT):
                if t % TB == 0:
                    ve.wait_ge(x_in, 16 * B)
                did(ve.bn_stats(stats[:, t, :], accB[:, t, :]))
            for t in range(NT):
                ve.wait_ge(ln_step, t + 1)
                did(ve.bn_aggr(mv[:, t, :], stats[:, t, :]))
            ve.wait_ge(ln_step, 2 * NT)
            did(ve.tensor_scalar(var[:, 0], mv[:, :, 1], 1e-05, None, ALU.add))
            assert done[0] == 2 * NT + 1
            ve.wait_ge(ln_pow, 1)
            ve.wait_ge(ln_step, 2 * NT + 1)
            for t in range(NT):
                did(ve.tensor_scalar(accA[:, t, :], accB[:, t, :], mv[:, t, 0:1], rstd[:, 0, t:t + 1],
                                     ALU.subtract, ALU.mult))
            ve.wait_ge(ln_ssq, NT)
            did(ve.tensor_scalar(var[:, 1], var[:, 3], 1.0 / D, 1e-06, ALU.mult, ALU.add))
            assert done[0] == 3 * NT + 2
            ve.wait_ge(ln_pow, 2)
            ve.wait_ge(ln_step, 3 * NT + 2)
            for t in range(NT):
                did(ve.tensor_scalar(xr[:, t, :], accA[:, t, :], rstd[:, 1, t:t + 1], None, ALU.mult))
            ve.wait_ge(cx_mm, 1)
            ve.tensor_copy(cols[:, 0:NROW], bank["zb"][:, 0:NROW])
            ve.tensor_copy(gate_keep[:, :], bank["zb"][:, 64:64 + KD * E]).then_inc(cx_ev, 1)

            def turned(dst, count0, banks, scale_at):
                for i in range(B * KD):
                    b, k = i // KD, i % KD
                    ve.wait_ge(x_hi, count0 + i + 1)
                    hi = dst[:, 0, k, b * S:(b + 1) * S].bitcast(f32)
                    lo = dst[:, 1, k, b * S:(b + 1) * S]
                    if scale_at is None:
                        ve.tensor_tensor(lo, banks[i][:, :], hi, ALU.subtract).then_inc(x_lo, 1)
                    else:
                        ve.scalar_tensor_tensor(out=lo, in0=banks[i][:, :],
                                                scalar=cols[:, scale_at + k:scale_at + k + 1], in1=hi,
                                                op0=ALU.mult, op1=ALU.subtract).then_inc(x_lo, 1)

            ve.wait_ge(cx_ev, 1)
            turned(xrT, 0, [bS[0], bS[1], bT[0], bT[1]], L1)
            turned(xnT, B * KD, [bJ[0], bJ[1], bank["zb"], bank["ob"]], None)
            ve.wait_ge(bc_in, 32)
            for t in range(NT):
                last = ve.tensor_tensor(accB[:, t, :], accB[:, t, :], bO_t[:, :], ALU.add)
            last.then_inc(zeroed, 1)
            ve.wait_ge(zeroed, 3)
            ve.wait_ge(consts, 5)
            ve.wait_ge(rope_in, 16)

            def mask_scores(u, i, it):
                until_apart(ve, s_mm, TB * u + i + 1, it, TB * GS)
                width = (i + 1) * P
                ve.tensor_tensor_reduce(pr[:, u % 2, P_OFF[i]:P_OFF[i] + width], bS[i % 2][:, 0:width],
                                        mask_t[:, S - width:S], INV_SCALE, BIG, ALU.add, ALU.min,
                                        nmax[:, u % 2, i:i + 1]).then_inc(s_free, 1)

            def invert(u, i, it):
                until(ve, e_done, TB * u + i + 1, it, TB * GS)
                ve.reciprocal(rinv[:, u % 2, i:i + 1], rsum[:, u % 2, i:i + 1]).then_inc(r_done, 1)

            def probs_lo(u, c, it):
                until(ve, pt_hi, 3 * u + c + 1, it, 3 * GS)
                a, b = PT_CHUNKS[c]
                cs = slice((a + 1) * P, (b + 1) * P)
                ve.tensor_tensor(pT[:, 1, cs], bT[(3 * u + c) % 2][:, 0:(b - a) * P],
                                 pT[:, 0, cs].bitcast(f32), ALU.subtract).then_inc(pt_lo, 1)

            def col_of(base, u, it):
                h = 4 * ((u - HALF) // GS) + u % 4 + base
                return cols[:, h:h + 1] if it is None else cols[:, bass.ds(it * 4 + h, 1)]

            def z_part(u, it):
                until(ve, z_hi, u + 1, it, GS)
                hi, lo = zT[:, u % 4, 0, :].bitcast(f32), zT[:, u % 4, 1, :]
                if u < HALF:
                    ve.tensor_tensor(lo, bank["zb"][:, :], hi, ALU.subtract).then_inc(z_lo, 1)
                else:
                    ve.scalar_tensor_tensor(out=lo, in0=bank["zb"][:, :], scalar=col_of(BV, u, it), in1=hi,
                                            op0=ALU.add, op1=ALU.subtract).then_inc(z_lo, 1)

            HI = {}
            for ch in CHUNK:
                if ch[0] not in ROT_W and ch[0] != "VT":
                    HI[ch] = len(HI)
            HI_W = [2, CHUNKS_W[1]]

            def chunk(ch, it):
                at, kind, v = CHUNK[ch], ch[0], ch[1]
                src = bJ[at % 2]
                phase = 0 if kind in ("Qrope", "Krope", "VT", "Vx") else 1
                if kind in ROT_W:
                    until(ve, j_mm, at + 1, it, CHUNKS_W[phase])
                    slots = 2 if kind == "Qrope" else 1
                    if v >= slots:
                        until(ve, rp_lo[kind], v + 1 - slots, it, ROT_W[kind])
                    until(ve, sw_done[kind], v + 1, it, ROT_W[kind])
                    ve.tensor_tensor(rot_sum(ch), src[:, :], cosT, ALU.mult).then_inc(j_lo, 1)
                elif kind != "VT":
                    until(ve, j_hi, HI[ch] + 1, it, HI_W[phase])
                    if kind in ("Q", "K"):
                        dst = (qT if kind == "Q" else kT)[:, v % 2]
                        ve.scalar_tensor_tensor(out=dst[:, 1], in0=src[:, :],
                                                scalar=col_of(BQ if kind == "Q" else BK, v, it),
                                                in1=dst[:, 0].bitcast(f32),
                                                op0=ALU.add, op1=ALU.subtract).then_inc(j_lo, 1)
                    elif kind == "Vx":
                        ve.tensor_tensor(vh[:, v % 2, 1, :, 0:P], src[:, :].rearrange("p (t e) -> p t e", t=TB),
                                         vh[:, v % 2, 0, :, 0:P].bitcast(f32), ALU.subtract).then_inc(j_lo, 1)
                    else:
                        ve.tensor_tensor(vh[:, v % 2, 1, ch[2], :], src[:, :],
                                         vh[:, v % 2, 0, ch[2], :].bitcast(f32), ALU.subtract).then_inc(j_lo, 1)

            def rope_sin(ch, it):
                if ch[0] in ROT_W:
                    half = swapped[ch[0]]
                    ve.tensor_tensor(half, half, sinT, ALU.mult).then_inc(rp_sin[ch[0]], 1)

            def rope_sum(ch, it):
                if ch[0] in ROT_W:
                    until(ve, rp_sin[ch[0]], ch[1] + 1, it, ROT_W[ch[0]])
                    ve.tensor_tensor(rot_sum(ch), rot_sum(ch), swapped[ch[0]], ALU.add
                                     ).then_inc(rp_sum[ch[0]], 1)

            def add_out(n, it):
                o = n - 2
                half, b = o % 2, o % GS // 4
                acc = accA if o < HALF else accB
                until(ve, o_mm, o + 1, it, GS)
                until(ve, o_add, o + 1, it, GS)
                t = b * TB + 2 * half
                tiles = acc[:, t:t + 2, :]
                ve.tensor_tensor(tiles, bank["ob"][:, :].rearrange("p (t d) -> p t d", t=2), tiles,
                                 ALU.add).then_inc(o_add, 1)

            def step(n, it):
                chs = chunks_of(n) if n < UNITS else []
                if n < 0:
                    for ch in chs:
                        chunk(ch, it)
                        rope_sin(ch, it)
                        rope_sum(ch, it)
                    if n == -1:
                        for i in range(TB):
                            mask_scores(0, i, it)
                        for i in range(TB):
                            invert(0, i, it)
                        probs_lo(0, 0, it)
                        probs_lo(0, 1, it)
                    return
                nxt = n + 1 < UNITS
                rotary = n + 2 < HALF
                if nxt:
                    mask_scores(n + 1, 0, it)
                    mask_scores(n + 1, 1, it)
                if rotary:
                    chunk(chs[0], it)
                if n < UNITS and not rotary:
                    probs_lo(n, 2, it)
                if nxt:
                    mask_scores(n + 1, 2, it)
                    invert(n + 1, 0, it)
                    invert(n + 1, 1, it)
                    mask_scores(n + 1, 3, it)
                    invert(n + 1, 2, it)
                if rotary:
                    probs_lo(n, 2, it)
                    rope_sin(chs[0], it)
                    rope_sum(chs[0], it)
                if nxt:
                    invert(n + 1, 3, it)
                if 2 <= n < UNITS + 2:
                    add_out(n, it)
                for ch in late_k(n, 1):
                    rope_sin(ch, it)
                for ch in [] if rotary else chs[:2]:
                    chunk(ch, it)
                if n < UNITS:
                    z_part(n, it)
                if nxt:
                    probs_lo(n + 1, 0, it)
                    probs_lo(n + 1, 1, it)
                for ch in late_k(n, 1):
                    rope_sum(ch, it)
                for ch in chs[1:2] if rotary else []:
                    chunk(ch, it)
                for ch in chs[2:]:
                    chunk(ch, it)

            windows(ve, step)

            for h in range(2):
                ve.memset(gateT[:, h].bitcast(f32), 0.0).then_inc(zeroed, 1)
            ve.wait_ge(zeroed, 5)
            gk = gate_keep[:, :].rearrange("p (k e) -> p k e", k=KD)
            ve.tensor_copy(gateT[:, 0, :, 0:E], gk).then_inc(g_hi, 1)
            ve.wait_ge(g_hi, 1)
            ve.tensor_tensor(gateT[:, 1, :, 0:E], gk, gateT[:, 0, :, 0:E].bitcast(f32),
                             ALU.subtract).then_inc(g_hi, 1)
            ve.wait_ge(ln_ssq, 2 * NT)
            did(ve.tensor_scalar(var[:, 2], var[:, 3], 1.0 / D, 1e-06, ALU.mult, ALU.add))
            assert done[0] == 4 * NT + 3
            ve.wait_ge(ln_pow, 3)
            for t in range(NT):
                did(ve.tensor_scalar(xr[:, t, :], accA[:, t, :], rstd[:, 2, t:t + 1], None, ALU.mult))
            turned(xrT, 2 * B * KD, [bJ[0], bJ[1], bank["zb"], bank["ob"]], L2)
            for b in range(B):
                ve.wait_ge(lg_mm, b + 1)
                ve.tensor_copy(lgT[0:E, b * S:(b + 1) * S], bS[b][0:E, :]).then_inc(lg_ev, 1)

            over = lambda ap: ap.unsqueeze(2).to_broadcast([P, NT, E])
            logits = bT[0][:, 0:NT * E].rearrange("p (t e) -> p t e", t=NT)
            probs, biased, left = (route[:, i, :, 0:E] for i in range(3))
            count = [0]

            def then(ins):
                count[0] += 1
                ins.then_inc(rt, 1)
                ve.wait_ge(rt, count[0])

            ve.wait_ge(lt_mm, 1)
            then(ve.tensor_reduce(rsm[:, 0], logits, AX.X, ALU.max))
            then(ve.tensor_tensor(probs, logits, over(rsm[:, 0]), ALU.subtract))
            ve.wait_ge(rt_exp, 1)
            then(ve.tensor_reduce(rsm[:, 1], probs, AX.X, ALU.add))
            then(ve.reciprocal(rsm[:, 2], rsm[:, 1]))
            then(ve.tensor_tensor(probs, probs, over(rsm[:, 2]), ALU.mult))
            then(ve.tensor_tensor(biased, probs, be_t[:, :].unsqueeze(1).to_broadcast([P, NT, E]), ALU.add))
            then(ve.memset(route[:, 1, :, E:RW], -BIG))
            for t in range(NT):
                then(ve.max(top8[:, t, :], route[:, 1, t, 0:E]))
            then(ve.memset(top8[:, :, TOPK:8], -BIG))
            for t in range(NT):
                then(ve.match_replace(out=route[:, 2, t, :], in_to_replace=top8[:, t, :],
                                      in_values=route[:, 1, t, :], imm_value=-0.5 * BIG))
            then(ve.tensor_tensor(left, left, biased, ALU.not_equal))
            then(ve.tensor_tensor(cw, probs, left, ALU.mult))
            then(ve.tensor_reduce(rsm[:, 3], cw, AX.X, ALU.add))
            then(ve.tensor_scalar(rsm[:, 0], rsm[:, 3], 1e-12, None, ALU.max))
            then(ve.reciprocal(rsm[:, 1], rsm[:, 0]))
            then(ve.tensor_tensor(cw, cw, over(rsm[:, 1]), ALU.mult))
            ve.tensor_tensor(accB_t[:, :], accB_t[:, :], accA_t[:, :], ALU.add).then_inc(res_done, 1)

            NW = 4 * (NPAIR + 1)

            def make_h(w, tt, it):
                M, g, tile = w // 4, 2 * w + tt, 2 * (w % 4) + tt
                until(ve, si_done, g + 1, it, 16)
                if M == 0:
                    ve.tensor_tensor(hrow[:, w % 2, tt, 0:P], bJ[g % 2][:, P:2 * P], silu[:, g % 2, 0:P],
                                     ALU.mult).then_inc(h_done, 1)
                    return
                for j in range(2):
                    e = 2 * (M - 1) + j
                    c = cw[:, tile, e:e + 1] if it is None else cw[:, tile, bass.ds(it * 4 + e, 1)]
                    last = ve.scalar_tensor_tensor(out=hrow[:, w % 2, tt, j * P:(j + 1) * P],
                                                   in0=silu[:, g % 2, j * P:(j + 1) * P], scalar=c,
                                                   in1=bJ[g % 2][:, (2 + j) * P:(3 + j) * P],
                                                   op0=ALU.mult, op1=ALU.mult)
                last.then_inc(h_done, 1)

            def h_lo(w, it):
                width = 2 * P if w < 4 else 4 * P
                until(ve, ht_hi, w + 1, it, 8)
                ve.tensor_tensor(hT[:, w % 2, 1, 0:width], bH[w % 2][:, 0:width],
                                 hT[:, w % 2, 0, 0:width].bitcast(f32), ALU.subtract).then_inc(ht_lo, 1)

            def expert_step(w, it):
                if w + 1 < NW:
                    make_h(w + 1, 0, it)
                h_lo(w, it)
                if w + 1 < NW:
                    make_h(w + 1, 1, it)

            make_h(0, 0, None)
            make_h(0, 1, None)
            for w in range(5):
                expert_step(w, None)
            with ve.Fori(0, NPAIR // 2 - 1) as it:
                for w in range(5, 13):
                    expert_step(w, it)
            for w in range(5 + 8 * (NPAIR // 2 - 1), NW):
                expert_step(w, None)
            ve.wait_ge(res_done, 1)
            for tp in range(NT // 2):
                ve.wait_ge(dn_mm, NW - 4 + tp + 1)
                tiles = accB[:, 2 * tp:2 * tp + 2, :]
                ve.tensor_tensor(tiles, bY[tp][:, :].rearrange("p (t d) -> p t d", t=2), tiles,
                                 ALU.add).then_inc(y_done, 1)


_A = ["x", "W_Q", "W_K", "W_V", "W_O", "b_Q", "b_K", "b_V", "b_O"]
_F = ["ln1_w", "ln2_w", "wq", "wk", "wv", "wo", "gate_w", "bias_e", "weg", "weu", "wed", "wsg", "wsu", "wsd"]
_INS = [f"L0_attn_{n}" for n in _A] + [f"L0_ffn_{n}" for n in _F]


def _rope_table(positions, d, theta):
    import numpy as np

    f = np.float32
    inv_freq = (f(1.0) / np.power(f(theta), np.arange(0, d, 2, dtype=f) / f(d))).astype(f)
    angle = (np.arange(positions, dtype=f)[None, :] * inv_freq[:, None]).astype(f)
    cos, sin = np.cos(angle).astype(f), np.sin(angle).astype(f)
    return np.concatenate([np.concatenate([cos, cos]), np.concatenate([-sin, sin])], axis=1)


def kernel(**inputs):
    import numpy as _np
    import concourse.bacc as _bacc
    from concourse import mybir as _mybir
    from concourse.bass_utils import run_bass_kernel_spmd as _run

    nc = _bacc.Bacc("TRN2", target_bir_lowering=False, num_devices=1)
    arrays, args = {}, []
    named = {n: _np.ascontiguousarray(inputs[n]) for n in _INS}
    seq, d_head = named["L0_attn_x"].shape[1], named["L0_attn_W_Q"].shape[2]
    named["rope_table"] = _rope_table(seq, d_head, 10000.0)
    for name, a in named.items():
        arrays[f"in_{name}_dram"] = a
        args.append(nc.dram_tensor(f"in_{name}_dram", a.shape, _mybir.dt.from_np(a.dtype), kind="ExternalInput").ap())
    shape = named["L0_attn_x"].shape
    args.append(nc.dram_tensor("out_0_dram", shape, _mybir.dt.float32, kind="ExternalOutput").ap())
    attention_pair_moe_kernel(nc, *args)
    r = _run(nc, [arrays], core_ids=[0])
    return r.results[0]["out_0_dram"]
```

```python
import concourse.bass as bass
from concourse import mybir
from contextlib import ExitStack


def attention_pair_moe_kernel(
    nc: bass.Bass,
    x: bass.AP, W_Q: bass.AP, W_K: bass.AP, W_V: bass.AP, W_O: bass.AP,
    b_Q: bass.AP, b_K: bass.AP, b_V: bass.AP, b_O: bass.AP,
    ln1_w: bass.AP, ln2_w: bass.AP,
    wq: bass.AP, wk: bass.AP, wv: bass.AP, wo: bass.AP,
    gate_w: bass.AP, bias_e: bass.AP,
    weg: bass.AP, weu: bass.AP, wed: bass.AP,
    wsg: bass.AP, wsu: bass.AP, wsd: bass.AP,
    rope_table: bass.AP,
    out: bass.AP,
):
    f32, f32r = mybir.dt.float32, mybir.dt.float32r
    ALU = mybir.AluOpType
    ACT = mybir.ActivationFunctionType
    AX = mybir.AxisListType

    B, S, D = x.shape
    P = 128
    NH = W_Q.shape[0]
    E = gate_w.shape[0]
    TOPK = 4
    KD = D // P
    NT = B * S // P
    TB = S // P
    HALF = NH * B
    UNITS = 2 * HALF
    GS = 4 * B
    NPAIR = E // 2
    INV_SCALE = -float(P) ** -0.5
    MASKED = -1.0e30
    BIG = 3.0e38

    def chunks_of(n):
        if n == -2:
            return [("Krope", 0), ("Qrope", 0)]
        if n == -1:
            return [("VT", 0), ("Qrope", 1), ("Vx", 0)]
        v, c1, found = n + 2, n // 4 + 1, []
        if v < HALF:
            found.append(("Qrope", v))
        elif v < UNITS:
            found += [("Q", v), ("K", v)]
        if c1 < HALF // 4:
            if n % 4 < 3:
                found.append([("Krope", c1), ("VT", c1), ("Vx", c1)][n % 4])
        elif c1 < UNITS // 4:
            found += [[("V", c1, 0), ("V", c1, 1)], [("V", c1, 2)], [("V", c1, 3)], []][n % 4]
        return found

    CHUNK = {}
    for n in range(-2, UNITS):
        for ch in chunks_of(n):
            CHUNK[ch] = len(CHUNK)

    def behind(n, steps, kind):
        at = n - steps
        return [ch for ch in chunks_of(at) if ch[0] == kind] if at >= 0 else []

    def over_from(n):
        return chunks_of(n - 1)[2:] if n > 0 else []

    def jobs_of(n):
        if n == -2:
            return [("KV", 0)] + [(f"Q{q}", 0) for q in range(4)]
        a, s, found = n // GS, n % GS, []
        if n < 0 or n >= UNITS:
            return found
        if s == 0:
            found.append(("O0", a))
        if s == 2:
            found.append(("O1", a))
        if s == 3 and a + 1 < UNITS // GS:
            found.append(("KV", a + 1))
        if 4 <= s < 8 and a + 1 < UNITS // GS:
            found.append((f"Q{s - 4}", a + 1))
        return found

    JOB = {}
    for n in range(-2, UNITS):
        for job in jobs_of(n):
            JOB[job] = len(JOB)
    LN = {}
    for b in range(B):
        for t in range(b * TB, (b + 1) * TB):
            LN["stats", t] = len(LN) + 1
        for t in range(b * TB, (b + 1) * TB):
            LN["mean_var", t] = len(LN) + 1
        LN["var", 0, b] = len(LN) + 1
    for t in range(NT):
        LN["xn", t] = len(LN) + 1
    for b in range(B):
        LN["var", 1, b] = len(LN) + 1
        for t in range(b * TB, (b + 1) * TB):
            LN["xr", t] = len(LN) + 1
    LN["var", 2] = len(LN) + 1
    for t in range(NT):
        LN["xr2", t] = len(LN) + 1

    GA = HALF // GS
    START = 3
    CHUNKS_W = [sum(len(chunks_of(n)) for n in range(w, w + GS)) for w in (START, HALF + START)]
    ROT_W = {"Qrope": GS, "Krope": GS // 4}
    JOBS_W = 7
    assert all(c % 2 == 0 for c in CHUNKS_W)

    BLOCKS = [(3, 3), (0, 0), (0, 1), (0, 2), (0, 3), (1, 1), (1, 2), (1, 3), (2, 2), (2, 3)]
    PT_CHUNKS = [(0, 4), (4, 8), (8, 10)]
    PT_COLS = len(BLOCKS) * P + P
    PT_ROW = {0: (2 * P, 0), 1: (6 * P, P), 2: (9 * P, 2 * P), 3: (0, 2 * P)}
    P_OFF = [i * (i + 1) // 2 * P for i in range(TB)]
    P_COLS = TB * (TB + 1) // 2 * P
    PASSES = [(0, 0), (0, 1), (1, 0)]

    ctx = ExitStack()
    with ctx:
        def sb(name, cols, dt=f32, rows=P):
            return ctx.enter_context(nc.sbuf_tensor(name, [rows, cols], dt))

        def sem(name):
            return ctx.enter_context(nc.semaphore(name))

        accB_t = sb("acc_b", NT * D)
        accA_t = sb("acc_a", NT * D)
        xnT_t = sb("xnT", 2 * KD * NT * P, f32r)
        xrT_t = sb("xrT", 2 * KD * NT * P, f32r)
        q_t = sb("q_heads", 2 * 2 * S, f32r)
        k_t = sb("k_heads", 2 * 2 * S, f32r)
        v_t = sb("v_heads", 2 * 2 * TB * 4 * P, f32r)
        p_t = sb("probs", 2 * P_COLS)
        pt_t = sb("probsT", 2 * PT_COLS, f32r)
        z_t = sb("zT", 4 * 2 * S, f32r)
        wqk_t = sb("w_qk", 4 * 2 * 2 * KD * P, f32r)
        wkv_t = sb("w_kv", 2 * KD * 4 * P, f32r)
        wo_t = sb("w_o", 2 * 2 * 2 * D, f32r)
        rq_t = sb("raw_qk", 4 * 2 * KD * P)
        rkv_t = sb("raw_kv", KD * 4 * P)
        ro_t = sb("raw_o", 2 * 2 * D)
        rope_t = sb("rope", 2 * S)
        t1_t = sb("rope_sum", 3 * S)
        sw_t = sb("rope_swapped", 2 * S)
        vt_t = sb("vT", S)
        mask_t = sb("mask", S)
        ident = sb("ident", P)
        rows_t = sb("const_rows", P)
        cols_t = sb("const_cols", 64)
        gate_keep = sb("gate_cols", KD * E)
        bO_t = sb("b_o", D)
        be_t = sb("bias_e", E)
        nmax_t = sb("neg_max", 2 * TB)
        sum_t = sb("row_sum", 2 * TB)
        inv_t = sb("inv_sum", 2 * TB)
        stats_t = sb("ln_stats", NT * 6)
        mv_t = sb("ln_mean_var", NT * 2)
        var_t = sb("var", 4 * NT)
        rstd_t = sb("rstd", 4 * NT)
        mhalf_t = sb("minus_half", NT)
        cw_t = sb("combine", NT * E)
        rt_t = sb("router", 3 * NT * (E + TOPK))
        small_t = sb("router_small", NT * 8 + 4 * NT)

        accB = accB_t[:, :].rearrange("p (t d) -> p t d", t=NT)
        accA = accA_t[:, :].rearrange("p (t d) -> p t d", t=NT)
        xnT = xnT_t[:, :].rearrange("p (h k t) -> p h k t", h=2, k=KD)
        xrT = xrT_t[:, :].rearrange("p (h k t) -> p h k t", h=2, k=KD)
        qT = q_t[:, :].rearrange("p (s h t) -> p s h t", s=2, h=2)
        kT = k_t[:, :].rearrange("p (s h t) -> p s h t", s=2, h=2)
        vh = v_t[:, :].rearrange("p (s h t c) -> p s h t c", s=2, h=2, t=TB)
        pr = p_t[:, :].rearrange("p (s c) -> p s c", s=2)
        pT = pt_t[:, :].rearrange("p (h c) -> p h c", h=2)
        zT = z_t[:, :].rearrange("p (s h t) -> p s h t", s=4, h=2)
        wqk = wqk_t[:, :].rearrange("p (q w h k e) -> p q w h k e", q=4, w=2, h=2, k=KD)
        wkvA = wkv_t[:, :].rearrange("p (h c) -> p h c", h=2)
        wkvB = wkv_t[:, :].rearrange("p (h k e) -> p h k e", h=2, k=KD)
        w_o = wo_t[:, :].rearrange("p (o h j d) -> p o h j d", o=2, h=2, j=2)
        rq = rq_t[:, :].rearrange("p (q w k e) -> p q w k e", q=4, w=2, k=KD)
        ro = ro_t[:, :].rearrange("p (o j d) -> p o j d", o=2, j=2)
        cosT, sinT = rope_t[:, 0:S], rope_t[:, S:2 * S]
        t1 = t1_t[:, :].rearrange("p (s t) -> p s t", s=3)
        swapped = {"Qrope": sw_t[:, 0:S], "Krope": sw_t[:, S:2 * S]}
        rot_sum = lambda ch: t1[:, ch[1] % 2 if ch[0] == "Qrope" else 2]
        nmax = nmax_t[:, :].rearrange("p (s i) -> p s i", s=2)
        rsum = sum_t[:, :].rearrange("p (s i) -> p s i", s=2)
        rinv = inv_t[:, :].rearrange("p (s i) -> p s i", s=2)
        stats = stats_t[:, :].rearrange("p (t c) -> p t c", t=NT)
        mv = mv_t[:, :].rearrange("p (t c) -> p t c", t=NT)
        var = var_t[:, :].rearrange("p (w t) -> p w t", w=4)
        rstd = rstd_t[:, :].rearrange("p (w t) -> p w t", w=4)
        gaterow_t = sw_t[:, S:S + D]
        xr = p_t[:, 0:NT * D].rearrange("p (t d) -> p t d", t=NT)
        BQ, BK, BV, L1, L2 = 0, NH, 2 * NH, 3 * NH, 3 * NH + KD
        NROW = 3 * NH + 2 * KD
        cols = cols_t
        mgu = wqk_t[:, :].rearrange("p (s h k c) -> p s h k c", s=2, h=2, k=KD)
        mwd = wkv_t[:, :].rearrange("p (s h j d) -> p s h j d", s=2, h=2, j=2)
        rgu = rq_t[:, :].rearrange("p (s k c) -> p s k c", s=2, k=KD)
        rwd = rkv_t[:, :].rearrange("p (s j d) -> p s j d", s=2, j=2)
        gateT = q_t[:, 0:2 * KD * P].rearrange("p (h k e) -> p h k e", h=2, k=KD)
        hrow = p_t[:, 0:4 * 2 * P].rearrange("p (s t c) -> p s t c", s=2, t=2)
        silu = p_t[:, 4 * 2 * P:6 * 2 * P].rearrange("p (s c) -> p s c", s=2)
        hT = z_t[:, 0:2 * 2 * 4 * P].rearrange("p (s h c) -> p s h c", s=2, h=2)
        lgT = sw_t
        xr2 = lambda t: (rope_t if t < TB else t1_t)[:, t % TB * D:(t % TB + 1) * D]
        RW = E + TOPK
        route = rt_t[:, :].rearrange("p (w t e) -> p w t e", w=3, t=NT)
        cw = cw_t[:, :].rearrange("p (t e) -> p t e", t=NT)
        top8 = small_t[:, 0:NT * 8].rearrange("p (t e) -> p t e", t=NT)
        rsm = small_t[:, NT * 8:NT * 8 + 4 * NT].rearrange("p (w t) -> p w t", w=4)

        bank = {n: ctx.enter_context(nc.psum_tensor(n, [P, 512], f32))
                for n in ("s0", "s1", "t0", "t1", "j0", "j1", "zb", "ob")}
        bS = [bank["s0"], bank["s1"]]
        bT = [bank["t0"], bank["t1"]]
        bJ = [bank["j0"], bank["j1"]]
        bY = [bank["s0"], bank["s1"], bank["t0"], bank["t1"]]
        bH = [bank["zb"], bank["ob"]]

        x_in = [sem(f"x_in_{b}") for b in range(B)]
        rows_in, rope_in, bc_in = sem("rows_in"), sem("rope_in"), sem("bc_in")
        raw_in = {w: sem(f"raw_in_{w}") for w in ("KV", "Q0", "Q1", "Q2", "Q3", "O0", "O1")}
        consts = sem("pool_consts")
        zeroed = sem("zeroed")
        ln_step = sem("ln_vector")
        ln_ssq, ln_pow = sem("ssq_done"), sem("rstd_done")
        bias_added = sem("bias_added")
        cx_mm, cx_ev = sem("const_turned"), sem("const_kept")
        x_mm, x_hi, x_lo = sem("x_turned"), sem("xT_hi"), sem("xT_lo")
        s_mm, s_free = sem("scores_done"), sem("scores_taken")
        e_done, r_done, p_norm = sem("exp_done"), sem("inverse_done"), sem("probs_normed")
        t_mm, pt_hi, pt_lo = sem("probs_turned"), sem("pT_hi"), sem("pT_lo")
        z_mm, z_hi, z_lo = sem("z_done"), sem("zT_hi"), sem("zT_lo")
        o_mm, o_add = sem("outproj_done"), sem("outproj_added")
        j_mm, j_hi, j_lo = sem("proj_done"), sem("proj_hi"), sem("proj_kept")
        sw_done, rp_sin, rp_sum, rp_hi, rp_lo = (
            {kind: sem(f"{kind}_{stage}") for kind in ("Qrope", "Krope")}
            for stage in ("swapped", "sin_done", "sum_done", "hi", "lo"))
        w_hi, w_done = sem("weights_hi"), sem("weights_split")
        lg_mm, lg_ev, lt_mm, rt = sem("logits_done"), sem("logits_kept"), sem("logits_turned"), sem("router_vector")
        rt_exp, cw_done = sem("router_exp"), sem("combine_done")
        g_hi = sem("gate_split")
        gu_mm, si_done, h_done = sem("gateup_done"), sem("silu_done"), sem("h_done")
        ht_mm, ht_hi, ht_lo = sem("h_turned"), sem("hT_hi"), sem("hT_lo")
        dn_mm = sem("down_done")
        mraw_gu = [sem("raw_gu0"), sem("raw_gu1")]
        mraw_d = [sem("raw_d0"), sem("raw_d1")]
        mw_hi, mw_done = sem("expert_weights_hi"), sem("expert_weights_split")
        waits_passed = sem("waits_passed")
        res_done, y_done, out_sem = sem("residual_sum"), sem("y_added"), sem("out_written")

        def until(eng, s, count, it=None, per=0):
            eng.wait_ge(s, count if it is None or per == 0 else it * per + count)

        def until_apart(eng, s, count, it=None, per=0):
            until(eng, s, count, it, per)
            stand_apart(eng, it)

        def stand_apart(eng, it):
            if it is not None:
                eng.sem_inc(waits_passed, 1)

        def windows(eng, step):
            for n in range(-2, START):
                step(n, None)
            for phase in range(2):
                first = phase * HALF + START
                with eng.Fori(0, GA - 1) as it:
                    for n in range(first, first + GS):
                        step(n, it)
                for n in range(first + (GA - 1) * GS, min(first + GA * GS, UNITS)):
                    step(n, None)

        block = ctx.enter_context(nc.Block())

        @block.sync
        def _(sp):
            xv = x.rearrange("b (t p) d -> p (b t) d", p=P)
            for b in range(B):
                sp.dma_start(accB[:, b * TB:(b + 1) * TB, :], xv[:, b * TB:(b + 1) * TB, :]).then_inc(x_in[b], 16)
            for at, src in ((BQ, b_Q), (BK, b_K), (BV, b_V)):
                sp.dma_start(rows_t[at:at + NH, :], src).then_inc(rows_in, 16)
            for at, src in ((L1, ln1_w), (L2, ln2_w)):
                sp.dma_start(rows_t[at:at + KD, :], src.rearrange("(k p) -> k p", p=P)).then_inc(rows_in, 16)
            sp.dma_start(gaterow_t[0:E, :], gate_w).then_inc(rows_in, 16)

            wqv = wq.rearrange("(k p) c -> p k c", p=P)
            wkv_ = wk.rearrange("(k p) c -> p k c", p=P)
            wvv = wv.rearrange("(k p) c -> p k c", p=P)
            wov = wo.rearrange("(h e) d -> e h d", e=P)

            def load(which, g, phase):
                if phase == 0:
                    if which == "KV":
                        for i, src in enumerate((wkv_, wvv)):
                            dst = rkv_t[:, i * KD * P:(i + 1) * KD * P].rearrange("p (k e) -> p k e", k=KD)
                            sp.dma_start(dst, src[:, :, bass.ds(g * P, P)]).then_inc(raw_in["KV"], 16)
                    elif which[0] == "Q":
                        q = int(which[1])
                        sp.dma_start(rq[:, q, 0], wqv[:, :, bass.ds(g * (4 * P) + q * P, P)]).then_inc(raw_in[which], 16)
                    else:
                        o = int(which[1])
                        sp.dma_start(ro[:, o], wov[:, bass.ds(g * 4 + 2 * o, 2), :]).then_inc(raw_in[which], 16)
                else:
                    if which == "KV":
                        for k in range(KD):
                            dst = rkv_t[:, k * 4 * P:(k + 1) * 4 * P].rearrange("p (h e) -> p h e", h=4)
                            sp.dma_start(dst, W_V[bass.ds(g * 4, 4), k * P:(k + 1) * P, :].rearrange("h p e -> p h e")
                                         ).then_inc(raw_in["KV"], 16)
                    elif which[0] == "Q":
                        q = int(which[1])
                        for i, src in enumerate((W_Q, W_K)):
                            sp.dma_start(rq[:, q, i], src[bass.ds(g * 4 + q, 1), :, :].rearrange("h (k p) e -> p (h k) e", p=P)
                                         ).then_inc(raw_in[which], 16)
                    else:
                        o = int(which[1])
                        sp.dma_start(ro[:, o], W_O[bass.ds(g * 4 + 2 * o, 2), :, :].rearrange("h e d -> e h d")
                                     ).then_inc(raw_in[which], 16)

            kinds = ("KV", "Q0", "Q1", "Q2", "Q3", "O0", "O1")
            for which in kinds:
                load(which, 0, 0)

            def loads(a, phase, g):
                for which in kinds:
                    done = {"KV": -6, "Q0": -5, "Q1": -4, "Q2": -3, "Q3": -2, "O0": -1, "O1": 0}[which]
                    sp.wait_ge(w_done, a * JOBS_W + done)
                    load(which, g, phase)

            with sp.Fori(1, GA) as a:
                loads(a, 0, a)
            with sp.Fori(GA, 2 * GA) as a:
                loads(a, 1, a - GA)

            sp.wait_ge(w_done, len(JOB))
            wsgv, wsuv = (w.rearrange("(k p) i -> p k i", p=P) for w in (wsg, wsu))

            def load_shared():
                for i, src in enumerate((wsgv, wsuv)):
                    sp.dma_start(rgu[:, 0, :, i * P:(i + 1) * P], src).then_inc(mraw_gu[0], 16)
                sp.dma_start(rwd[:, 0, 0], wsd).then_inc(mraw_d[0], 16)

            def load_pair(slot, m):
                for i, src in enumerate((weg, weu)):
                    for j in range(2):
                        at = (2 * i + j) * P
                        sp.dma_start(rgu[:, slot, :, at:at + P],
                                     src[bass.ds(m * 2 + j, 1), :, :].rearrange("e (k p) i -> p (e k) i", p=P)
                                     ).then_inc(mraw_gu[slot], 16)
                sp.dma_start(rwd[:, slot], wed[bass.ds(m * 2, 2), :, :].rearrange("e i d -> i e d")
                             ).then_inc(mraw_d[slot], 16)

            load_shared()
            load_pair(1, 0)
            with sp.Fori(1, NPAIR // 2) as r:
                for j in range(2):
                    sp.wait_ge(mw_done, r * 4 + 2 * j - 2)
                    load_pair(j, r * 2 + (j - 1))
            sp.wait_ge(mw_done, 2 * (NPAIR - 2) + 2)
            load_pair(0, NPAIR - 1)

            ov = out.rearrange("b (t p) d -> p (b t) d", p=P)
            for tp in range(NT // 2):
                sp.wait_ge(y_done, tp + 1)
                sp.dma_start(ov[:, 2 * tp:2 * tp + 2, :], accB[:, 2 * tp:2 * tp + 2, :]).then_inc(out_sem, 16)
            sp.wait_ge(out_sem, 16 * (NT // 2))

        @block.gpsimd
        def _(pool):
            pool.memset(ident[:, :], 0.0).then_inc(consts, 1)
            pool.memset(mask_t[:, :], 0.0).then_inc(consts, 1)
            pool.memset(mhalf_t[:, :], -0.5).then_inc(consts, 1)
            pool.wait_ge(consts, 2)
            pool.affine_select(out=ident[:, :], in_=ident[:, :], compare_op=ALU.not_equal, fill=1.0,
                               base=0, pattern=[[-1, P]], channel_multiplier=1).then_inc(consts, 1)
            diag = mask_t[:, S - P:S]
            pool.affine_select(out=diag, in_=diag, compare_op=ALU.is_ge, fill=MASKED,
                               base=0, pattern=[[-1, P]], channel_multiplier=1).then_inc(consts, 1)

            def power(w, b):
                ts = slice(0, NT) if b is None else slice(b * TB, (b + 1) * TB)
                pool.wait_ge(ln_step, LN["var", w] if b is None else LN["var", w, b])
                pool.tensor_tensor(rstd[:, w, ts], var[:, w, ts], mhalf_t[:, ts], ALU.pow).then_inc(ln_pow, 1)

            pool.wait_ge(consts, 3)
            for b in range(B):
                power(0, b)

            def weights(job, it):
                which, a = job
                phase, at = (0 if a < GA else 1), JOB[job]
                if which[0] == "Q":
                    count, per = (16 * (a + 1), 16) if phase == 0 else (16 * GA + 32 * (a - GA + 1), 32)
                elif which == "KV":
                    count, per = 32 * (a + 1), 32
                else:
                    count, per = 16 * (a + 1), 16
                until(pool, raw_in[which], count, it, per)
                if which[0] == "Q" and a:
                    v = GS * (a - 1) + 4 + int(which[1])
                    last = ("Qrope", v) if v < HALF else ("K", v)
                    until(pool, j_mm, CHUNK[last] + 1, it, CHUNKS_W[0 if v < HALF else 1])
                if which == "KV" and a:
                    c = 2 * (a - 1) + 1
                    last = ("VT", c) if c < HALF // 4 else ("V", c, 3)
                    until(pool, j_mm, CHUNK[last] + 1, it, CHUNKS_W[0 if c < HALF // 4 else 1])
                if which == "O0" and a:
                    until(pool, o_mm, GS * a - 2, it, GS)
                if which == "O1" and a:
                    until(pool, o_mm, GS * a, it, GS)
                if which[0] == "Q" and phase == 0:
                    q = int(which[1])
                    view = lambda ap: ap.rearrange("p k (w i) -> p k w i", w=2)
                    parts = [(view(wqk[:, q, 0, 0]), view(wqk[:, q, 0, 1]),
                              rq[:, q, 0].rearrange("p k (i w) -> p k w i", w=2))]
                elif which[0] == "Q":
                    q = int(which[1])
                    parts = [(wqk[:, q, :, 0], wqk[:, q, :, 1], rq[:, q])]
                elif which == "KV" and phase == 0:
                    half = KD * P
                    kk = lambda ap: ap[:, 0:half].rearrange("p (k w i) -> p k w i", k=KD, w=2)
                    parts = [(kk(wkvA[:, 0]), kk(wkvA[:, 1]),
                              rkv_t[:, 0:half].rearrange("p (k i w) -> p k w i", k=KD, w=2)),
                             (wkvA[:, 0, half:2 * half], wkvA[:, 1, half:2 * half], rkv_t[:, half:2 * half])]
                elif which == "KV":
                    parts = [(wkvA[:, 0], wkvA[:, 1], rkv_t[:, :])]
                else:
                    o = int(which[1])
                    parts = [(w_o[:, o, 0], w_o[:, o, 1], ro[:, o])]
                stand_apart(pool, it)
                for hi, _, raw in parts:
                    last = pool.tensor_scalar(hi, raw, 1.0, 1.0, ALU.mult, ALU.mult)
                last.then_inc(w_hi, 1)
                until(pool, w_hi, at + 1, it, JOBS_W)
                for hi, lo, raw in parts:
                    last = pool.tensor_tensor(lo, raw, hi.bitcast(f32), ALU.subtract)
                last.then_inc(w_done, 1)

            def normalise(n, it):
                if -1 <= n < UNITS - 1:
                    u = n + 1
                    for i in range(TB):
                        until_apart(pool, r_done, TB * u + i + 1, it, TB * GS)
                        piece = pr[:, u % 2, P_OFF[i]:P_OFF[i] + (i + 1) * P]
                        pool.tensor_scalar(piece, piece, rinv[:, u % 2, i:i + 1], 1.0,
                                           ALU.mult, ALU.mult).then_inc(p_norm, 1)

            def rope_los(n, it):
                if n < 0:
                    found = [ch for ch in chunks_of(n) if ch[0] in ROT_W]
                else:
                    found = [ch for ch in chunks_of(n) if ch[0] == "Qrope"] + behind(n, 2, "Krope")
                for kind, v in found:
                    until(pool, rp_hi[kind], v + 1, it, ROT_W[kind])
                    dst = (qT if kind == "Qrope" else kT)[:, v % 2]
                    pool.tensor_tensor(dst[:, 1], rot_sum((kind, v)), dst[:, 0].bitcast(f32),
                                       ALU.subtract).then_inc(rp_lo[kind], 1)

            def step(n, it):
                if n >= 0:
                    normalise(n, it)
                    rope_los(n, it)
                if n == UNITS - 3:
                    power(2, None)
                for job in jobs_of(n)[1 if n == -2 else 0:]:
                    if n == -2 and job[0] == "Q2":
                        rope_los(n, it)
                    weights(job, it)
                if n == -1:
                    normalise(n, it)
                    rope_los(n, it)
                if n in (1, 2):
                    pool.wait_ge(bc_in, 32)
                    half = NT // 2
                    tiles = accB[:, (n - 1) * half:n * half, :]
                    pool.tensor_tensor(tiles, tiles, bO_t[:, :].unsqueeze(1).to_broadcast([P, half, D]),
                                       ALU.add).then_inc(bias_added, 1)

            weights(("KV", 0), None)
            for b in range(B):
                power(1, b)
            windows(pool, step)

            pool.wait_ge(j_mm, len(CHUNK))

            def expert_split(kind, M, it, raw_count, raw_per):
                slot = M % 2
                at = 2 * M + (kind == "d")
                if kind == "gu":
                    width = 2 * P if M == 0 else 4 * P
                    until(pool, mraw_gu[slot], raw_count, it, raw_per)
                    if M >= 2:
                        until(pool, gu_mm, 8 * M - 8, it, 16)
                    hi, lo, raw = mgu[:, slot, 0, :, 0:width], mgu[:, slot, 1, :, 0:width], rgu[:, slot, :, 0:width]
                else:
                    ne = 1 if M == 0 else 2
                    until(pool, mraw_d[slot], raw_count, it, raw_per)
                    if M >= 2:
                        until(pool, dn_mm, 4 * M - 4, it, 8)
                    hi, lo, raw = mwd[:, slot, 0, 0:ne], mwd[:, slot, 1, 0:ne], rwd[:, slot, 0:ne]
                stand_apart(pool, it)
                pool.tensor_scalar(hi, raw, 1.0, 1.0, ALU.mult, ALU.mult).then_inc(mw_hi, 1)
                until(pool, mw_hi, at + 1, it, 4)
                pool.tensor_tensor(lo, raw, hi.bitcast(f32), ALU.subtract).then_inc(mw_done, 1)

            def gu_raw(M):
                return 32 + 64 * (M // 2) if M % 2 == 0 else 64 * (M // 2 + 1)

            def d_raw(M):
                return 16 * (M // 2 + 1)

            expert_split("gu", 0, None, gu_raw(0), 0)
            expert_split("d", 0, None, d_raw(0), 0)
            expert_split("gu", 1, None, gu_raw(1), 0)
            expert_split("d", 1, None, d_raw(1), 0)
            expert_split("gu", 2, None, gu_raw(2), 0)
            with pool.Fori(0, NPAIR // 2 - 1) as it:
                expert_split("d", 2, it, d_raw(2), 16)
                expert_split("gu", 3, it, gu_raw(3), 64)
                expert_split("d", 3, it, d_raw(3), 16)
                expert_split("gu", 4, it, gu_raw(4), 64)
            expert_split("d", NPAIR, None, d_raw(NPAIR), 0)
            pool.wait_ge(o_add, UNITS + 1)
            pool.tensor_tensor(accB_t[:, :], accB_t[:, :], accA_t[:, :], ALU.add).then_inc(res_done, 1)

        @block.tensor
        def _(pe):
            pe.wait_ge(consts, 4)
            pe.wait_ge(rows_in, 16 * 6)
            pe.transpose(bank["zb"][:, 0:NROW], rows_t[0:NROW, :], ident[0:NROW, 0:NROW])
            for k in range(KD):
                last = pe.transpose(bank["zb"][:, 64 + k * E:64 + (k + 1) * E],
                                    gaterow_t[0:E, k * P:(k + 1) * P], ident[0:E, 0:E])
            last.then_inc(cx_mm, 1)

            def turn_x(dst, src, what, b, k):
                for t in range(TB):
                    pe.wait_ge(ln_step, LN[what, b * TB + t])
                    m = pe.transpose(dst[:, t * P:(t + 1) * P], src(b * TB + t)[:, k * P:(k + 1) * P],
                                     ident[:, :])
                m.then_inc(x_mm, 1)

            def turn_xr(b):
                for k in range(KD):
                    turn_x((bS if b == 0 else bT)[k], lambda t: xr[:, t, :], "xr", b, k)

            def turn_xn(b):
                for k in range(KD):
                    if b:
                        pe.wait_ge(x_lo, B * KD + k + 1)
                    turn_x((bank["zb"], bank["ob"])[k], lambda t: accA[:, t, :], "xn", b, k)

            turn_xr(0)

            def mm3(dst, lhs, rhs, first, last_, skip=False):
                for i, (a, b) in enumerate(PASSES):
                    m = pe.matmul(dst, lhs(a), rhs(b), start=first and i == 0,
                                  stop=last_ and i == 2, skip_group_check=skip)
                return m

            def project(ch, it):
                at = CHUNK[ch]
                dst = bJ[at % 2]
                until(pe, j_lo, at + 1, it, per_of(ch))
                kind, v = ch[0], ch[1]
                if kind in ("Qrope", "Q", "K"):
                    a, b, q = v // GS, v % GS // 4, v % 4
                    src = xrT if kind == "Qrope" else xnT
                    until(pe, w_done, JOB[(f"Q{q}", a)] + 1, it, JOBS_W)
                    w = wqk[:, q, 1 if kind == "K" else 0]
                    for k in range(KD):
                        m = mm3(dst[:, :], lambda p: w[:, p, k, :],
                                lambda p: src[:, p, k, b * S:(b + 1) * S], k == 0, k == KD - 1)
                elif kind in ("Krope", "VT"):
                    a, b = v // 2, v % 2
                    until(pe, w_done, JOB[("KV", a)] + 1, it, JOBS_W)
                    half = KD * P
                    off = 0 if kind == "Krope" else half
                    for k in range(KD):
                        m = mm3(dst[:, :], lambda p: wkvA[:, p, off + k * P:off + (k + 1) * P],
                                lambda p: xrT[:, p, k, b * S:(b + 1) * S], k == 0, k == KD - 1)
                elif kind == "Vx":
                    until(pe, j_lo, CHUNK[("VT", v)] + 3, it, per_of(ch))
                    for t in range(TB):
                        m = pe.transpose(dst[:, t * P:(t + 1) * P], vt_t[:, t * P:(t + 1) * P], ident[:, :])
                else:
                    a, b, t = v // 2, v % 2, ch[2]
                    until(pe, w_done, JOB[("KV", a)] + 1, it, JOBS_W)
                    tok = (b * TB + t) * P
                    for k in range(KD):
                        m = mm3(dst[:, :], lambda p: xnT[:, p, k, tok:tok + P],
                                lambda p: wkvB[:, p, k, :], k == 0, k == KD - 1)
                m.then_inc(j_mm, 1)

            def per_of(ch):
                lim = HALF if ch[0] in ("Qrope", "Q", "K") else HALF // 4
                return CHUNKS_W[0 if ch[1] < lim else 1]

            def scores(u, i, it):
                until(pe, s_free, TB * u + i + 1, it, TB * GS)
                if i == 0:
                    if u < HALF:
                        until(pe, rp_lo["Qrope"], u + 1, it, ROT_W["Qrope"])
                        if u % 4 == 0:
                            until(pe, rp_lo["Krope"], u // 4 + 1, it, ROT_W["Krope"])
                    else:
                        until(pe, j_lo, CHUNK[("K", u)] + 3, it, CHUNKS_W[1])
                ks = u // 4 % 2 if u < HALF else u % 2
                width = max(2 * P, (i + 1) * P)
                mm3(bS[i % 2][:, 0:width], lambda p: qT[:, u % 2, p, i * P:(i + 1) * P],
                    lambda p: kT[:, ks, p, 0:width], True, True).then_inc(s_mm, 1)

            def turn_probs(u, c, it):
                at = 3 * u + c
                if c == 0:
                    until(pe, p_norm, TB * (u + 1), it, TB * GS)
                until(pe, pt_lo, at + 1, it, 3 * GS)
                lo_, hi_ = PT_CHUNKS[c]
                for j in range(lo_, hi_):
                    kt, qt = BLOCKS[j]
                    m = pe.transpose(bT[at % 2][:, (j - lo_) * P:(j - lo_ + 1) * P],
                                     pr[:, u % 2, P_OFF[qt] + kt * P:P_OFF[qt] + (kt + 1) * P], ident[:, :])
                m.then_inc(t_mm, 1)

            def attend(u, it):
                until(pe, pt_lo, 3 * u + 5, it, 3 * GS)
                until(pe, z_lo, u + 1, it, GS)
                if u % 4 == 0:
                    vc = ("Vx", u // 4) if u < HALF else ("V", u // 4, TB - 1)
                    until(pe, j_lo, CHUNK[vc] + 3, it, CHUNKS_W[0 if u < HALF else 1])
                col = 0 if u < HALF else u % 4 * P
                dst = bank["zb"]
                for kt in range(TB):
                    at, q0 = PT_ROW[kt]
                    m = mm3(dst[:, q0:S], lambda p: vh[:, u // 4 % 2, p, kt, col:col + P],
                            lambda p: pT[:, p, at:at + S - q0], kt == 0, kt == TB - 1, skip=True)
                m.then_inc(z_mm, 1)

            def out_project(n, t, it):
                o = n - 2
                m_, half = o // 2, o % 2
                a, b, hp = o // GS, o % GS // 4, m_ % 2
                if half == 0 and t == 0:
                    until(pe, z_lo, 2 * m_ + 3, it, GS)
                    until(pe, w_done, JOB[(f"O{hp}", a)] + 1, it, JOBS_W)
                if t == 0:
                    until(pe, o_add, o + 1, it, GS)
                tok = (2 * half + t) * P
                for j in range(2):
                    m = mm3(bank["ob"][:, t * D:(t + 1) * D],
                            lambda p: zT[:, (2 * m_ + j) % 4, p, tok:tok + P],
                            lambda p: w_o[:, hp, p, j, :], t == 0 and j == 0, t == 1 and j == 1, skip=True)
                if t == 1:
                    m.then_inc(o_mm, 1)

            def step(n, it):
                chs = chunks_of(n) if n < UNITS else []
                if n < 0:
                    if n == -2:
                        pe.wait_ge(x_lo, KD)
                    for ch in chs:
                        project(ch, it)
                    if n == -1:
                        turn_xr(1)
                        pe.wait_ge(x_lo, KD)
                        for i in range(TB):
                            scores(0, i, it)
                        pe.wait_ge(cx_ev, 1)
                        turn_xn(0)
                        pe.wait_ge(x_lo, 2 * KD)
                        for c in range(2):
                            turn_probs(0, c, it)
                        turn_xn(1)
                    return
                nxt = n + 1 < UNITS
                rotary = n + 2 < HALF
                if rotary:
                    for ch in over_from(n) + chs[:1]:
                        project(ch, it)
                if nxt:
                    scores(n + 1, 0, it)
                    scores(n + 1, 1, it)
                for ch in [] if rotary else over_from(n):
                    project(ch, it)
                if not rotary and 2 <= n < UNITS + 2:
                    out_project(n, 0, it)
                if n < UNITS:
                    turn_probs(n, 2, it)
                if nxt:
                    scores(n + 1, 2, it)
                    scores(n + 1, 3, it)
                if rotary and 2 <= n:
                    out_project(n, 0, it)
                if 2 <= n < UNITS + 2:
                    out_project(n, 1, it)
                for ch in [] if rotary else chs[:2]:
                    project(ch, it)
                if n == UNITS - 1:
                    turn_x2(2)
                if n == 0:
                    pe.wait_ge(x_lo, 2 * B * KD)
                attend(n, it)
                for ch in chs[1:2] if rotary else []:
                    project(ch, it)
                if nxt:
                    turn_probs(n + 1, 0, it)
                    turn_probs(n + 1, 1, it)
                if n == UNITS - 2:
                    turn_x2(0)
                    turn_x2(1)

            def turn_x2(i):
                b, k = i // KD, i % KD
                if i < 2:
                    pe.wait_ge(j_lo, len(CHUNK) + 2 - 1 + i)
                else:
                    pe.wait_ge(x_lo, 2 * B * KD + i - 1)
                turn_x(bJ[i % 2], xr2, "xr2", b, k)

            windows(pe, step)

            turn_x2(3)
            pe.wait_ge(g_hi, 2)
            for b in range(B):
                pe.wait_ge(x_lo, 2 * B * KD + (b + 1) * KD)
                for k in range(KD):
                    m = mm3(bS[b][:, :], lambda p: gateT[:, p, k, :],
                            lambda p: xrT[:, p, k, b * S:(b + 1) * S], k == 0, k == KD - 1)
                m.then_inc(lg_mm, 1)
            out_project(UNITS, 0, None)
            out_project(UNITS, 1, None)
            pe.wait_ge(lg_ev, 2)
            for t in range(NT):
                m = pe.transpose(bT[0][:, t * E:(t + 1) * E], lgT[0:E, t * P:(t + 1) * P], ident[0:E, 0:E])
            m.then_inc(lt_mm, 1)

            NW = 4 * (NPAIR + 1)

            def gate_up(w, tt, it):
                M, tp, g = w // 4, w % 4, 2 * w + tt
                if g >= 2:
                    until(pe, h_done, g - 1, it, 16)
                if tt == 0:
                    until(pe, mw_done, 2 * M + 1, it, 4)
                width = 2 * P if M == 0 else 4 * P
                tok = (2 * tp + tt) * P
                for k in range(KD):
                    m = mm3(bJ[g % 2][:, 0:width], lambda p: xrT[:, p, k, tok:tok + P],
                            lambda p: mgu[:, M % 2, p, k, 0:width], k == 0, k == KD - 1)
                m.then_inc(gu_mm, 1)

            def turn_h(w, it):
                ne = 1 if w < 4 else 2
                until(pe, h_done, 2 * w + 2, it, 16)
                if w >= 2:
                    until(pe, ht_lo, w - 1, it, 8)
                for tt in range(2):
                    for j in range(ne):
                        c = tt * ne + j
                        m = pe.transpose(bH[w % 2][:, c * P:(c + 1) * P],
                                         hrow[:, w % 2, tt, j * P:(j + 1) * P], ident[:, :])
                m.then_inc(ht_mm, 1)

            def down(w, it):
                M, tp, ne = w // 4, w % 4, 1 if w < 4 else 2
                until(pe, ht_lo, w + 1, it, 8)
                if tp == 0:
                    until(pe, mw_done, 2 * M + 2, it, 4)
                for tt in range(2):
                    for j in range(ne):
                        c = tt * ne + j
                        m = mm3(bY[tp][:, tt * D:(tt + 1) * D],
                                lambda p: hT[:, w % 2, p, c * P:(c + 1) * P],
                                lambda p: mwd[:, M % 2, p, j, :],
                                w < 4 and tt == 0 and j == 0, w >= NW - 4, skip=True)
                m.then_inc(dn_mm, 1)

            def expert_step(w, it):
                if w + 1 < NW:
                    gate_up(w + 1, 0, it)
                turn_h(w, it)
                if w + 1 < NW:
                    gate_up(w + 1, 1, it)
                if w >= 1:
                    down(w - 1, it)

            out_project(UNITS + 1, 0, None)
            out_project(UNITS + 1, 1, None)
            gate_up(0, 0, None)
            gate_up(0, 1, None)
            pe.wait_ge(o_add, UNITS + 1)
            pe.wait_ge(rt, 2)
            for w in range(5):
                expert_step(w, None)
            with pe.Fori(0, NPAIR // 2 - 1) as it:
                for w in range(5, 13):
                    expert_step(w, it)
            for w in range(5 + 8 * (NPAIR // 2 - 1), NW):
                expert_step(w, None)
            down(NW - 1, None)

        @block.scalar
        def _(act):
            act.dma_start(rope_t[:, :], rope_table).then_inc(rope_in, 16)
            act.dma_start(bO_t[:, :], b_O.rearrange("(a d) -> a d", a=1).broadcast_to([P, D])).then_inc(bc_in, 16)
            act.dma_start(be_t[:, :], bias_e.rearrange("(a d) -> a d", a=1).broadcast_to([P, E])).then_inc(bc_in, 16)

            def squares(src, scratch, w, tiles):
                for t in tiles:
                    if w == 1:
                        act.wait_ge(ln_step, LN["xn", t])
                    if t or w == 2:
                        act.wait_ge(ln_ssq, (w - 1) * NT + t)
                    act.activation(scratch, src[:, t, :], ACT.Square,
                                   accum_out=var[:, 3, t:t + 1]).then_inc(ln_ssq, 1)

            squares(accA, t1_t[:, 0:D], 1, range(NT))

            def turned(dst, b, at, banks, scale_at):
                for k in range(KD):
                    act.wait_ge(x_mm, at + k + 1)
                    hi = dst[:, 0, k, b * S:(b + 1) * S]
                    if scale_at is None:
                        act.activation(hi, banks[k][:, :], ACT.Copy).then_inc(x_hi, 1)
                    else:
                        act.activation(hi, banks[k][:, :], ACT.Identity,
                                       scale=cols[:, scale_at + k:scale_at + k + 1]).then_inc(x_hi, 1)

            def turned2(i):
                b, k = i // KD, i % KD
                act.wait_ge(x_mm, 2 * B * KD + i + 1)
                act.activation(xrT[:, 0, k, b * S:(b + 1) * S], bJ[i % 2][:, :], ACT.Identity,
                               scale=cols[:, L2 + k:L2 + k + 1]).then_inc(x_hi, 1)

            act.wait_ge(cx_ev, 1)
            turned(xrT, 0, 0, bS, L1)

            def exp(u, i, it):
                until(act, s_free, TB * u + i + 3, it, TB * GS)
                piece = pr[:, u % 2, P_OFF[i]:P_OFF[i] + (i + 1) * P]
                act.activation(piece, piece, ACT.Exp, bias=nmax[:, u % 2, i:i + 1], scale=-1.0,
                               accum_out=rsum[:, u % 2, i:i + 1]).then_inc(e_done, 1)

            def probs_hi(u, c, it):
                until(act, t_mm, 3 * u + c + 1, it, 3 * GS)
                a, b = PT_CHUNKS[c]
                act.activation(pT[:, 0, (a + 1) * P:(b + 1) * P], bT[(3 * u + c) % 2][:, 0:(b - a) * P],
                               ACT.Copy).then_inc(pt_hi, 1)

            def z_part(u, it):
                until(act, z_mm, u + 1, it, GS)
                dst = zT[:, u % 4, 0, :]
                if u < HALF:
                    act.activation(dst, bank["zb"][:, :], ACT.Copy).then_inc(z_hi, 1)
                else:
                    stand_apart(act, it)
                    act.activation(dst, bank["zb"][:, :], ACT.Identity, bias=col_of(BV, u, it)).then_inc(z_hi, 1)

            def col_of(base, u, it):
                h = 4 * ((u - HALF) // GS) + u % 4 + base
                return cols[:, h:h + 1] if it is None else cols[:, bass.ds(it * 4 + h, 1)]

            def chunk_a(ch, it):
                at, kind, v = CHUNK[ch], ch[0], ch[1]
                src = bJ[at % 2]
                per = CHUNKS_W[0 if kind in ("Qrope", "Krope", "VT", "Vx") else 1]
                until(act, j_mm, at + 1, it, per)
                if kind in ROT_W:
                    if v:
                        until(act, rp_sum[kind], v, it, ROT_W[kind])
                    act.activation(swapped[kind][0:P // 2, :], src[P // 2:P, :], ACT.Copy)
                    act.activation(swapped[kind][P // 2:P, :], src[0:P // 2, :],
                                   ACT.Copy).then_inc(sw_done[kind], 1)
                elif kind == "VT":
                    until(act, j_lo, at + 2, it, per)
                    act.activation(vt_t[:, :], src[:, :], ACT.Copy).then_inc(j_lo, 1)
                elif kind in ("Q", "K"):
                    dst = (qT if kind == "Q" else kT)[:, v % 2, 0]
                    stand_apart(act, it)
                    act.activation(dst, src[:, :], ACT.Identity,
                                   bias=col_of(BQ if kind == "Q" else BK, v, it)).then_inc(j_hi, 1)
                elif kind == "Vx":
                    act.activation(vh[:, v % 2, 0, :, 0:P], src[:, :].rearrange("p (t e) -> p t e", t=TB),
                                   ACT.Copy).then_inc(j_hi, 1)
                else:
                    act.activation(vh[:, v % 2, 0, ch[2], :], src[:, :], ACT.Copy).then_inc(j_hi, 1)

            def chunk_b(ch, it):
                kind, v = ch[0], ch[1]
                if kind in ROT_W:
                    until(act, rp_sum[kind], v + 1, it, ROT_W[kind])
                    dst = (qT if kind == "Qrope" else kT)[:, v % 2, 0]
                    act.activation(dst, rot_sum(ch), ACT.Copy).then_inc(rp_hi[kind], 1)

            def step(n, it):
                chs = chunks_of(n) if n < UNITS else []
                if n == -2:
                    for ch in chs:
                        chunk_a(ch, it)
                    chunk_b(chs[0], it)
                    return
                if n == -1:
                    vt, q1, vx = chs
                    chunk_a(vt, it)
                    chunk_b(("Qrope", 0), it)
                    chunk_a(q1, it)
                    chunk_a(vx, it)
                    turned(xrT, 1, KD, bT, L1)
                    for i in range(TB):
                        exp(0, i, it)
                    chunk_b(q1, it)
                    turned(xnT, 0, B * KD, (bank["zb"], bank["ob"]), None)
                    probs_hi(0, 0, it)
                    probs_hi(0, 1, it)
                    turned(xnT, 1, B * KD + KD, (bank["zb"], bank["ob"]), None)
                    return
                nxt = n + 1 < UNITS
                rotary = n + 2 < HALF
                if rotary:
                    for ch in over_from(n) + chs[:1]:
                        chunk_a(ch, it)
                if nxt:
                    exp(n + 1, 0, it)
                    exp(n + 1, 1, it)
                for ch in [] if rotary else over_from(n):
                    chunk_a(ch, it)
                probs_hi(n, 2, it)
                for ch in behind(n, 1, "Krope"):
                    chunk_a(ch, it)
                if nxt:
                    exp(n + 1, 2, it)
                    exp(n + 1, 3, it)
                if rotary:
                    chunk_b(chs[0], it)
                for ch in behind(n, 2, "Krope"):
                    chunk_b(ch, it)
                for ch in [] if rotary else chs[:2]:
                    chunk_a(ch, it)
                if n == UNITS - 1:
                    turned2(2)
                z_part(n, it)
                if nxt:
                    probs_hi(n + 1, 0, it)
                    probs_hi(n + 1, 1, it)
                for ch in chs[1:2] if rotary else []:
                    if ch[0] != "Krope":
                        chunk_a(ch, it)
                if n == UNITS - 5:
                    act.wait_ge(o_add, HALF + 1)
                    squares(accA, vt_t[:, 0:D], 2, range(TB))
                if n == UNITS - 4:
                    squares(accA, vt_t[:, 0:D], 2, range(TB, NT))
                if n == UNITS - 2:
                    turned2(0)
                    turned2(1)

            windows(act, step)

            turned2(3)
            act.wait_ge(rt, 2)
            act.activation(route[:, 0, :, 0:E], route[:, 0, :, 0:E], ACT.Exp).then_inc(rt_exp, 1)

            NW = 4 * (NPAIR + 1)

            def silu_of(w, tt, it):
                g, width = 2 * w + tt, P if w < 4 else 2 * P
                until(act, gu_mm, g + 1, it, 16)
                if g >= 2:
                    until(act, h_done, g - 1, it, 16)
                act.activation(silu[:, g % 2, 0:width], bJ[g % 2][:, 0:width], ACT.Silu).then_inc(si_done, 1)

            def h_hi(w, it):
                width = 2 * P if w < 4 else 4 * P
                until(act, ht_mm, w + 1, it, 8)
                act.activation(hT[:, w % 2, 0, 0:width], bH[w % 2][:, 0:width], ACT.Copy).then_inc(ht_hi, 1)

            def expert_step(w, it):
                if w + 1 < NW:
                    silu_of(w + 1, 0, it)
                h_hi(w, it)
                if w + 1 < NW:
                    silu_of(w + 1, 1, it)

            silu_of(0, 0, None)
            silu_of(0, 1, None)
            for w in range(5):
                expert_step(w, None)
            with act.Fori(0, NPAIR // 2 - 1) as it:
                for w in range(5, 13):
                    expert_step(w, it)
            for w in range(5 + 8 * (NPAIR // 2 - 1), NW):
                expert_step(w, None)

        @block.vector
        def _(ve):
            ve.memset(pT[:, 0, 0:P].bitcast(f32), 0.0).then_inc(zeroed, 1)
            ve.memset(pT[:, 1, 0:P].bitcast(f32), 0.0).then_inc(zeroed, 1)
            ve.sem_inc(s_free, 2)
            ve.sem_inc(pt_lo, 2)
            ve.sem_inc(j_lo, 2)
            ve.sem_inc(z_lo, 1)
            ve.sem_inc(o_add, 1)

            done = [0]

            def did(ins, *what):
                done[0] += 1
                assert LN[what] == done[0]
                ins.then_inc(ln_step, 1)

            def tiles_of(b):
                return range(b * TB, (b + 1) * TB)

            for b in range(B):
                ve.wait_ge(x_in[b], 16)
                for t in tiles_of(b):
                    did(ve.bn_stats(stats[:, t, :], accB[:, t, :]), "stats", t)
                for t in tiles_of(b):
                    ve.wait_ge(ln_step, LN["stats", t])
                    did(ve.bn_aggr(mv[:, t, :], stats[:, t, :]), "mean_var", t)
                ve.wait_ge(ln_step, LN["mean_var", (b + 1) * TB - 1])
                ts = slice(b * TB, (b + 1) * TB)
                did(ve.tensor_scalar(var[:, 0, ts], mv[:, ts, 1], 1e-05, None, ALU.add), "var", 0, b)
            for b in range(B):
                ve.wait_ge(ln_pow, b + 1)
                for t in tiles_of(b):
                    did(ve.tensor_scalar(accA[:, t, :], accB[:, t, :], mv[:, t, 0:1], rstd[:, 0, t:t + 1],
                                         ALU.subtract, ALU.mult), "xn", t)

            def first_rms(b):
                ts = slice(b * TB, (b + 1) * TB)
                ve.wait_ge(ln_ssq, (b + 1) * TB)
                did(ve.tensor_scalar(var[:, 1, ts], var[:, 3, ts], 1.0 / D, 1e-06, ALU.mult, ALU.add), "var", 1, b)
                ve.wait_ge(ln_pow, B + b + 1)
                for t in tiles_of(b):
                    did(ve.tensor_scalar(xr[:, t, :], accA[:, t, :], rstd[:, 1, t:t + 1], None, ALU.mult), "xr", t)

            first_rms(0)
            ve.wait_ge(cx_mm, 1)
            ve.tensor_copy(cols[:, 0:NROW], bank["zb"][:, 0:NROW])
            ve.tensor_copy(gate_keep[:, :], bank["zb"][:, 64:64 + KD * E]).then_inc(cx_ev, 1)

            def turned(dst, b, at, banks, scale_at, blocks=range(KD)):
                for k in blocks:
                    ve.wait_ge(x_hi, at + k + 1)
                    hi = dst[:, 0, k, b * S:(b + 1) * S].bitcast(f32)
                    lo = dst[:, 1, k, b * S:(b + 1) * S]
                    if scale_at is None:
                        ve.tensor_tensor(lo, banks[k][:, :], hi, ALU.subtract).then_inc(x_lo, 1)
                    else:
                        ve.scalar_tensor_tensor(out=lo, in0=banks[k][:, :],
                                                scalar=cols[:, scale_at + k:scale_at + k + 1], in1=hi,
                                                op0=ALU.mult, op1=ALU.subtract).then_inc(x_lo, 1)

            ve.wait_ge(cx_ev, 1)
            turned(xrT, 0, 0, bS, L1)
            first_rms(1)
            ve.wait_ge(zeroed, 2)
            ve.wait_ge(consts, 5)
            ve.wait_ge(rope_in, 16)

            def mask_scores(u, i, it):
                until_apart(ve, s_mm, TB * u + i + 1, it, TB * GS)
                width = (i + 1) * P
                ve.tensor_tensor_reduce(pr[:, u % 2, P_OFF[i]:P_OFF[i] + width], bS[i % 2][:, 0:width],
                                        mask_t[:, S - width:S], INV_SCALE, BIG, ALU.add, ALU.min,
                                        nmax[:, u % 2, i:i + 1]).then_inc(s_free, 1)

            def invert(u, i, it):
                until(ve, e_done, TB * u + i + 1, it, TB * GS)
                ve.reciprocal(rinv[:, u % 2, i:i + 1], rsum[:, u % 2, i:i + 1]).then_inc(r_done, 1)

            def probs_lo(u, c, it):
                until(ve, pt_hi, 3 * u + c + 1, it, 3 * GS)
                a, b = PT_CHUNKS[c]
                cs = slice((a + 1) * P, (b + 1) * P)
                ve.tensor_tensor(pT[:, 1, cs], bT[(3 * u + c) % 2][:, 0:(b - a) * P],
                                 pT[:, 0, cs].bitcast(f32), ALU.subtract).then_inc(pt_lo, 1)

            def col_of(base, u, it):
                h = 4 * ((u - HALF) // GS) + u % 4 + base
                return cols[:, h:h + 1] if it is None else cols[:, bass.ds(it * 4 + h, 1)]

            def z_part(u, it):
                until(ve, z_hi, u + 1, it, GS)
                hi, lo = zT[:, u % 4, 0, :].bitcast(f32), zT[:, u % 4, 1, :]
                if u < HALF:
                    ve.tensor_tensor(lo, bank["zb"][:, :], hi, ALU.subtract).then_inc(z_lo, 1)
                else:
                    ve.scalar_tensor_tensor(out=lo, in0=bank["zb"][:, :], scalar=col_of(BV, u, it), in1=hi,
                                            op0=ALU.add, op1=ALU.subtract).then_inc(z_lo, 1)

            HI = {}
            for ch in CHUNK:
                if ch[0] not in ROT_W and ch[0] != "VT":
                    HI[ch] = len(HI)
            HI_W = [2, CHUNKS_W[1]]

            def chunk(ch, it):
                at, kind, v = CHUNK[ch], ch[0], ch[1]
                src = bJ[at % 2]
                phase = 0 if kind in ("Qrope", "Krope", "VT", "Vx") else 1
                if kind in ROT_W:
                    until(ve, j_mm, at + 1, it, CHUNKS_W[phase])
                    slots = 2 if kind == "Qrope" else 1
                    if v >= slots:
                        until(ve, rp_lo[kind], v + 1 - slots, it, ROT_W[kind])
                    until(ve, sw_done[kind], v + 1, it, ROT_W[kind])
                    ve.tensor_tensor(rot_sum(ch), src[:, :], cosT, ALU.mult).then_inc(j_lo, 1)
                elif kind != "VT":
                    until(ve, j_hi, HI[ch] + 1, it, HI_W[phase])
                    if kind in ("Q", "K"):
                        dst = (qT if kind == "Q" else kT)[:, v % 2]
                        ve.scalar_tensor_tensor(out=dst[:, 1], in0=src[:, :],
                                                scalar=col_of(BQ if kind == "Q" else BK, v, it),
                                                in1=dst[:, 0].bitcast(f32),
                                                op0=ALU.add, op1=ALU.subtract).then_inc(j_lo, 1)
                    elif kind == "Vx":
                        ve.tensor_tensor(vh[:, v % 2, 1, :, 0:P], src[:, :].rearrange("p (t e) -> p t e", t=TB),
                                         vh[:, v % 2, 0, :, 0:P].bitcast(f32), ALU.subtract).then_inc(j_lo, 1)
                    else:
                        ve.tensor_tensor(vh[:, v % 2, 1, ch[2], :], src[:, :],
                                         vh[:, v % 2, 0, ch[2], :].bitcast(f32), ALU.subtract).then_inc(j_lo, 1)

            def rope_sin(ch, it):
                if ch[0] in ROT_W:
                    half = swapped[ch[0]]
                    ve.tensor_tensor(half, half, sinT, ALU.mult).then_inc(rp_sin[ch[0]], 1)

            def rope_sum(ch, it):
                if ch[0] in ROT_W:
                    until(ve, rp_sin[ch[0]], ch[1] + 1, it, ROT_W[ch[0]])
                    ve.tensor_tensor(rot_sum(ch), rot_sum(ch), swapped[ch[0]], ALU.add
                                     ).then_inc(rp_sum[ch[0]], 1)

            def add_out(n, it):
                o = n - 2
                half, b = o % 2, o % GS // 4
                acc = accA if o < HALF else accB
                if o == HALF:
                    ve.wait_ge(bias_added, 2)
                until(ve, o_mm, o + 1, it, GS)
                until(ve, o_add, o + 1, it, GS)
                t = b * TB + 2 * half
                tiles = acc[:, t:t + 2, :]
                ve.tensor_tensor(tiles, bank["ob"][:, :].rearrange("p (t d) -> p t d", t=2), tiles,
                                 ALU.add).then_inc(o_add, 1)

            def step(n, it):
                chs = chunks_of(n) if n < UNITS else []
                if n < 0:
                    for ch in chs if n == -2 else []:
                        chunk(ch, it)
                        rope_sin(ch, it)
                        rope_sum(ch, it)
                    if n == -1:
                        _, q1, vx = chs
                        mask_scores(0, 0, it)
                        mask_scores(0, 1, it)
                        turned(xrT, 1, KD, bT, L1, [0])
                        mask_scores(0, 2, it)
                        turned(xrT, 1, KD, bT, L1, [1])
                        mask_scores(0, 3, it)
                        chunk(q1, it)
                        for i in range(TB):
                            invert(0, i, it)
                        rope_sin(q1, it)
                        rope_sum(q1, it)
                        chunk(vx, it)
                        turned(xnT, 0, B * KD, (bank["zb"], bank["ob"]), None)
                        probs_lo(0, 0, it)
                        probs_lo(0, 1, it)
                        turned(xnT, 1, B * KD + KD, (bank["zb"], bank["ob"]), None)
                    return
                nxt = n + 1 < UNITS
                rotary = n + 2 < HALF
                if nxt:
                    mask_scores(n + 1, 0, it)
                    mask_scores(n + 1, 1, it)
                for ch in over_from(n):
                    chunk(ch, it)
                v_behind = behind(n, 1, "Vx")
                k_behind = behind(n, 1, "Krope")
                if not rotary:
                    probs_lo(n, 2, it)
                elif v_behind:
                    chunk(v_behind[0], it)
                elif not k_behind:
                    chunk(chs[0], it)
                if nxt:
                    mask_scores(n + 1, 2, it)
                    invert(n + 1, 0, it)
                    invert(n + 1, 1, it)
                early = rotary and n % 4 < 2
                if early:
                    probs_lo(n, 2, it)
                if nxt:
                    mask_scores(n + 1, 3, it)
                    invert(n + 1, 2, it)
                if rotary:
                    if not early:
                        probs_lo(n, 2, it)
                    for ch in k_behind:
                        chunk(ch, it)
                    if v_behind or k_behind:
                        chunk(chs[0], it)
                    rope_sin(chs[0], it)
                if nxt:
                    invert(n + 1, 3, it)
                if rotary:
                    rope_sum(chs[0], it)
                if 2 <= n:
                    add_out(n, it)
                for ch in k_behind:
                    rope_sin(ch, it)
                    rope_sum(ch, it)
                if n == UNITS - 3:
                    ve.wait_ge(ln_ssq, 2 * NT)
                    did(ve.tensor_scalar(var[:, 2], var[:, 3], 1.0 / D, 1e-06, ALU.mult, ALU.add), "var", 2)
                for ch in [] if rotary else chs[:2]:
                    chunk(ch, it)
                if n == UNITS - 2:
                    split_gate()
                    scale_rows(range(TB, NT))
                if n == UNITS - 1:
                    turned2(2)
                z_part(n, it)
                if nxt:
                    probs_lo(n + 1, 0, it)
                    probs_lo(n + 1, 1, it)
                if n == UNITS - 3:
                    scale_rows(range(TB))
                if n == UNITS - 2:
                    turned2(0)
                    turned2(1)
                for ch in chs[1:2] if rotary else []:
                    if ch[0] == "V":
                        chunk(ch, it)

            def split_gate():
                for h in range(2):
                    ve.memset(gateT[:, h].bitcast(f32), 0.0).then_inc(zeroed, 1)
                ve.wait_ge(zeroed, 4)
                gk = gate_keep[:, :].rearrange("p (k e) -> p k e", k=KD)
                ve.tensor_copy(gateT[:, 0, :, 0:E], gk).then_inc(g_hi, 1)
                ve.wait_ge(g_hi, 1)
                ve.tensor_tensor(gateT[:, 1, :, 0:E], gk, gateT[:, 0, :, 0:E].bitcast(f32),
                                 ALU.subtract).then_inc(g_hi, 1)

            def scale_rows(tiles):
                ve.wait_ge(ln_pow, 2 * B + 1)
                for t in tiles:
                    did(ve.tensor_scalar(xr2(t), accA[:, t, :], rstd[:, 2, t:t + 1], None, ALU.mult), "xr2", t)

            def turned2(i):
                b, k = i // KD, i % KD
                ve.wait_ge(x_hi, 2 * B * KD + i + 1)
                cs = slice(b * S, (b + 1) * S)
                ve.scalar_tensor_tensor(out=xrT[:, 1, k, cs], in0=bJ[i % 2][:, :],
                                        scalar=cols[:, L2 + k:L2 + k + 1], in1=xrT[:, 0, k, cs].bitcast(f32),
                                        op0=ALU.mult, op1=ALU.subtract).then_inc(x_lo, 1)

            windows(ve, step)

            turned2(3)
            for b in range(B):
                ve.wait_ge(lg_mm, b + 1)
                ve.tensor_copy(lgT[0:E, b * S:(b + 1) * S], bS[b][0:E, :]).then_inc(lg_ev, 1)
            add_out(UNITS, None)

            over = lambda ap: ap.unsqueeze(2).to_broadcast([P, NT, E])
            logits = bT[0][:, 0:NT * E].rearrange("p (t e) -> p t e", t=NT)
            probs, biased, left = (route[:, i, :, 0:E] for i in range(3))
            count = [0]

            def then(ins):
                count[0] += 1
                ins.then_inc(rt, 1)
                ve.wait_ge(rt, count[0])

            def select(part):
                if part == 0:
                    ve.wait_ge(lt_mm, 1)
                    then(ve.tensor_reduce(rsm[:, 0], logits, AX.X, ALU.max))
                    then(ve.tensor_tensor(probs, logits, over(rsm[:, 0]), ALU.subtract))
                elif part == 1:
                    ve.wait_ge(rt_exp, 1)
                    then(ve.tensor_reduce(rsm[:, 1], probs, AX.X, ALU.add))
                    then(ve.reciprocal(rsm[:, 2], rsm[:, 1]))
                    then(ve.tensor_tensor(probs, probs, over(rsm[:, 2]), ALU.mult))
                    then(ve.tensor_tensor(biased, probs, be_t[:, :].unsqueeze(1).to_broadcast([P, NT, E]), ALU.add))
                elif part == 2:
                    ve.memset(route[:, 1, :, E:RW], -BIG)
                    for t in range(NT):
                        last = ve.max(top8[:, t, :], route[:, 1, t, 0:E])
                    then(last)
                    then(ve.memset(top8[:, :, TOPK:8], -BIG))
                elif part == 3:
                    for t in range(NT):
                        last = ve.match_replace(out=route[:, 2, t, :], in_to_replace=top8[:, t, :],
                                                in_values=route[:, 1, t, :], imm_value=-0.5 * BIG)
                    then(last)
                    then(ve.tensor_tensor(left, left, biased, ALU.not_equal))
                else:
                    then(ve.tensor_tensor(cw, probs, left, ALU.mult))
                    then(ve.tensor_reduce(rsm[:, 3], cw, AX.X, ALU.add))
                    then(ve.tensor_scalar(rsm[:, 0], rsm[:, 3], 1e-12, None, ALU.max))
                    then(ve.reciprocal(rsm[:, 1], rsm[:, 0]))
                    then(ve.tensor_tensor(cw, cw, over(rsm[:, 1]), ALU.mult))

            NW = 4 * (NPAIR + 1)

            def make_h(w, tt, it):
                M, g, tile = w // 4, 2 * w + tt, 2 * (w % 4) + tt
                until(ve, si_done, g + 1, it, 16)
                if M == 0:
                    ve.tensor_tensor(hrow[:, w % 2, tt, 0:P], bJ[g % 2][:, P:2 * P], silu[:, g % 2, 0:P],
                                     ALU.mult).then_inc(h_done, 1)
                    return
                for j in range(2):
                    e = 2 * (M - 1) + j
                    c = cw[:, tile, e:e + 1] if it is None else cw[:, tile, bass.ds(it * 4 + e, 1)]
                    last = ve.scalar_tensor_tensor(out=hrow[:, w % 2, tt, j * P:(j + 1) * P],
                                                   in0=silu[:, g % 2, j * P:(j + 1) * P], scalar=c,
                                                   in1=bJ[g % 2][:, (2 + j) * P:(3 + j) * P],
                                                   op0=ALU.mult, op1=ALU.mult)
                last.then_inc(h_done, 1)

            def h_lo(w, it):
                width = 2 * P if w < 4 else 4 * P
                until(ve, ht_hi, w + 1, it, 8)
                ve.tensor_tensor(hT[:, w % 2, 1, 0:width], bH[w % 2][:, 0:width],
                                 hT[:, w % 2, 0, 0:width].bitcast(f32), ALU.subtract).then_inc(ht_lo, 1)

            def expert_step(w, it):
                if w + 1 < NW:
                    make_h(w + 1, 0, it)
                h_lo(w, it)
                if w + 1 < NW:
                    make_h(w + 1, 1, it)

            select(0)
            add_out(UNITS + 1, None)
            select(1)
            make_h(0, 0, None)
            make_h(0, 1, None)
            for w in range(3):
                expert_step(w, None)
                select(w + 2)
            for w in range(3, 5):
                expert_step(w, None)
            with ve.Fori(0, NPAIR // 2 - 1) as it:
                for w in range(5, 13):
                    expert_step(w, it)
            for w in range(5 + 8 * (NPAIR // 2 - 1), NW):
                expert_step(w, None)
            ve.wait_ge(res_done, 1)
            for tp in range(NT // 2):
                ve.wait_ge(dn_mm, NW - 4 + tp + 1)
                tiles = accB[:, 2 * tp:2 * tp + 2, :]
                ve.tensor_tensor(tiles, bY[tp][:, :].rearrange("p (t d) -> p t d", t=2), tiles,
                                 ALU.add).then_inc(y_done, 1)


_A = ["x", "W_Q", "W_K", "W_V", "W_O", "b_Q", "b_K", "b_V", "b_O"]
_F = ["ln1_w", "ln2_w", "wq", "wk", "wv", "wo", "gate_w", "bias_e", "weg", "weu", "wed", "wsg", "wsu", "wsd"]
_INS = [f"L0_attn_{n}" for n in _A] + [f"L0_ffn_{n}" for n in _F]


def _rope_table(positions, d, theta):
    import numpy as np

    f = np.float32
    inv_freq = (f(1.0) / np.power(f(theta), np.arange(0, d, 2, dtype=f) / f(d))).astype(f)
    angle = (np.arange(positions, dtype=f)[None, :] * inv_freq[:, None]).astype(f)
    cos, sin = np.cos(angle).astype(f), np.sin(angle).astype(f)
    return np.concatenate([np.concatenate([cos, cos]), np.concatenate([-sin, sin])], axis=1)


def kernel(**inputs):
    import numpy as _np
    import concourse.bacc as _bacc
    from concourse import mybir as _mybir
    from concourse.bass_utils import run_bass_kernel_spmd as _run

    nc = _bacc.Bacc("TRN2", target_bir_lowering=False, num_devices=1)
    arrays, args = {}, []
    named = {n: _np.ascontiguousarray(inputs[n]) for n in _INS}
    seq, d_head = named["L0_attn_x"].shape[1], named["L0_attn_W_Q"].shape[2]
    named["rope_table"] = _rope_table(seq, d_head, 10000.0)
    for name, a in named.items():
        arrays[f"in_{name}_dram"] = a
        args.append(nc.dram_tensor(f"in_{name}_dram", a.shape, _mybir.dt.from_np(a.dtype), kind="ExternalInput").ap())
    shape = named["L0_attn_x"].shape
    args.append(nc.dram_tensor("out_0_dram", shape, _mybir.dt.float32, kind="ExternalOutput").ap())
    attention_pair_moe_kernel(nc, *args)
    r = _run(nc, [arrays], core_ids=[0])
    return r.results[0]["out_0_dram"]
```

```python
import concourse.bass as bass
from concourse import mybir
from contextlib import ExitStack


def attention_pair_moe_kernel(
    nc: bass.Bass,
    x: bass.AP, W_Q: bass.AP, W_K: bass.AP, W_V: bass.AP, W_O: bass.AP,
    b_Q: bass.AP, b_K: bass.AP, b_V: bass.AP, b_O: bass.AP,
    ln1_w: bass.AP, ln2_w: bass.AP,
    wq: bass.AP, wk: bass.AP, wv: bass.AP, wo: bass.AP,
    gate_w: bass.AP, bias_e: bass.AP,
    weg: bass.AP, weu: bass.AP, wed: bass.AP,
    wsg: bass.AP, wsu: bass.AP, wsd: bass.AP,
    rope_table: bass.AP,
    out: bass.AP,
):
    f32, f32r = mybir.dt.float32, mybir.dt.float32r
    ALU = mybir.AluOpType
    ACT = mybir.ActivationFunctionType
    AX = mybir.AxisListType

    B, S, D = x.shape
    P = 128
    NH = W_Q.shape[0]
    E = gate_w.shape[0]
    TOPK = 4
    KD = D // P
    NT = B * S // P
    TB = S // P
    HALF = NH * B
    UNITS = 2 * HALF
    GS = 4 * B
    NPAIR = E // 2
    INV_SCALE = -float(P) ** -0.5
    MASKED = -1.0e30
    BIG = 3.0e38

    def chunks_of(n):
        if n == -2:
            return [("Krope", 0), ("Qrope", 0)]
        if n == -1:
            return [("VT", 0), ("Qrope", 1), ("Vx", 0)]
        v, c1, found = n + 2, n // 4 + 1, []
        if v < HALF:
            found.append(("Qrope", v))
        elif v < UNITS:
            found += [("Q", v), ("K", v)]
        if c1 < HALF // 4:
            if n % 4 < 3:
                found.append([("Krope", c1), ("VT", c1), ("Vx", c1)][n % 4])
        elif c1 < UNITS // 4:
            found.append(("V", c1, n % 4))
        return found

    CHUNK = {}
    for n in range(-2, UNITS):
        for ch in chunks_of(n):
            CHUNK[ch] = len(CHUNK)

    def behind(n, steps, kind):
        at = n - steps
        return [ch for ch in chunks_of(at) if ch[0] == kind] if at >= 0 else []

    def over_from(n):
        return chunks_of(n - 1)[2:] if n > 0 else []

    def jobs_of(n):
        if n == -2:
            return [("KV", 0)] + [(f"Q{q}", 0) for q in range(4)]
        a, s, found = n // GS, n % GS, []
        if n < 0 or n >= UNITS:
            return found
        if s == 0:
            found.append(("O0", a))
        if s == 2:
            found.append(("O1", a))
        if s == (3 if a + 1 <= HALF // GS else 4) and a + 1 < UNITS // GS:
            found.append(("KV", a + 1))
        if 4 <= s < 8 and a + 1 < UNITS // GS:
            found.append((f"Q{s - 4}", a + 1))
        return found

    JOB = {}
    for n in range(-2, UNITS):
        for job in jobs_of(n):
            JOB[job] = len(JOB)
    LN = {}
    for b in range(B):
        for t in range(b * TB, (b + 1) * TB):
            LN["stats", t] = len(LN) + 1
        for t in range(b * TB, (b + 1) * TB):
            LN["mean_var", t] = len(LN) + 1
        LN["var", 0, b] = len(LN) + 1
    for t in range(NT):
        LN["xn", t] = len(LN) + 1
    for b in range(B):
        LN["var", 1, b] = len(LN) + 1
        for t in range(b * TB, (b + 1) * TB):
            LN["xr", t] = len(LN) + 1
    LN["var", 2] = len(LN) + 1
    for t in range(NT):
        LN["xr2", t] = len(LN) + 1

    GA = HALF // GS
    START = 3
    CHUNKS_W = [sum(len(chunks_of(n)) for n in range(w, w + GS)) for w in (START, HALF + START)]
    ROT_W = {"Qrope": GS, "Krope": GS // 4}
    JOBS_W = 7
    assert all(c % 2 == 0 for c in CHUNKS_W)

    NW = B + 2 * B * NPAIR

    def expert_of(w):
        return (0, 0, w) if w < B else ((w - B) // (2 * B) + 1, (w - B) // B % 2, (w - B) % B)

    def first_of(M):
        return 0 if M == 0 else B + 2 * B * (M - 1)

    UNITS_W = 4 * B
    WSTART = 3
    TURNS = NPAIR // 2 - 1

    BLOCKS = [(3, 3), (0, 0), (0, 1), (0, 2), (0, 3), (1, 1), (1, 2), (1, 3), (2, 2), (2, 3)]
    PT_CHUNKS = [(0, 4), (4, 8), (8, 10)]
    PT_COLS = len(BLOCKS) * P + P
    PT_ROW = {0: (2 * P, 0), 1: (6 * P, P), 2: (9 * P, 2 * P), 3: (0, 2 * P)}
    P_OFF = [i * (i + 1) // 2 * P for i in range(TB)]
    P_COLS = TB * (TB + 1) // 2 * P
    PASSES = [(0, 0), (0, 1), (1, 0)]

    ctx = ExitStack()
    with ctx:
        def sb(name, cols, dt=f32, rows=P):
            return ctx.enter_context(nc.sbuf_tensor(name, [rows, cols], dt))

        def sem(name):
            return ctx.enter_context(nc.semaphore(name))

        accB_t = sb("acc_b", NT * D)
        accA_t = sb("acc_a", NT * D)
        xnT_t = sb("xnT", 2 * KD * NT * P, f32r)
        xrT_t = sb("xrT", 2 * KD * NT * P, f32r)
        q_t = sb("q_heads", 2 * 2 * S, f32r)
        k_t = sb("k_heads", 2 * 2 * S, f32r)
        v_t = sb("v_heads", 2 * 2 * TB * 4 * P, f32r)
        p_t = sb("probs", 2 * P_COLS)
        pt_t = sb("probsT", 2 * PT_COLS, f32r)
        z_t = sb("zT", 4 * 2 * S, f32r)
        wqk_t = sb("w_qk", 4 * 2 * 2 * KD * P, f32r)
        wkv_t = sb("w_kv", 2 * KD * 4 * P, f32r)
        wo_t = sb("w_o", 2 * 2 * 2 * D, f32r)
        rq_t = sb("raw_qk", 4 * 2 * KD * P)
        rkv_t = sb("raw_kv", KD * 4 * P)
        ro_t = sb("raw_o", 2 * 2 * D)
        rope_t = sb("rope", 2 * S)
        t1_t = sb("rope_sum", 3 * S)
        sw_t = sb("rope_swapped", 2 * S)
        vt_t = sb("vT", S)
        mask_t = sb("mask", S)
        ident = sb("ident", P)
        rows_t = sb("const_rows", P)
        cols_t = sb("const_cols", 64)
        gate_keep = sb("gate_cols", KD * E)
        bO_t = sb("b_o", D)
        be_t = sb("bias_e", E)
        nmax_t = sb("neg_max", 2 * TB)
        sum_t = sb("row_sum", 2 * TB)
        inv_t = sb("inv_sum", 2 * TB)
        stats_t = sb("ln_stats", NT * 6)
        mv_t = sb("ln_mean_var", NT * 2)
        var_t = sb("var", 4 * NT)
        rstd_t = sb("rstd", 4 * NT)
        mhalf_t = sb("minus_half", NT)
        cw_t = sb("combine", NT * E)
        rt_t = sb("router", 3 * NT * (E + TOPK))
        small_t = sb("router_small", NT * 8 + 4 * NT)

        accB = accB_t[:, :].rearrange("p (t d) -> p t d", t=NT)
        accA = accA_t[:, :].rearrange("p (t d) -> p t d", t=NT)
        xnT = xnT_t[:, :].rearrange("p (h k t) -> p h k t", h=2, k=KD)
        xrT = xrT_t[:, :].rearrange("p (h k t) -> p h k t", h=2, k=KD)
        qT = q_t[:, :].rearrange("p (s h t) -> p s h t", s=2, h=2)
        kT = k_t[:, :].rearrange("p (s h t) -> p s h t", s=2, h=2)
        vh = v_t[:, :].rearrange("p (s h t c) -> p s h t c", s=2, h=2, t=TB)
        pr = p_t[:, :].rearrange("p (s c) -> p s c", s=2)
        pT = pt_t[:, :].rearrange("p (h c) -> p h c", h=2)
        zT = z_t[:, :].rearrange("p (s h t) -> p s h t", s=4, h=2)
        wqk = wqk_t[:, :].rearrange("p (q w h k e) -> p q w h k e", q=4, w=2, h=2, k=KD)
        wkvA = wkv_t[:, :].rearrange("p (h c) -> p h c", h=2)
        wkvB = wkv_t[:, :].rearrange("p (h k e) -> p h k e", h=2, k=KD)
        w_o = wo_t[:, :].rearrange("p (o h j d) -> p o h j d", o=2, h=2, j=2)
        rq = rq_t[:, :].rearrange("p (q w k e) -> p q w k e", q=4, w=2, k=KD)
        ro = ro_t[:, :].rearrange("p (o j d) -> p o j d", o=2, j=2)
        cosT, sinT = rope_t[:, 0:S], rope_t[:, S:2 * S]
        t1 = t1_t[:, :].rearrange("p (s t) -> p s t", s=3)
        swapped = {"Qrope": sw_t[:, 0:S], "Krope": sw_t[:, S:2 * S]}
        rot_sum = lambda ch: t1[:, ch[1] % 2 if ch[0] == "Qrope" else 2]
        nmax = nmax_t[:, :].rearrange("p (s i) -> p s i", s=2)
        rsum = sum_t[:, :].rearrange("p (s i) -> p s i", s=2)
        rinv = inv_t[:, :].rearrange("p (s i) -> p s i", s=2)
        stats = stats_t[:, :].rearrange("p (t c) -> p t c", t=NT)
        mv = mv_t[:, :].rearrange("p (t c) -> p t c", t=NT)
        var = var_t[:, :].rearrange("p (w t) -> p w t", w=4)
        rstd = rstd_t[:, :].rearrange("p (w t) -> p w t", w=4)
        gaterow_t = sw_t[:, S:S + D]
        xr = p_t[:, 0:NT * D].rearrange("p (t d) -> p t d", t=NT)
        BQ, BK, BV, L1, L2 = 0, NH, 2 * NH, 3 * NH, 3 * NH + KD
        NROW = 3 * NH + 2 * KD
        cols = cols_t
        mgu = wqk_t[:, :].rearrange("p (s h k c) -> p s h k c", s=2, h=2, k=KD)
        mwd = wkv_t[:, :].rearrange("p (s h j d) -> p s h j d", s=2, h=2, j=2)
        rgu = rq_t[:, :].rearrange("p (s k c) -> p s k c", s=2, k=KD)
        rwd = rkv_t[:, :].rearrange("p (s j d) -> p s j d", s=2, j=2)
        gateT = q_t[:, 0:2 * KD * P].rearrange("p (h k e) -> p h k e", h=2, k=KD)
        h_raw = p_t[:, 0:2 * S].rearrange("p (s t) -> p s t", s=2)
        silu = p_t[:, 2 * S:4 * S].rearrange("p (s t) -> p s t", s=2)
        hT = z_t[:, 0:2 * 2 * S].rearrange("p (s h t) -> p s h t", s=2, h=2)
        lgT = sw_t
        xr2 = lambda t: (rope_t if t < TB else t1_t)[:, t % TB * D:(t % TB + 1) * D]
        RW = E + TOPK
        route = rt_t[:, :].rearrange("p (w t e) -> p w t e", w=3, t=NT)
        cw = cw_t[:, :].rearrange("p (t e) -> p t e", t=NT)
        top8 = small_t[:, 0:NT * 8].rearrange("p (t e) -> p t e", t=NT)
        rsm = small_t[:, NT * 8:NT * 8 + 4 * NT].rearrange("p (w t) -> p w t", w=4)

        bank = {n: ctx.enter_context(nc.psum_tensor(n, [P, 512], f32))
                for n in ("s0", "s1", "t0", "t1", "j0", "j1", "zb", "ob")}
        bS = [bank["s0"], bank["s1"]]
        bT = [bank["t0"], bank["t1"]]
        bJ = [bank["j0"], bank["j1"]]
        bY = [[bank["s0"], bank["s1"]], [bank["t0"], bank["t1"]]]
        bG = [bank["j0"], bank["zb"]]
        bU = [bank["j1"], bank["ob"]]

        x_in = [sem(f"x_in_{b}") for b in range(B)]
        rows_in, rope_in, bc_in = sem("rows_in"), sem("rope_in"), sem("bc_in")
        raw_in = {w: sem(f"raw_in_{w}") for w in ("KV", "Q0", "Q1", "Q2", "Q3", "O0", "O1")}
        consts = sem("pool_consts")
        zeroed = sem("zeroed")
        ln_step = sem("ln_vector")
        ln_ssq, ln_pow = sem("ssq_done"), sem("rstd_done")
        bias_added = sem("bias_added")
        cx_mm, cx_ev = sem("const_turned"), sem("const_kept")
        x_mm, x_hi, x_lo = sem("x_turned"), sem("xT_hi"), sem("xT_lo")
        s_mm, s_free = sem("scores_done"), sem("scores_taken")
        e_done, r_done, p_norm = sem("exp_done"), sem("inverse_done"), sem("probs_normed")
        t_mm, pt_hi, pt_lo = sem("probs_turned"), sem("pT_hi"), sem("pT_lo")
        z_mm, z_hi, z_lo = sem("z_done"), sem("zT_hi"), sem("zT_lo")
        o_mm, o_add = sem("outproj_done"), sem("outproj_added")
        j_mm, j_hi, j_lo = sem("proj_done"), sem("proj_hi"), sem("proj_kept")
        sw_done, rp_sin, rp_sum, rp_hi, rp_lo = (
            {kind: sem(f"{kind}_{stage}") for kind in ("Qrope", "Krope")}
            for stage in ("swapped", "sin_done", "sum_done", "hi", "lo"))
        w_hi, w_done = sem("weights_hi"), sem("weights_split")
        lg_mm, lg_ev, lt_mm, rt = sem("logits_done"), sem("logits_kept"), sem("logits_turned"), sem("router_vector")
        rt_exp = sem("router_exp")
        g_hi = sem("gate_split")
        gu_mm, si_done, h_done = sem("gateup_done"), sem("silu_done"), sem("h_done")
        ht_hi, ht_lo = sem("hT_hi"), sem("hT_lo")
        dn_mm = sem("down_done")
        mraw_gu = [sem("raw_gu0"), sem("raw_gu1")]
        mraw_d = [sem("raw_d0"), sem("raw_d1")]
        mw_hi, mw_done = sem("expert_weights_hi"), sem("expert_weights_split")
        waits_passed = sem("waits_passed")
        res_done, y_acc, out_sem = sem("residual_sum"), sem("y_added"), sem("out_written")

        def until(eng, s, count, it=None, per=0):
            eng.wait_ge(s, count if it is None or per == 0 else it * per + count)

        def until_apart(eng, s, count, it=None, per=0):
            until(eng, s, count, it, per)
            stand_apart(eng, it)

        def stand_apart(eng, it):
            if it is not None:
                eng.sem_inc(waits_passed, 1)

        def windows(eng, step):
            for n in range(-2, START):
                step(n, None)
            for phase in range(2):
                first = phase * HALF + START
                with eng.Fori(0, GA - 1) as it:
                    for n in range(first, first + GS):
                        step(n, it)
                for n in range(first + (GA - 1) * GS, min(first + GA * GS, UNITS)):
                    step(n, None)

        block = ctx.enter_context(nc.Block())

        @block.sync
        def _(sp):
            xv = x.rearrange("b (t p) d -> p (b t) d", p=P)
            for b in range(B):
                sp.dma_start(accB[:, b * TB:(b + 1) * TB, :], xv[:, b * TB:(b + 1) * TB, :]).then_inc(x_in[b], 16)
            for at, src in ((BQ, b_Q), (BK, b_K), (BV, b_V)):
                sp.dma_start(rows_t[at:at + NH, :], src).then_inc(rows_in, 16)
            for at, src in ((L1, ln1_w), (L2, ln2_w)):
                sp.dma_start(rows_t[at:at + KD, :], src.rearrange("(k p) -> k p", p=P)).then_inc(rows_in, 16)
            sp.dma_start(gaterow_t[0:E, :], gate_w).then_inc(rows_in, 16)

            wqv = wq.rearrange("(k p) c -> p k c", p=P)
            wkv_ = wk.rearrange("(k p) c -> p k c", p=P)
            wvv = wv.rearrange("(k p) c -> p k c", p=P)
            wov = wo.rearrange("(h e) d -> e h d", e=P)

            def load(which, g, phase):
                if phase == 0:
                    if which == "KV":
                        for i, src in enumerate((wkv_, wvv)):
                            dst = rkv_t[:, i * KD * P:(i + 1) * KD * P].rearrange("p (k e) -> p k e", k=KD)
                            sp.dma_start(dst, src[:, :, bass.ds(g * P, P)]).then_inc(raw_in["KV"], 16)
                    elif which[0] == "Q":
                        q = int(which[1])
                        sp.dma_start(rq[:, q, 0], wqv[:, :, bass.ds(g * (4 * P) + q * P, P)]).then_inc(raw_in[which], 16)
                    else:
                        o = int(which[1])
                        sp.dma_start(ro[:, o], wov[:, bass.ds(g * 4 + 2 * o, 2), :]).then_inc(raw_in[which], 16)
                else:
                    if which == "KV":
                        for k in range(KD):
                            dst = rkv_t[:, k * 4 * P:(k + 1) * 4 * P].rearrange("p (h e) -> p h e", h=4)
                            sp.dma_start(dst, W_V[bass.ds(g * 4, 4), k * P:(k + 1) * P, :].rearrange("h p e -> p h e")
                                         ).then_inc(raw_in["KV"], 16)
                    elif which[0] == "Q":
                        q = int(which[1])
                        for i, src in enumerate((W_Q, W_K)):
                            sp.dma_start(rq[:, q, i], src[bass.ds(g * 4 + q, 1), :, :].rearrange("h (k p) e -> p (h k) e", p=P)
                                         ).then_inc(raw_in[which], 16)
                    else:
                        o = int(which[1])
                        sp.dma_start(ro[:, o], W_O[bass.ds(g * 4 + 2 * o, 2), :, :].rearrange("h e d -> e h d")
                                     ).then_inc(raw_in[which], 16)

            kinds = ("KV", "Q0", "Q1", "Q2", "Q3", "O0", "O1")
            for which in kinds:
                load(which, 0, 0)

            def loads(a, phase, g):
                for which in kinds:
                    done = {"KV": -6, "Q0": -5, "Q1": -4, "Q2": -3, "Q3": -2, "O0": -1, "O1": 0}[which]
                    sp.wait_ge(w_done, a * JOBS_W + done)
                    load(which, g, phase)

            with sp.Fori(1, GA) as a:
                loads(a, 0, a)
            with sp.Fori(GA, 2 * GA) as a:
                loads(a, 1, a - GA)

            sp.wait_ge(w_done, len(JOB))
            wsgv, wsuv = (w.rearrange("(k p) i -> p k i", p=P) for w in (wsg, wsu))

            def load_shared():
                for i, src in enumerate((wsgv, wsuv)):
                    sp.dma_start(rgu[:, 0, :, i * P:(i + 1) * P], src).then_inc(mraw_gu[0], 16)
                sp.dma_start(rwd[:, 0, 0], wsd).then_inc(mraw_d[0], 16)

            def load_pair(slot, m):
                for i, src in enumerate((weg, weu)):
                    for j in range(2):
                        at = (2 * i + j) * P
                        sp.dma_start(rgu[:, slot, :, at:at + P],
                                     src[bass.ds(m * 2 + j, 1), :, :].rearrange("e (k p) i -> p (e k) i", p=P)
                                     ).then_inc(mraw_gu[slot], 16)
                sp.dma_start(rwd[:, slot], wed[bass.ds(m * 2, 2), :, :].rearrange("e i d -> i e d")
                             ).then_inc(mraw_d[slot], 16)

            load_shared()
            load_pair(1, 0)
            with sp.Fori(1, NPAIR // 2) as r:
                for j in range(2):
                    sp.wait_ge(mw_done, r * 4 + 2 * j - 2)
                    load_pair(j, r * 2 + (j - 1))
            sp.wait_ge(mw_done, 2 * (NPAIR - 2) + 2)
            load_pair(0, NPAIR - 1)

            ov = out.rearrange("b (t p) d -> p (b t) d", p=P)
            for tp in range(NT // 2):
                sp.wait_ge(y_acc, 2 * (NW - B) + tp + 1)
                sp.dma_start(ov[:, 2 * tp:2 * tp + 2, :], accB[:, 2 * tp:2 * tp + 2, :]).then_inc(out_sem, 16)
            sp.wait_ge(out_sem, 16 * (NT // 2))

        @block.gpsimd
        def _(pool):
            pool.memset(ident[:, :], 0.0).then_inc(consts, 1)
            pool.memset(mask_t[:, :], 0.0).then_inc(consts, 1)
            pool.memset(mhalf_t[:, :], -0.5).then_inc(consts, 1)
            pool.wait_ge(consts, 2)
            pool.affine_select(out=ident[:, :], in_=ident[:, :], compare_op=ALU.not_equal, fill=1.0,
                               base=0, pattern=[[-1, P]], channel_multiplier=1).then_inc(consts, 1)
            diag = mask_t[:, S - P:S]
            pool.affine_select(out=diag, in_=diag, compare_op=ALU.is_ge, fill=MASKED,
                               base=0, pattern=[[-1, P]], channel_multiplier=1).then_inc(consts, 1)

            def power(w, b):
                ts = slice(0, NT) if b is None else slice(b * TB, (b + 1) * TB)
                pool.wait_ge(ln_step, LN["var", w] if b is None else LN["var", w, b])
                pool.tensor_tensor(rstd[:, w, ts], var[:, w, ts], mhalf_t[:, ts], ALU.pow).then_inc(ln_pow, 1)

            pool.wait_ge(consts, 3)
            for b in range(B):
                power(0, b)

            def weights(job, it):
                which, a = job
                phase, at = (0 if a < GA else 1), JOB[job]
                if which[0] == "Q":
                    count, per = (16 * (a + 1), 16) if phase == 0 else (16 * GA + 32 * (a - GA + 1), 32)
                elif which == "KV":
                    count, per = 32 * (a + 1), 32
                else:
                    count, per = 16 * (a + 1), 16
                until(pool, raw_in[which], count, it, per)
                if which[0] == "Q" and a:
                    v = GS * (a - 1) + 4 + int(which[1])
                    last = ("Qrope", v) if v < HALF else ("K", v)
                    until(pool, j_mm, CHUNK[last] + 1, it, CHUNKS_W[0 if v < HALF else 1])
                if which == "KV" and a:
                    c = 2 * (a - 1) + 1
                    last = ("VT", c) if c < HALF // 4 else ("V", c, 3)
                    until(pool, j_mm, CHUNK[last] + 1, it, CHUNKS_W[0 if c < HALF // 4 else 1])
                if which == "O0" and a:
                    until(pool, o_mm, GS * a - 2, it, GS)
                if which == "O1" and a:
                    until(pool, o_mm, GS * a, it, GS)
                if which[0] == "Q" and phase == 0:
                    q = int(which[1])
                    view = lambda ap: ap.rearrange("p k (w i) -> p k w i", w=2)
                    parts = [(view(wqk[:, q, 0, 0]), view(wqk[:, q, 0, 1]),
                              rq[:, q, 0].rearrange("p k (i w) -> p k w i", w=2))]
                elif which[0] == "Q":
                    q = int(which[1])
                    parts = [(wqk[:, q, :, 0], wqk[:, q, :, 1], rq[:, q])]
                elif which == "KV" and phase == 0:
                    half = KD * P
                    kk = lambda ap: ap[:, 0:half].rearrange("p (k w i) -> p k w i", k=KD, w=2)
                    parts = [(kk(wkvA[:, 0]), kk(wkvA[:, 1]),
                              rkv_t[:, 0:half].rearrange("p (k i w) -> p k w i", k=KD, w=2)),
                             (wkvA[:, 0, half:2 * half], wkvA[:, 1, half:2 * half], rkv_t[:, half:2 * half])]
                elif which == "KV":
                    parts = [(wkvA[:, 0], wkvA[:, 1], rkv_t[:, :])]
                else:
                    o = int(which[1])
                    parts = [(w_o[:, o, 0], w_o[:, o, 1], ro[:, o])]
                stand_apart(pool, it)
                for hi, _, raw in parts:
                    last = pool.tensor_scalar(hi, raw, 1.0, 1.0, ALU.mult, ALU.mult)
                last.then_inc(w_hi, 1)
                until(pool, w_hi, at + 1, it, JOBS_W)
                for hi, lo, raw in parts:
                    last = pool.tensor_tensor(lo, raw, hi.bitcast(f32), ALU.subtract)
                last.then_inc(w_done, 1)

            def normalise(n, it):
                if -1 <= n < UNITS - 1:
                    u = n + 1
                    for i in range(TB):
                        until_apart(pool, r_done, TB * u + i + 1, it, TB * GS)
                        piece = pr[:, u % 2, P_OFF[i]:P_OFF[i] + (i + 1) * P]
                        pool.tensor_scalar(piece, piece, rinv[:, u % 2, i:i + 1], 1.0,
                                           ALU.mult, ALU.mult).then_inc(p_norm, 1)

            def q_sin(n, it):
                for kind, v, *_ in chunks_of(n):
                    if kind == "Qrope":
                        until(pool, sw_done[kind], v + 1, it, ROT_W[kind])
                        pool.tensor_tensor(swapped[kind], swapped[kind], sinT, ALU.mult).then_inc(rp_sin[kind], 1)

            def q_lo(n, it):
                for kind, v, *_ in chunks_of(n):
                    if kind == "Qrope":
                        until(pool, rp_hi[kind], v + 1, it, ROT_W[kind])
                        pool.tensor_tensor(qT[:, v % 2, 1], rot_sum((kind, v)), qT[:, v % 2, 0].bitcast(f32),
                                           ALU.subtract).then_inc(rp_lo[kind], 1)

            def step(n, it):
                first_jobs = [j for j in jobs_of(n) if j[0] == "KV" and j[1] > GA]
                for job in first_jobs:
                    weights(job, it)
                if n >= 0:
                    q_sin(n, it)
                    normalise(n, it)
                    q_lo(n, it)
                if n == UNITS - 4:
                    power(2, None)
                for job in jobs_of(n)[1 if n == -2 else len(first_jobs):]:
                    if n == -2 and job[0] == "Q2":
                        q_sin(n, it)
                        q_lo(n, it)
                    weights(job, it)
                if n == -1:
                    q_sin(n, it)
                    normalise(n, it)
                    q_lo(n, it)
                if n in (1, 2):
                    pool.wait_ge(bc_in, 32)
                    half = NT // 2
                    tiles = accB[:, (n - 1) * half:n * half, :]
                    pool.tensor_tensor(tiles, tiles, bO_t[:, :].unsqueeze(1).to_broadcast([P, half, D]),
                                       ALU.add).then_inc(bias_added, 1)

            weights(("KV", 0), None)
            for b in range(B):
                power(1, b)
            pool.wait_ge(rope_in, 16)
            windows(pool, step)

            pool.wait_ge(j_mm, len(CHUNK))

            def expert_split(kind, M, it, raw_count, raw_per):
                slot = M % 2
                at = 2 * M + (kind == "d")
                if kind == "gu":
                    width = 2 * P if M == 0 else 4 * P
                    until(pool, mraw_gu[slot], raw_count, it, raw_per)
                    if M >= 2:
                        until(pool, gu_mm, 2 * first_of(M - 1), it, 2 * UNITS_W)
                    hi, lo, raw = mgu[:, slot, 0, :, 0:width], mgu[:, slot, 1, :, 0:width], rgu[:, slot, :, 0:width]
                else:
                    ne = 1 if M == 0 else 2
                    until(pool, mraw_d[slot], raw_count, it, raw_per)
                    if M >= 2:
                        until(pool, dn_mm, 2 * first_of(M - 1), it, 2 * UNITS_W)
                    hi, lo, raw = mwd[:, slot, 0, 0:ne], mwd[:, slot, 1, 0:ne], rwd[:, slot, 0:ne]
                stand_apart(pool, it)
                pool.tensor_scalar(hi, raw, 1.0, 1.0, ALU.mult, ALU.mult).then_inc(mw_hi, 1)
                until(pool, mw_hi, at + 1, it, 4)
                pool.tensor_tensor(lo, raw, hi.bitcast(f32), ALU.subtract).then_inc(mw_done, 1)

            def gu_raw(M):
                return 32 + 64 * (M // 2) if M % 2 == 0 else 64 * (M // 2 + 1)

            def d_raw(M):
                return 16 * (M // 2 + 1)

            expert_split("gu", 0, None, gu_raw(0), 0)
            expert_split("d", 0, None, d_raw(0), 0)
            expert_split("gu", 1, None, gu_raw(1), 0)
            expert_split("d", 1, None, d_raw(1), 0)
            pool.wait_ge(o_add, UNITS + 1)
            for b in range(B):
                tiles = slice(b * TB, (b + 1) * TB)
                pool.tensor_tensor(accB[:, tiles, :], accB[:, tiles, :], accA[:, tiles, :],
                                   ALU.add).then_inc(res_done, 1)
            expert_split("gu", 2, None, gu_raw(2), 0)
            with pool.Fori(0, NPAIR // 2 - 1) as it:
                expert_split("d", 2, it, d_raw(2), 16)
                expert_split("gu", 3, it, gu_raw(3), 64)
                expert_split("d", 3, it, d_raw(3), 16)
                expert_split("gu", 4, it, gu_raw(4), 64)
            expert_split("d", NPAIR, None, d_raw(NPAIR), 0)

        @block.tensor
        def _(pe):
            pe.wait_ge(consts, 4)
            pe.wait_ge(rows_in, 16 * 6)
            pe.transpose(bank["zb"][:, 0:NROW], rows_t[0:NROW, :], ident[0:NROW, 0:NROW])
            for k in range(KD):
                last = pe.transpose(bank["zb"][:, 64 + k * E:64 + (k + 1) * E],
                                    gaterow_t[0:E, k * P:(k + 1) * P], ident[0:E, 0:E])
            last.then_inc(cx_mm, 1)

            def turn_x(dst, src, what, b, k):
                for t in range(TB):
                    pe.wait_ge(ln_step, LN[what, b * TB + t])
                    m = pe.transpose(dst[:, t * P:(t + 1) * P], src(b * TB + t)[:, k * P:(k + 1) * P],
                                     ident[:, :])
                m.then_inc(x_mm, 1)

            def turn_xr(b):
                for k in range(KD):
                    turn_x((bS if b == 0 else bT)[k], lambda t: xr[:, t, :], "xr", b, k)

            def turn_xn(b):
                for k in range(KD):
                    if b:
                        pe.wait_ge(x_lo, B * KD + k + 1)
                    turn_x((bank["zb"], bank["ob"])[k], lambda t: accA[:, t, :], "xn", b, k)

            turn_xr(0)

            def mm3(dst, lhs, rhs, first, last_, skip=False):
                for i, (a, b) in enumerate(PASSES):
                    m = pe.matmul(dst, lhs(a), rhs(b), start=first and i == 0,
                                  stop=last_ and i == 2, skip_group_check=skip)
                return m

            def project(ch, it):
                at = CHUNK[ch]
                dst = bJ[at % 2]
                until(pe, j_lo, at + 1, it, per_of(ch))
                kind, v = ch[0], ch[1]
                if kind in ("Qrope", "Q", "K"):
                    a, b, q = v // GS, v % GS // 4, v % 4
                    src = xrT if kind == "Qrope" else xnT
                    until(pe, w_done, JOB[(f"Q{q}", a)] + 1, it, JOBS_W)
                    w = wqk[:, q, 1 if kind == "K" else 0]
                    for k in range(KD):
                        m = mm3(dst[:, :], lambda p: w[:, p, k, :],
                                lambda p: src[:, p, k, b * S:(b + 1) * S], k == 0, k == KD - 1)
                elif kind in ("Krope", "VT"):
                    a, b = v // 2, v % 2
                    until(pe, w_done, JOB[("KV", a)] + 1, it, JOBS_W)
                    half = KD * P
                    off = 0 if kind == "Krope" else half
                    for k in range(KD):
                        if ch == ("Krope", 0):
                            pe.wait_ge(x_lo, k + 1)
                        m = mm3(dst[:, :], lambda p: wkvA[:, p, off + k * P:off + (k + 1) * P],
                                lambda p: xrT[:, p, k, b * S:(b + 1) * S], k == 0, k == KD - 1)
                elif kind == "Vx":
                    until(pe, j_lo, CHUNK[("VT", v)] + 3, it, per_of(ch))
                    for t in range(TB):
                        m = pe.transpose(dst[:, t * P:(t + 1) * P], vt_t[:, t * P:(t + 1) * P], ident[:, :])
                else:
                    a, b, t = v // 2, v % 2, ch[2]
                    until(pe, w_done, JOB[("KV", a)] + 1, it, JOBS_W)
                    tok = (b * TB + t) * P
                    for k in range(KD):
                        m = mm3(dst[:, :], lambda p: xnT[:, p, k, tok:tok + P],
                                lambda p: wkvB[:, p, k, :], k == 0, k == KD - 1)
                m.then_inc(j_mm, 1)

            def per_of(ch):
                lim = HALF if ch[0] in ("Qrope", "Q", "K") else HALF // 4
                return CHUNKS_W[0 if ch[1] < lim else 1]

            def scores(u, i, it):
                until(pe, s_free, TB * u + i + 1, it, TB * GS)
                if i == 0:
                    if u < HALF:
                        until(pe, rp_lo["Qrope"], u + 1, it, ROT_W["Qrope"])
                        if u % 4 == 0:
                            until(pe, rp_lo["Krope"], u // 4 + 1, it, ROT_W["Krope"])
                    else:
                        until(pe, j_lo, CHUNK[("K", u)] + 3, it, CHUNKS_W[1])
                ks = u // 4 % 2 if u < HALF else u % 2
                width = max(2 * P, (i + 1) * P)
                mm3(bS[i % 2][:, 0:width], lambda p: qT[:, u % 2, p, i * P:(i + 1) * P],
                    lambda p: kT[:, ks, p, 0:width], True, True).then_inc(s_mm, 1)

            def turn_probs(u, c, it):
                at = 3 * u + c
                if c == 0:
                    until(pe, p_norm, TB * (u + 1), it, TB * GS)
                until(pe, pt_lo, at + 1, it, 3 * GS)
                lo_, hi_ = PT_CHUNKS[c]
                for j in range(lo_, hi_):
                    kt, qt = BLOCKS[j]
                    m = pe.transpose(bT[at % 2][:, (j - lo_) * P:(j - lo_ + 1) * P],
                                     pr[:, u % 2, P_OFF[qt] + kt * P:P_OFF[qt] + (kt + 1) * P], ident[:, :])
                m.then_inc(t_mm, 1)

            def attend(u, it):
                until(pe, pt_lo, 3 * u + 5, it, 3 * GS)
                until(pe, z_lo, u + 1, it, GS)
                if u % 4 == 0:
                    vc = ("Vx", u // 4) if u < HALF else ("V", u // 4, TB - 1)
                    until(pe, j_lo, CHUNK[vc] + 3, it, CHUNKS_W[0 if u < HALF else 1])
                col = 0 if u < HALF else u % 4 * P
                dst = bank["zb"]
                for kt in range(TB):
                    at, q0 = PT_ROW[kt]
                    m = mm3(dst[:, q0:S], lambda p: vh[:, u // 4 % 2, p, kt, col:col + P],
                            lambda p: pT[:, p, at:at + S - q0], kt == 0, kt == TB - 1, skip=True)
                m.then_inc(z_mm, 1)

            def out_project(n, t, it):
                o = n - 2
                m_, half = o // 2, o % 2
                a, b, hp = o // GS, o % GS // 4, m_ % 2
                if half == 0 and t == 0:
                    until(pe, z_lo, 2 * m_ + 3, it, GS)
                    until(pe, w_done, JOB[(f"O{hp}", a)] + 1, it, JOBS_W)
                if t == 0:
                    until(pe, o_add, o + 1, it, GS)
                tok = (2 * half + t) * P
                for j in range(2):
                    m = mm3(bank["ob"][:, t * D:(t + 1) * D],
                            lambda p: zT[:, (2 * m_ + j) % 4, p, tok:tok + P],
                            lambda p: w_o[:, hp, p, j, :], t == 0 and j == 0, t == 1 and j == 1, skip=True)
                if t == 1:
                    m.then_inc(o_mm, 1)

            def step(n, it):
                chs = chunks_of(n) if n < UNITS else []
                if n < 0:
                    for ch in chs:
                        project(ch, it)
                    if n == -1:
                        turn_xr(1)
                        pe.wait_ge(x_lo, KD)
                        for i in range(TB):
                            scores(0, i, it)
                        pe.wait_ge(cx_ev, 1)
                        turn_xn(0)
                        project(("Qrope", 2), it)
                        pe.wait_ge(x_lo, 2 * KD)
                        for c in range(2):
                            turn_probs(0, c, it)
                        turn_xn(1)
                    return
                nxt = n + 1 < UNITS
                rotary = n + 2 < HALF
                if rotary:
                    for ch in over_from(n) + (chs[:1] if n else []):
                        project(ch, it)
                if nxt:
                    scores(n + 1, 0, it)
                    scores(n + 1, 1, it)
                for ch in [] if rotary else over_from(n):
                    project(ch, it)
                o_first = not rotary or n % 4 < 2
                if o_first and 2 <= n:
                    out_project(n, 0, it)
                if n < UNITS:
                    turn_probs(n, 2, it)
                if nxt:
                    scores(n + 1, 2, it)
                    scores(n + 1, 3, it)
                if not o_first and 2 <= n:
                    out_project(n, 0, it)
                if 2 <= n:
                    out_project(n, 1, it)
                for ch in [] if rotary else chs[:2]:
                    project(ch, it)
                if n == UNITS - 2:
                    turn_x2(0)
                    turn_x2(1)
                if n == UNITS - 1:
                    logits()
                if n == 0:
                    pe.wait_ge(x_lo, 2 * B * KD)
                attend(n, it)
                for ch in chs[1:2] if rotary else []:
                    project(ch, it)
                if nxt:
                    turn_probs(n + 1, 0, it)
                    turn_probs(n + 1, 1, it)
                if n == UNITS - 2:
                    turn_x2(2)
                    turn_x2(3)

            def turn_x2(i):
                b, k = i // KD, i % KD
                if i < 2:
                    pe.wait_ge(j_lo, len(CHUNK) + 2 - 1 + i)
                else:
                    pe.wait_ge(x_lo, 2 * B * KD + i - 1)
                turn_x(bJ[i % 2], xr2, "xr2", b, k)

            def logits():
                pe.wait_ge(g_hi, 2)
                pe.wait_ge(s_free, TB * UNITS + 2)
                for b in range(B):
                    pe.wait_ge(x_lo, 2 * B * KD + (b + 1) * KD)
                    for k in range(KD):
                        m = mm3(bS[b][:, :], lambda p: gateT[:, p, k, :],
                                lambda p: xrT[:, p, k, b * S:(b + 1) * S], k == 0, k == KD - 1)
                    m.then_inc(lg_mm, 1)

            windows(pe, step)

            def gate_or_up(w, up, it):
                M, j, b = expert_of(w)
                if not up:
                    if w >= 2:
                        until(pe, h_done, w - 1, it, UNITS_W)
                    if w == first_of(M):
                        until(pe, mw_done, 2 * M + 1, it, 4)
                ne = 1 if M == 0 else 2
                at = (up * ne + j) * P
                for k in range(KD):
                    m = mm3((bU if up else bG)[w % 2][:, :], lambda p: mgu[:, M % 2, p, k, at:at + P],
                            lambda p: xrT[:, p, k, b * S:(b + 1) * S], k == 0, k == KD - 1)
                m.then_inc(gu_mm, 1)

            def down(w, it):
                M, j, b = expert_of(w)
                until(pe, ht_lo, w + 1, it, UNITS_W)
                if w >= 2:
                    until(pe, y_acc, 2 * (w - 1), it, 2 * UNITS_W)
                if w == first_of(M):
                    until(pe, mw_done, 2 * M + 2, it, 4)
                for half in range(2):
                    for t in range(2):
                        tok = (2 * half + t) * P
                        m = mm3(bY[w % 2][half][:, t * D:(t + 1) * D], lambda p: hT[:, w % 2, p, tok:tok + P],
                                lambda p: mwd[:, M % 2, p, j, :], t == 0, t == 1, skip=True)
                    m.then_inc(dn_mm, 1)

            def expert_step(w, it):
                if w + 1 < NW:
                    gate_or_up(w + 1, 0, it)
                    gate_or_up(w + 1, 1, it)
                if w >= 1:
                    down(w - 1, it)

            pe.wait_ge(lg_ev, 2)
            for t in range(NT):
                m = pe.transpose(bT[0][:, t * E:(t + 1) * E], lgT[0:E, t * P:(t + 1) * P], ident[0:E, 0:E])
            m.then_inc(lt_mm, 1)
            gate_or_up(0, 0, None)
            out_project(UNITS, 0, None)
            out_project(UNITS, 1, None)
            gate_or_up(0, 1, None)
            out_project(UNITS + 1, 0, None)
            out_project(UNITS + 1, 1, None)
            gate_or_up(1, 0, None)
            pe.wait_ge(o_add, UNITS + 1)
            gate_or_up(1, 1, None)
            pe.wait_ge(rt, 2)
            for w in range(1, WSTART):
                expert_step(w, None)
            with pe.Fori(0, TURNS) as it:
                for w in range(WSTART, WSTART + UNITS_W):
                    expert_step(w, it)
            for w in range(WSTART + TURNS * UNITS_W, NW + 1):
                expert_step(w, None)

        @block.scalar
        def _(act):
            act.dma_start(rope_t[:, :], rope_table).then_inc(rope_in, 16)
            act.dma_start(bO_t[:, :], b_O.rearrange("(a d) -> a d", a=1).broadcast_to([P, D])).then_inc(bc_in, 16)
            act.dma_start(be_t[:, :], bias_e.rearrange("(a d) -> a d", a=1).broadcast_to([P, E])).then_inc(bc_in, 16)

            def squares(src, scratch, w, tiles):
                for t in tiles:
                    if w == 1:
                        act.wait_ge(ln_step, LN["xn", t])
                    if t or w == 2:
                        act.wait_ge(ln_ssq, (w - 1) * NT + t)
                    act.activation(scratch, src[:, t, :], ACT.Square,
                                   accum_out=var[:, 3, t:t + 1]).then_inc(ln_ssq, 1)

            squares(accA, t1_t[:, 0:D], 1, range(NT))

            def turned(dst, b, at, banks, scale_at):
                for k in range(KD):
                    act.wait_ge(x_mm, at + k + 1)
                    hi = dst[:, 0, k, b * S:(b + 1) * S]
                    if scale_at is None:
                        act.activation(hi, banks[k][:, :], ACT.Copy).then_inc(x_hi, 1)
                    else:
                        act.activation(hi, banks[k][:, :], ACT.Identity,
                                       scale=cols[:, scale_at + k:scale_at + k + 1]).then_inc(x_hi, 1)

            def turned2(i):
                b, k = i // KD, i % KD
                act.wait_ge(x_mm, 2 * B * KD + i + 1)
                act.activation(xrT[:, 0, k, b * S:(b + 1) * S], bJ[i % 2][:, :], ACT.Identity,
                               scale=cols[:, L2 + k:L2 + k + 1]).then_inc(x_hi, 1)

            act.wait_ge(cx_ev, 1)
            turned(xrT, 0, 0, bS, L1)

            def exp(u, i, it):
                until(act, s_free, TB * u + i + 3, it, TB * GS)
                piece = pr[:, u % 2, P_OFF[i]:P_OFF[i] + (i + 1) * P]
                act.activation(piece, piece, ACT.Exp, bias=nmax[:, u % 2, i:i + 1], scale=-1.0,
                               accum_out=rsum[:, u % 2, i:i + 1]).then_inc(e_done, 1)

            def probs_hi(u, c, it):
                until(act, t_mm, 3 * u + c + 1, it, 3 * GS)
                a, b = PT_CHUNKS[c]
                act.activation(pT[:, 0, (a + 1) * P:(b + 1) * P], bT[(3 * u + c) % 2][:, 0:(b - a) * P],
                               ACT.Copy).then_inc(pt_hi, 1)

            def z_part(u, it):
                until(act, z_mm, u + 1, it, GS)
                dst = zT[:, u % 4, 0, :]
                if u < HALF:
                    act.activation(dst, bank["zb"][:, :], ACT.Copy).then_inc(z_hi, 1)
                else:
                    stand_apart(act, it)
                    act.activation(dst, bank["zb"][:, :], ACT.Identity, bias=col_of(BV, u, it)).then_inc(z_hi, 1)

            def col_of(base, u, it):
                h = 4 * ((u - HALF) // GS) + u % 4 + base
                return cols[:, h:h + 1] if it is None else cols[:, bass.ds(it * 4 + h, 1)]

            def chunk_a(ch, it):
                at, kind, v = CHUNK[ch], ch[0], ch[1]
                src = bJ[at % 2]
                per = CHUNKS_W[0 if kind in ("Qrope", "Krope", "VT", "Vx") else 1]
                until(act, j_mm, at + 1, it, per)
                if kind in ROT_W:
                    if v:
                        until(act, rp_sum[kind], v, it, ROT_W[kind])
                    act.activation(swapped[kind][0:P // 2, :], src[P // 2:P, :], ACT.Copy)
                    act.activation(swapped[kind][P // 2:P, :], src[0:P // 2, :],
                                   ACT.Copy).then_inc(sw_done[kind], 1)
                elif kind == "VT":
                    until(act, j_lo, at + 2, it, per)
                    act.activation(vt_t[:, :], src[:, :], ACT.Copy).then_inc(j_lo, 1)
                elif kind in ("Q", "K"):
                    dst = (qT if kind == "Q" else kT)[:, v % 2, 0]
                    stand_apart(act, it)
                    act.activation(dst, src[:, :], ACT.Identity,
                                   bias=col_of(BQ if kind == "Q" else BK, v, it)).then_inc(j_hi, 1)
                elif kind == "Vx":
                    act.activation(vh[:, v % 2, 0, :, 0:P], src[:, :].rearrange("p (t e) -> p t e", t=TB),
                                   ACT.Copy).then_inc(j_hi, 1)
                else:
                    act.activation(vh[:, v % 2, 0, ch[2], :], src[:, :], ACT.Copy).then_inc(j_hi, 1)

            def chunk_b(ch, it):
                kind, v = ch[0], ch[1]
                if kind in ROT_W:
                    until(act, rp_sum[kind], v + 1, it, ROT_W[kind])
                    dst = (qT if kind == "Qrope" else kT)[:, v % 2, 0]
                    act.activation(dst, rot_sum(ch), ACT.Copy).then_inc(rp_hi[kind], 1)

            def step(n, it):
                chs = chunks_of(n) if n < UNITS else []
                if n == -2:
                    for ch in chs:
                        chunk_a(ch, it)
                    chunk_b(chs[0], it)
                    return
                if n == -1:
                    vt, q1, vx = chs
                    chunk_a(vt, it)
                    chunk_b(("Qrope", 0), it)
                    chunk_a(q1, it)
                    chunk_a(vx, it)
                    turned(xrT, 1, KD, bT, L1)
                    for i in range(TB):
                        exp(0, i, it)
                    chunk_b(q1, it)
                    turned(xnT, 0, B * KD, (bank["zb"], bank["ob"]), None)
                    probs_hi(0, 0, it)
                    probs_hi(0, 1, it)
                    turned(xnT, 1, B * KD + KD, (bank["zb"], bank["ob"]), None)
                    return
                nxt = n + 1 < UNITS
                rotary = n + 2 < HALF
                if rotary:
                    for ch in over_from(n) + chs[:1]:
                        chunk_a(ch, it)
                if nxt:
                    exp(n + 1, 0, it)
                    exp(n + 1, 1, it)
                for ch in [] if rotary else over_from(n):
                    chunk_a(ch, it)
                probs_hi(n, 2, it)
                for ch in behind(n, 1, "Krope"):
                    chunk_a(ch, it)
                if nxt:
                    exp(n + 1, 2, it)
                    exp(n + 1, 3, it)
                for ch in behind(n, 2, "Krope"):
                    chunk_b(ch, it)
                if rotary:
                    chunk_b(chs[0], it)
                for ch in [] if rotary else chs[:2]:
                    chunk_a(ch, it)
                if n == UNITS - 2:
                    turned2(0)
                    turned2(1)
                if n == UNITS - 5:
                    act.wait_ge(o_add, HALF + 1)
                    squares(accA, vt_t[:, 0:D], 2, range(TB))
                z_part(n, it)
                if nxt:
                    probs_hi(n + 1, 0, it)
                    probs_hi(n + 1, 1, it)
                for ch in chs[1:2] if rotary else []:
                    if ch[0] != "Krope":
                        chunk_a(ch, it)
                if n == UNITS - 5:
                    squares(accA, vt_t[:, 0:D], 2, range(TB, NT))
                if n == UNITS - 2:
                    turned2(2)
                    turned2(3)

            windows(act, step)

            act.wait_ge(rt, 2)
            act.activation(route[:, 0, :, 0:E], route[:, 0, :, 0:E], ACT.Exp).then_inc(rt_exp, 1)

            def silu_and_hi(w, it):
                until(act, gu_mm, 2 * w + 1, it, 2 * UNITS_W)
                if w >= 2:
                    until(act, h_done, w - 1, it, UNITS_W)
                act.activation(silu[:, w % 2], bG[w % 2][:, :], ACT.Silu).then_inc(si_done, 1)
                until(act, h_done, w + 1, it, UNITS_W)
                if w >= 2:
                    until(act, dn_mm, 2 * (w - 1), it, 2 * UNITS_W)
                act.activation(hT[:, w % 2, 0], h_raw[:, w % 2], ACT.Copy).then_inc(ht_hi, 1)

            for w in range(WSTART + 1):
                silu_and_hi(w, None)
            with act.Fori(0, TURNS) as it:
                for w in range(WSTART, WSTART + UNITS_W):
                    silu_and_hi(w + 1, it)
            for w in range(WSTART + TURNS * UNITS_W, NW - 1):
                silu_and_hi(w + 1, None)

        @block.vector
        def _(ve):
            ve.memset(pT[:, 0, 0:P].bitcast(f32), 0.0).then_inc(zeroed, 1)
            ve.memset(pT[:, 1, 0:P].bitcast(f32), 0.0).then_inc(zeroed, 1)
            ve.sem_inc(s_free, 2)
            ve.sem_inc(pt_lo, 2)
            ve.sem_inc(j_lo, 2)
            ve.sem_inc(z_lo, 1)
            ve.sem_inc(o_add, 1)

            done = [0]

            def did(ins, *what):
                done[0] += 1
                assert LN[what] == done[0]
                ins.then_inc(ln_step, 1)

            def tiles_of(b):
                return range(b * TB, (b + 1) * TB)

            for b in range(B):
                ve.wait_ge(x_in[b], 16)
                for t in tiles_of(b):
                    did(ve.bn_stats(stats[:, t, :], accB[:, t, :]), "stats", t)
                for t in tiles_of(b):
                    ve.wait_ge(ln_step, LN["stats", t])
                    did(ve.bn_aggr(mv[:, t, :], stats[:, t, :]), "mean_var", t)
                ve.wait_ge(ln_step, LN["mean_var", (b + 1) * TB - 1])
                ts = slice(b * TB, (b + 1) * TB)
                did(ve.tensor_scalar(var[:, 0, ts], mv[:, ts, 1], 1e-05, None, ALU.add), "var", 0, b)
            for b in range(B):
                ve.wait_ge(ln_pow, b + 1)
                for t in tiles_of(b):
                    did(ve.tensor_scalar(accA[:, t, :], accB[:, t, :], mv[:, t, 0:1], rstd[:, 0, t:t + 1],
                                         ALU.subtract, ALU.mult), "xn", t)

            def first_rms(b):
                ts = slice(b * TB, (b + 1) * TB)
                ve.wait_ge(ln_ssq, (b + 1) * TB)
                did(ve.tensor_scalar(var[:, 1, ts], var[:, 3, ts], 1.0 / D, 1e-06, ALU.mult, ALU.add), "var", 1, b)
                ve.wait_ge(ln_pow, B + b + 1)
                for t in tiles_of(b):
                    did(ve.tensor_scalar(xr[:, t, :], accA[:, t, :], rstd[:, 1, t:t + 1], None, ALU.mult), "xr", t)

            first_rms(0)
            ve.wait_ge(cx_mm, 1)
            ve.tensor_copy(cols[:, 0:NROW], bank["zb"][:, 0:NROW])
            ve.tensor_copy(gate_keep[:, :], bank["zb"][:, 64:64 + KD * E]).then_inc(cx_ev, 1)

            def turned(dst, b, at, banks, scale_at, blocks=range(KD)):
                for k in blocks:
                    ve.wait_ge(x_hi, at + k + 1)
                    hi = dst[:, 0, k, b * S:(b + 1) * S].bitcast(f32)
                    lo = dst[:, 1, k, b * S:(b + 1) * S]
                    if scale_at is None:
                        ve.tensor_tensor(lo, banks[k][:, :], hi, ALU.subtract).then_inc(x_lo, 1)
                    else:
                        ve.scalar_tensor_tensor(out=lo, in0=banks[k][:, :],
                                                scalar=cols[:, scale_at + k:scale_at + k + 1], in1=hi,
                                                op0=ALU.mult, op1=ALU.subtract).then_inc(x_lo, 1)

            ve.wait_ge(cx_ev, 1)
            turned(xrT, 0, 0, bS, L1)
            first_rms(1)
            ve.wait_ge(zeroed, 2)
            ve.wait_ge(consts, 5)
            ve.wait_ge(rope_in, 16)

            def mask_scores(u, i, it):
                until_apart(ve, s_mm, TB * u + i + 1, it, TB * GS)
                width = (i + 1) * P
                ve.tensor_tensor_reduce(pr[:, u % 2, P_OFF[i]:P_OFF[i] + width], bS[i % 2][:, 0:width],
                                        mask_t[:, S - width:S], INV_SCALE, BIG, ALU.add, ALU.min,
                                        nmax[:, u % 2, i:i + 1]).then_inc(s_free, 1)

            def invert(u, i, it):
                until(ve, e_done, TB * u + i + 1, it, TB * GS)
                ve.reciprocal(rinv[:, u % 2, i:i + 1], rsum[:, u % 2, i:i + 1]).then_inc(r_done, 1)

            def probs_lo(u, c, it):
                until(ve, pt_hi, 3 * u + c + 1, it, 3 * GS)
                a, b = PT_CHUNKS[c]
                cs = slice((a + 1) * P, (b + 1) * P)
                ve.tensor_tensor(pT[:, 1, cs], bT[(3 * u + c) % 2][:, 0:(b - a) * P],
                                 pT[:, 0, cs].bitcast(f32), ALU.subtract).then_inc(pt_lo, 1)

            def col_of(base, u, it):
                h = 4 * ((u - HALF) // GS) + u % 4 + base
                return cols[:, h:h + 1] if it is None else cols[:, bass.ds(it * 4 + h, 1)]

            def z_part(u, it):
                until(ve, z_hi, u + 1, it, GS)
                hi, lo = zT[:, u % 4, 0, :].bitcast(f32), zT[:, u % 4, 1, :]
                if u < HALF:
                    ve.tensor_tensor(lo, bank["zb"][:, :], hi, ALU.subtract).then_inc(z_lo, 1)
                else:
                    ve.scalar_tensor_tensor(out=lo, in0=bank["zb"][:, :], scalar=col_of(BV, u, it), in1=hi,
                                            op0=ALU.add, op1=ALU.subtract).then_inc(z_lo, 1)

            HI = {}
            for ch in CHUNK:
                if ch[0] not in ROT_W and ch[0] != "VT":
                    HI[ch] = len(HI)
            HI_W = [GS // 4, CHUNKS_W[1]]

            def chunk(ch, it):
                at, kind, v = CHUNK[ch], ch[0], ch[1]
                src = bJ[at % 2]
                phase = 0 if kind in ("Qrope", "Krope", "VT", "Vx") else 1
                if kind in ROT_W:
                    until(ve, j_mm, at + 1, it, CHUNKS_W[phase])
                    slots = 2 if kind == "Qrope" else 1
                    if v >= slots:
                        until(ve, rp_lo[kind], v + 1 - slots, it, ROT_W[kind])
                    until(ve, sw_done[kind], v + 1, it, ROT_W[kind])
                    ve.tensor_tensor(rot_sum(ch), src[:, :], cosT, ALU.mult).then_inc(j_lo, 1)
                elif kind != "VT":
                    until(ve, j_hi, HI[ch] + 1, it, HI_W[phase])
                    if kind in ("Q", "K"):
                        dst = (qT if kind == "Q" else kT)[:, v % 2]
                        ve.scalar_tensor_tensor(out=dst[:, 1], in0=src[:, :],
                                                scalar=col_of(BQ if kind == "Q" else BK, v, it),
                                                in1=dst[:, 0].bitcast(f32),
                                                op0=ALU.add, op1=ALU.subtract).then_inc(j_lo, 1)
                    elif kind == "Vx":
                        ve.tensor_tensor(vh[:, v % 2, 1, :, 0:P], src[:, :].rearrange("p (t e) -> p t e", t=TB),
                                         vh[:, v % 2, 0, :, 0:P].bitcast(f32), ALU.subtract).then_inc(j_lo, 1)
                    else:
                        ve.tensor_tensor(vh[:, v % 2, 1, ch[2], :], src[:, :],
                                         vh[:, v % 2, 0, ch[2], :].bitcast(f32), ALU.subtract).then_inc(j_lo, 1)

            def k_sin(ch, it):
                half = swapped["Krope"]
                ve.tensor_tensor(half, half, sinT, ALU.mult).then_inc(rp_sin["Krope"], 1)

            def k_lo(ch, it):
                v = ch[1]
                until(ve, rp_hi["Krope"], v + 1, it, ROT_W["Krope"])
                ve.tensor_tensor(kT[:, v % 2, 1], rot_sum(ch), kT[:, v % 2, 0].bitcast(f32),
                                 ALU.subtract).then_inc(rp_lo["Krope"], 1)

            def rope_sum(ch, it):
                if ch[0] in ROT_W:
                    until(ve, rp_sin[ch[0]], ch[1] + 1, it, ROT_W[ch[0]])
                    if ch[0] == "Qrope":
                        until(ve, j_lo, CHUNK[ch] + 3, it, CHUNKS_W[0])
                    ve.tensor_tensor(rot_sum(ch), rot_sum(ch), swapped[ch[0]], ALU.add
                                     ).then_inc(rp_sum[ch[0]], 1)

            def add_out(n, it):
                o = n - 2
                half, b = o % 2, o % GS // 4
                acc = accA if o < HALF else accB
                if o == HALF:
                    ve.wait_ge(bias_added, 2)
                until(ve, o_mm, o + 1, it, GS)
                until(ve, o_add, o + 1, it, GS)
                t = b * TB + 2 * half
                tiles = acc[:, t:t + 2, :]
                ve.tensor_tensor(tiles, bank["ob"][:, :].rearrange("p (t d) -> p t d", t=2), tiles,
                                 ALU.add).then_inc(o_add, 1)

            def step(n, it):
                chs = chunks_of(n) if n < UNITS else []
                if n < 0:
                    if n == -2:
                        k, q = chs
                        chunk(k, it)
                        k_sin(k, it)
                        rope_sum(k, it)
                        chunk(q, it)
                        rope_sum(q, it)
                        k_lo(k, it)
                    if n == -1:
                        _, q1, vx = chs
                        chunk(q1, it)
                        mask_scores(0, 0, it)
                        mask_scores(0, 1, it)
                        turned(xrT, 1, KD, bT, L1, [0])
                        mask_scores(0, 2, it)
                        mask_scores(0, 3, it)
                        for i in range(3):
                            invert(0, i, it)
                        turned(xrT, 1, KD, bT, L1, range(1, KD))
                        invert(0, 3, it)
                        rope_sum(q1, it)
                        chunk(vx, it)
                        turned(xnT, 0, B * KD, (bank["zb"], bank["ob"]), None)
                        probs_lo(0, 0, it)
                        probs_lo(0, 1, it)
                        turned(xnT, 1, B * KD + KD, (bank["zb"], bank["ob"]), None)
                    return
                nxt = n + 1 < UNITS
                rotary = n + 2 < HALF
                if nxt:
                    mask_scores(n + 1, 0, it)
                    mask_scores(n + 1, 1, it)
                for ch in over_from(n):
                    chunk(ch, it)
                if not rotary:
                    probs_lo(n, 2, it)
                    if nxt:
                        mask_scores(n + 1, 2, it)
                        invert(n + 1, 0, it)
                        invert(n + 1, 1, it)
                        mask_scores(n + 1, 3, it)
                        invert(n + 1, 2, it)
                        invert(n + 1, 3, it)
                else:
                    k_product, k_last = behind(n, 1, "Krope"), behind(n, 2, "Krope")
                    v_last = behind(n, 1, "Vx")
                    for ch in v_last:
                        chunk(ch, it)
                    if not k_product and not v_last:
                        chunk(chs[0], it)
                    mask_scores(n + 1, 2, it)
                    invert(n + 1, 0, it)
                    invert(n + 1, 1, it)
                    probs_lo(n, 2, it)
                    mask_scores(n + 1, 3, it)
                    invert(n + 1, 2, it)
                    for ch in k_product:
                        chunk(ch, it)
                    if v_last:
                        chunk(chs[0], it)
                    for ch in k_last:
                        rope_sum(ch, it)
                    invert(n + 1, 3, it)
                    if k_product:
                        chunk(chs[0], it)
                    rope_sum(chs[0], it)
                if 2 <= n:
                    add_out(n, it)
                if rotary:
                    for ch in k_product:
                        k_sin(ch, it)
                    for ch in k_last:
                        k_lo(ch, it)
                if n == UNITS - 4:
                    ve.wait_ge(ln_ssq, 2 * NT)
                    did(ve.tensor_scalar(var[:, 2], var[:, 3], 1.0 / D, 1e-06, ALU.mult, ALU.add), "var", 2)
                for ch in [] if rotary else chs[:2]:
                    chunk(ch, it)
                if n == UNITS - 3:
                    scale_rows(range(TB))
                if n == UNITS - 2:
                    split_gate()
                    turned2(0)
                    turned2(1)
                if n == UNITS - 1:
                    for b in range(B):
                        ve.wait_ge(lg_mm, b + 1)
                        ve.tensor_copy(lgT[0:E, b * S:(b + 1) * S], bS[b][0:E, :]).then_inc(lg_ev, 1)
                z_part(n, it)
                if nxt:
                    probs_lo(n + 1, 0, it)
                    probs_lo(n + 1, 1, it)
                if n == UNITS - 3:
                    scale_rows(range(TB, NT))
                if n == UNITS - 2:
                    turned2(2)
                    turned2(3)
                for ch in chs[1:2] if rotary else []:
                    if ch[0] == "V":
                        chunk(ch, it)

            def split_gate():
                for h in range(2):
                    ve.memset(gateT[:, h].bitcast(f32), 0.0).then_inc(zeroed, 1)
                ve.wait_ge(zeroed, 4)
                gk = gate_keep[:, :].rearrange("p (k e) -> p k e", k=KD)
                ve.tensor_copy(gateT[:, 0, :, 0:E], gk).then_inc(g_hi, 1)
                ve.wait_ge(g_hi, 1)
                ve.tensor_tensor(gateT[:, 1, :, 0:E], gk, gateT[:, 0, :, 0:E].bitcast(f32),
                                 ALU.subtract).then_inc(g_hi, 1)

            def scale_rows(tiles):
                ve.wait_ge(ln_pow, 2 * B + 1)
                for t in tiles:
                    did(ve.tensor_scalar(xr2(t), accA[:, t, :], rstd[:, 2, t:t + 1], None, ALU.mult), "xr2", t)

            def turned2(i):
                b, k = i // KD, i % KD
                ve.wait_ge(x_hi, 2 * B * KD + i + 1)
                cs = slice(b * S, (b + 1) * S)
                ve.scalar_tensor_tensor(out=xrT[:, 1, k, cs], in0=bJ[i % 2][:, :],
                                        scalar=cols[:, L2 + k:L2 + k + 1], in1=xrT[:, 0, k, cs].bitcast(f32),
                                        op0=ALU.mult, op1=ALU.subtract).then_inc(x_lo, 1)

            windows(ve, step)

            over = lambda ap: ap.unsqueeze(2).to_broadcast([P, NT, E])
            logits = bT[0][:, 0:NT * E].rearrange("p (t e) -> p t e", t=NT)
            probs, biased, left = (route[:, i, :, 0:E] for i in range(3))
            count = [0]

            def then(ins):
                count[0] += 1
                ins.then_inc(rt, 1)
                ve.wait_ge(rt, count[0])

            def select(part):
                if part == 0:
                    ve.wait_ge(lt_mm, 1)
                    then(ve.tensor_reduce(rsm[:, 0], logits, AX.X, ALU.max))
                    then(ve.tensor_tensor(probs, logits, over(rsm[:, 0]), ALU.subtract))
                elif part == 1:
                    ve.wait_ge(rt_exp, 1)
                    then(ve.tensor_reduce(rsm[:, 1], probs, AX.X, ALU.add))
                    then(ve.reciprocal(rsm[:, 2], rsm[:, 1]))
                    then(ve.tensor_tensor(probs, probs, over(rsm[:, 2]), ALU.mult))
                    then(ve.tensor_tensor(biased, probs, be_t[:, :].unsqueeze(1).to_broadcast([P, NT, E]), ALU.add))
                elif part == 2:
                    ve.memset(route[:, 1, :, E:RW], -BIG)
                    for t in range(NT):
                        last = ve.max(top8[:, t, :], route[:, 1, t, 0:E])
                    then(last)
                    then(ve.memset(top8[:, :, TOPK:8], -BIG))
                elif part == 3:
                    for t in range(NT):
                        last = ve.match_replace(out=route[:, 2, t, :], in_to_replace=top8[:, t, :],
                                                in_values=route[:, 1, t, :], imm_value=-0.5 * BIG)
                    then(last)
                    then(ve.tensor_tensor(left, left, biased, ALU.not_equal))
                else:
                    then(ve.tensor_tensor(cw, probs, left, ALU.mult))
                    then(ve.tensor_reduce(rsm[:, 3], cw, AX.X, ALU.add))
                    then(ve.tensor_scalar(rsm[:, 0], rsm[:, 3], 1e-12, None, ALU.max))
                    then(ve.reciprocal(rsm[:, 1], rsm[:, 0]))
                    then(ve.tensor_tensor(cw, cw, over(rsm[:, 1]), ALU.mult))

            def make_h(w, it):
                until(ve, si_done, w + 1, it, UNITS_W)
                until(ve, gu_mm, 2 * w + 2, it, 2 * UNITS_W)
                if w >= 2:
                    until(ve, ht_lo, w - 1, it, UNITS_W)
                ve.tensor_tensor(h_raw[:, w % 2], bU[w % 2][:, :], silu[:, w % 2], ALU.mult).then_inc(h_done, 1)

            def h_lo(w, it):
                until(ve, ht_hi, w + 1, it, UNITS_W)
                ve.tensor_tensor(hT[:, w % 2, 1], h_raw[:, w % 2], hT[:, w % 2, 0].bitcast(f32),
                                 ALU.subtract).then_inc(ht_lo, 1)

            def add_y(w, half, it):
                M, j, b = expert_of(w)
                t0 = b * TB + 2 * half
                until(ve, dn_mm, 2 * w + half + 1, it, 2 * UNITS_W)
                if w < 2:
                    ve.wait_ge(res_done, b + 1)
                else:
                    until(ve, y_acc, 2 * (w - 2) + half + 1, it, 2 * UNITS_W)
                if M == 0:
                    tiles = accB[:, t0:t0 + 2, :]
                    ve.tensor_tensor(tiles, bY[w % 2][half][:, :].rearrange("p (t d) -> p t d", t=2), tiles,
                                     ALU.add).then_inc(y_acc, 1)
                    return
                e = 2 * (M - 1) + j
                for t in range(2):
                    c = cw[:, t0 + t, e:e + 1] if it is None else cw[:, t0 + t, bass.ds(it * 4 + e, 1)]
                    last = ve.scalar_tensor_tensor(out=accB[:, t0 + t, :], in0=bY[w % 2][half][:, t * D:(t + 1) * D],
                                                   scalar=c, in1=accB[:, t0 + t, :], op0=ALU.mult, op1=ALU.add)
                last.then_inc(y_acc, 1)

            def expert_step(w, it):
                if w + 1 < NW:
                    make_h(w + 1, it)
                if w >= 1:
                    add_y(w - 1, 0, it)
                if w + 1 < NW:
                    h_lo(w + 1, it)
                if w >= 1:
                    add_y(w - 1, 1, it)

            select(0)
            add_out(UNITS, None)
            make_h(0, None)
            h_lo(0, None)
            add_out(UNITS + 1, None)
            select(1)
            for w in range(WSTART):
                expert_step(w, None)
                select(w + 2)
            with ve.Fori(0, TURNS) as it:
                for w in range(WSTART, WSTART + UNITS_W):
                    expert_step(w, it)
            for w in range(WSTART + TURNS * UNITS_W, NW + 1):
                expert_step(w, None)


_A = ["x", "W_Q", "W_K", "W_V", "W_O", "b_Q", "b_K", "b_V", "b_O"]
_F = ["ln1_w", "ln2_w", "wq", "wk", "wv", "wo", "gate_w", "bias_e", "weg", "weu", "wed", "wsg", "wsu", "wsd"]
_INS = [f"L0_attn_{n}" for n in _A] + [f"L0_ffn_{n}" for n in _F]


def _rope_table(positions, d, theta):
    import numpy as np

    f = np.float32
    inv_freq = (f(1.0) / np.power(f(theta), np.arange(0, d, 2, dtype=f) / f(d))).astype(f)
    angle = (np.arange(positions, dtype=f)[None, :] * inv_freq[:, None]).astype(f)
    cos, sin = np.cos(angle).astype(f), np.sin(angle).astype(f)
    return np.concatenate([np.concatenate([cos, cos]), np.concatenate([-sin, sin])], axis=1)


def kernel(**inputs):
    import numpy as _np
    import concourse.bacc as _bacc
    from concourse import mybir as _mybir
    from concourse.bass_utils import run_bass_kernel_spmd as _run

    nc = _bacc.Bacc("TRN2", target_bir_lowering=False, num_devices=1)
    arrays, args = {}, []
    named = {n: _np.ascontiguousarray(inputs[n]) for n in _INS}
    seq, d_head = named["L0_attn_x"].shape[1], named["L0_attn_W_Q"].shape[2]
    named["rope_table"] = _rope_table(seq, d_head, 10000.0)
    for name, a in named.items():
        arrays[f"in_{name}_dram"] = a
        args.append(nc.dram_tensor(f"in_{name}_dram", a.shape, _mybir.dt.from_np(a.dtype), kind="ExternalInput").ap())
    shape = named["L0_attn_x"].shape
    args.append(nc.dram_tensor("out_0_dram", shape, _mybir.dt.float32, kind="ExternalOutput").ap())
    attention_pair_moe_kernel(nc, *args)
    r = _run(nc, [arrays], core_ids=[0])
    return r.results[0]["out_0_dram"]
```
